# Optimizing a Trainium2 kernel written in Bass

```python
import numpy as np
import jax
import jax.numpy as jnp

def _softmax(x, axis=-1):
    return jax.nn.softmax(x, axis=axis)

def _gelu(x):
    return jax.nn.gelu(x, approximate=True)

def _silu(x):
    return jax.nn.silu(x)

def _sigmoid(x):
    return jax.nn.sigmoid(x)

def _layernorm(x, axis=-1, eps=1e-05):
    m = jnp.mean(x, axis=axis, keepdims=True)
    v = jnp.var(x, axis=axis, keepdims=True)
    return (x - m) / jnp.sqrt(v + eps)

def _scatter_add(tgt, idx, src, axis=0):
    return tgt.at[idx].add(src)

def _segment_sum(src, seg, n):
    return jax.ops.segment_sum(src, seg, n)
kernel_name = 'mk_adaln_d2_jaxref_r4_4264cc'

def setup_inputs(seed: int=0):
    np.random.seed(seed)
    _w = jnp.asarray

    def _L0_attn_setup():
        import jax, jax.numpy as jnp
        import numpy as np
        import math
        B, N, D, H = (1, 1024, 256, 16)
        HS = D // H
        NEG_INF = -10000.0
        key = jax.random.key(seed)
        k1, k2, k3, k4, k5 = jax.random.split(key, 5)
        return {'encodings': jax.random.normal(k1, (B, N, D), dtype=jnp.float32), 'attn_W': jax.random.normal(k2, (D, 3 * D), dtype=jnp.float32) * 0.02, 'attn_b': jax.random.normal(k3, (3 * D,), dtype=jnp.float32) * 0.02, 'out_W': jax.random.normal(k4, (D, D), dtype=jnp.float32) * 0.02, 'out_b': jax.random.normal(k5, (D,), dtype=jnp.float32) * 0.02}
    _L0_attn_in = _L0_attn_setup()

    def _L0_ffn_setup():
        import jax, jax.numpy as jnp
        import numpy as np
        TOP_K = 8
        CAPACITY = 128

        def _silu(x):
            return x * jax.nn.sigmoid(x)
        key = jax.random.key(seed)
        ks = jax.random.split(key, 7)
        B, S, H, E, I, Is = (2, 256, 256, 64, 128, 512)
        s = 0.05
        return {'hidden_states': jax.random.normal(ks[0], (B, S, H), jnp.float32), 'gate_w': jax.random.normal(ks[1], (H, E), jnp.float32) * s, 'shared_gate_w': jax.random.normal(ks[2], (H, 1), jnp.float32) * s, 'shared_gate_up_w': jax.random.normal(ks[3], (H, 2 * Is), jnp.float32) * s, 'shared_down_w': jax.random.normal(ks[4], (Is, H), jnp.float32) * s, 'expert_gate_up_w': jax.random.normal(ks[5], (E, H, 2 * I), jnp.float32) * s, 'expert_down_w': jax.random.normal(ks[6], (E, I, H), jnp.float32) * s}
    _L0_ffn_in = _L0_ffn_setup()
    _L0_c = _w((lambda *s: np.random.randn(*s).astype(np.float32) * 0.05)(1, 256))
    _L0_wmod = _w((lambda *s: np.random.randn(*s).astype(np.float32) * 0.05)(256, 6 * 256) * 256 ** (-0.5))

    def _L1_attn_setup():
        import jax, jax.numpy as jnp
        import numpy as np
        key = jax.random.key(seed)
        k1, k2, k3 = jax.random.split(key, 3)
        B, S, D, N = (2, 512, 256, 16)
        H = D // N
        x = jax.random.normal(k1, (B, S, D), dtype=jnp.float32)
        W_qkv = jax.random.normal(k2, (N, D, 3 * H), dtype=jnp.float32) / np.sqrt(D).astype(np.float32)
        W_out = jax.random.normal(k3, (N, H, D), dtype=jnp.float32) / np.sqrt(D).astype(np.float32)
        return {'x': x, 'W_qkv': W_qkv, 'W_out': W_out}
    _L1_attn_in = _L1_attn_setup()

    def _L1_ffn_setup():
        import jax, jax.numpy as jnp
        import numpy as np
        B, S, D = (2, 512, 256)
        DFF = 512
        E_FFN = 8
        E_ZERO = 4
        E_TOT = E_FFN + E_ZERO
        TOP_K = 2
        key = jax.random.key(seed)
        k1, k2, k3, k4 = jax.random.split(key, 4)
        x = jax.random.normal(k1, (B, S, D), dtype=jnp.float32)
        gate_w = jax.random.normal(k2, (E_TOT, D), dtype=jnp.float32) * (1.0 / np.sqrt(D))
        expert_bias = jnp.zeros((E_TOT,), dtype=jnp.float32)
        w1 = jax.random.normal(k3, (E_FFN, DFF, D), dtype=jnp.float32) * (1.0 / np.sqrt(D))
        w2 = jax.random.normal(k4, (E_FFN, D, DFF), dtype=jnp.float32) * (1.0 / np.sqrt(DFF))
        return {'x': x, 'gate_w': gate_w, 'expert_bias': expert_bias, 'w1': w1, 'w2': w2}
    _L1_ffn_in = _L1_ffn_setup()
    _L1_c = _w((lambda *s: np.random.randn(*s).astype(np.float32) * 0.05)(1, 256))
    _L1_wmod = _w((lambda *s: np.random.randn(*s).astype(np.float32) * 0.05)(256, 6 * 256) * 256 ** (-0.5))
    _d = {'L0_attn_encodings': _L0_attn_in['encodings'], 'L0_attn_attn_W': _L0_attn_in['attn_W'], 'L0_attn_attn_b': _L0_attn_in['attn_b'], 'L0_attn_out_W': _L0_attn_in['out_W'], 'L0_attn_out_b': _L0_attn_in['out_b'], 'L0_ffn_gate_w': _L0_ffn_in['gate_w'], 'L0_ffn_shared_gate_w': _L0_ffn_in['shared_gate_w'], 'L0_ffn_shared_gate_up_w': _L0_ffn_in['shared_gate_up_w'], 'L0_ffn_shared_down_w': _L0_ffn_in['shared_down_w'], 'L0_ffn_expert_gate_up_w': _L0_ffn_in['expert_gate_up_w'], 'L0_ffn_expert_down_w': _L0_ffn_in['expert_down_w'], 'L0_c': _L0_c, 'L0_wmod': _L0_wmod, 'L1_attn_W_qkv': _L1_attn_in['W_qkv'], 'L1_attn_W_out': _L1_attn_in['W_out'], 'L1_ffn_gate_w': _L1_ffn_in['gate_w'], 'L1_ffn_expert_bias': _L1_ffn_in['expert_bias'], 'L1_ffn_w1': _L1_ffn_in['w1'], 'L1_ffn_w2': _L1_ffn_in['w2'], 'L1_c': _L1_c, 'L1_wmod': _L1_wmod}
    _x0 = _d['L0_attn_encodings']
    _d['L0_attn_encodings'] = jax.random.normal(jax.random.fold_in(jax.random.key(seed), 1), (1, 4096, 256), dtype=_x0.dtype)
    del _x0
    return _d

def reference(L0_attn_encodings, L0_attn_attn_W, L0_attn_attn_b, L0_attn_out_W, L0_attn_out_b, L0_ffn_gate_w, L0_ffn_shared_gate_w, L0_ffn_shared_gate_up_w, L0_ffn_shared_down_w, L0_ffn_expert_gate_up_w, L0_ffn_expert_down_w, L0_c, L0_wmod, L1_attn_W_qkv, L1_attn_W_out, L1_ffn_gate_w, L1_ffn_expert_bias, L1_ffn_w1, L1_ffn_w2, L1_c, L1_wmod):

    def _L0_attn_ref(encodings, attn_W, attn_b, out_W, out_b):
        import jax, jax.numpy as jnp
        import numpy as np
        import math
        B, N, D, H = (1, 1024, 256, 16)
        HS = D // H
        NEG_INF = -10000.0
        b, n, d = encodings.shape
        qkv = encodings @ attn_W + attn_b
        qkv = qkv.reshape(b, n, H, 3 * HS).transpose(0, 2, 1, 3)
        q, k, v = jnp.split(qkv, 3, axis=-1)
        scores = jnp.einsum('bhki,bhqi->bhkq', k, q) / math.sqrt(HS)
        mask = jnp.arange(n)[:, None] <= jnp.arange(n)[None, :]
        scores = jnp.where(mask, scores, jnp.float32(NEG_INF))
        prob = jax.nn.softmax(scores, axis=2)
        combined = jnp.einsum('bhkq,bhkl->bhql', prob, v)
        out = combined.transpose(0, 2, 1, 3).reshape(b, n, d)
        return out @ out_W + out_b

    def _L0_ffn_ref(hidden_states, gate_w, shared_gate_w, shared_gate_up_w, shared_down_w, expert_gate_up_w, expert_down_w):
        import jax, jax.numpy as jnp
        import numpy as np
        TOP_K = 8
        CAPACITY = 128

        def _silu(x):
            return x * jax.nn.sigmoid(x)
        B, S, H = hidden_states.shape
        x = hidden_states.reshape(-1, H)
        T = x.shape[0]
        E = gate_w.shape[1]
        Is = shared_gate_up_w.shape[1] // 2
        I = expert_gate_up_w.shape[2] // 2
        gu = x @ shared_gate_up_w
        shared = _silu(gu[:, :Is]) * gu[:, Is:] @ shared_down_w
        shared = shared * jax.nn.sigmoid(x @ shared_gate_w)
        logits = x @ gate_w
        probs = jax.nn.softmax(logits.astype(jnp.float32), axis=-1)
        w, idx = jax.lax.top_k(probs, TOP_K)
        w = (w / jnp.sum(w, axis=-1, keepdims=True)).astype(x.dtype)
        e_flat = idx.reshape(-1)
        w_flat = w.reshape(-1)
        A = e_flat.shape[0]
        tok = jnp.arange(A) // TOP_K
        onehot = jax.nn.one_hot(e_flat, E, dtype=jnp.int32)
        pos = jnp.take_along_axis(jnp.cumsum(onehot, axis=0) - 1, e_flat[:, None], axis=1)[:, 0]
        slot = jnp.minimum(pos, CAPACITY)
        buf = jnp.zeros((E, CAPACITY + 1, H), x.dtype).at[e_flat, slot].set(x[tok])
        gu_e = jnp.einsum('ech,ehf->ecf', buf, expert_gate_up_w)
        act = _silu(gu_e[..., :I]) * gu_e[..., I:]
        out_e = jnp.einsum('eci,eih->ech', act, expert_down_w)
        y = out_e[e_flat, slot] * w_flat[:, None]
        y = jnp.where((pos < CAPACITY)[:, None], y, jnp.zeros_like(y))
        y = y.reshape(T, TOP_K, H).sum(axis=1)
        return (y + shared).reshape(B, S, H)

    def _L1_attn_ref(x, W_qkv, W_out):
        import jax, jax.numpy as jnp
        import numpy as np
        B, S, D = x.shape
        head_dim = W_qkv.shape[-1] // 3
        qkv = jnp.einsum('bsd,ndh->bnsh', x, W_qkv)
        q, k, v = jnp.split(qkv, 3, axis=-1)
        scale = jnp.asarray(1.0 / np.sqrt(head_dim), dtype=x.dtype)
        attn = jnp.einsum('bnqh,bnkh->bnqk', q, k) * scale
        mask = jnp.asarray(-10000000000.0, dtype=x.dtype) * (1.0 - jnp.tril(jnp.ones((S, S), dtype=x.dtype)))
        attn = jax.nn.softmax(attn + mask, axis=-1)
        out = jnp.einsum('bnqk,bnkh->bnqh', attn, v)
        out = out.reshape(B, -1, S)
        return jnp.einsum('bds,nhd->bsd', out, W_out)

    def _L1_ffn_ref(x, gate_w, expert_bias, w1, w2):
        import jax, jax.numpy as jnp
        import numpy as np
        B, S, D = (2, 512, 256)
        DFF = 512
        E_FFN = 8
        E_ZERO = 4
        E_TOT = E_FFN + E_ZERO
        TOP_K = 2
        logits = jnp.einsum('btd,ed->bte', x, gate_w) + expert_bias
        topk_logits, topk_idx = jax.lax.top_k(logits, TOP_K)
        topk_w = jax.nn.softmax(topk_logits, axis=-1)
        onehot = jax.nn.one_hot(topk_idx, E_TOT, dtype=x.dtype)
        w = jnp.einsum('btk,btke->bte', topk_w, onehot)
        w_ffn = w[..., :E_FFN]
        w_zero = jnp.sum(w[..., E_FFN:], axis=-1)
        h = jax.nn.silu(jnp.einsum('btd,efd->btef', x, w1))
        y = jnp.einsum('btef,edf->bted', h, w2)
        out = jnp.einsum('bte,bted->btd', w_ffn, y) + w_zero[..., None] * x
        return out
    x = L0_attn_encodings
    mod = (_silu(L0_c) @ L0_wmod).reshape(L0_c.shape[0], 6, 1, -1)
    sa, ca, ga, sb, cb, gb = (mod[:, 0], mod[:, 1], mod[:, 2], mod[:, 3], mod[:, 4], mod[:, 5])
    ga = (2 * (ga >= 0) - 1) * jnp.maximum(jnp.abs(ga), 0.25)
    gb = (2 * (gb >= 0) - 1) * jnp.maximum(jnp.abs(gb), 0.25)
    h = _layernorm(x, axis=-1) * (1 + ca) + sa
    x = x + ga * _L0_attn_ref(h, L0_attn_attn_W, L0_attn_attn_b, L0_attn_out_W, L0_attn_out_b)
    h = _layernorm(x, axis=-1) * (1 + cb) + sb
    x = x + gb * _L0_ffn_ref(h, L0_ffn_gate_w, L0_ffn_shared_gate_w, L0_ffn_shared_gate_up_w, L0_ffn_shared_down_w, L0_ffn_expert_gate_up_w, L0_ffn_expert_down_w)
    mod = (_silu(L1_c) @ L1_wmod).reshape(L1_c.shape[0], 6, 1, -1)
    sa, ca, ga, sb, cb, gb = (mod[:, 0], mod[:, 1], mod[:, 2], mod[:, 3], mod[:, 4], mod[:, 5])
    ga = (2 * (ga >= 0) - 1) * jnp.maximum(jnp.abs(ga), 0.25)
    gb = (2 * (gb >= 0) - 1) * jnp.maximum(jnp.abs(gb), 0.25)
    h = _layernorm(x, axis=-1) * (1 + ca) + sa
    x = x + ga * _L1_attn_ref(h, L1_attn_W_qkv, L1_attn_W_out)
    h = _layernorm(x, axis=-1) * (1 + cb) + sb
    x = x + gb * _L1_ffn_ref(h, L1_ffn_gate_w, L1_ffn_expert_bias, L1_ffn_w1, L1_ffn_w2)
    return x

_drawn_inputs = setup_inputs


def setup_inputs(seed=0):
    import zlib

    import numpy as np

    out = dict(_drawn_inputs(seed))
    spreads = {'L1_ffn_expert_bias': (0.0, 2.0)}
    factors = {'L0_attn_attn_W': 8.0,
     'L0_attn_attn_b': 8.0,
     'L0_attn_out_W': 8.0,
     'L0_attn_out_b': 5.959,
     'L0_ffn_gate_w': 4.857,
     'L0_ffn_expert_gate_up_w': 4.539,
     'L0_ffn_expert_down_w': 4.804,
     'L0_ffn_shared_gate_w': 7.361,
     'L1_attn_W_qkv': 4.984,
     'L1_attn_W_out': 5.05,
     'L1_ffn_gate_w': 3.128,
     'L1_ffn_w1': 4.08,
     'L1_ffn_w2': 3.841}
    for name, (base, spread) in spreads.items():
        noise = np.random.default_rng([zlib.crc32(name.encode()), seed]).standard_normal(out[name].shape)
        drawn = base * np.exp(spread * noise) if base else spread * noise
        out[name] = jnp.asarray(drawn.astype(out[name].dtype))
    for name, factor in factors.items():
        out[name] = (out[name] * factor).astype(out[name].dtype)
    return out
```

```python
import concourse.bass as bass
import numpy as np
from concourse import mybir
from contextlib import ExitStack

F32 = mybir.dt.float32
BF16 = mybir.dt.bfloat16
I32 = mybir.dt.int32
U32 = mybir.dt.uint32
ALU = mybir.AluOpType
ACT = mybir.ActivationFunctionType
AX = mybir.AxisListType

P = 128
T = 4096
D = 256
KD = D // P
NT = T // P
CH = 512
NC = T // CH
TPC = CH // P
H = 16
HS = D // H
EPS = 1e-5
MASKED = -1e30
PARTS = 3
PAIRS = [(0, 0), (1, 0), (2, 0), (0, 1), (1, 1), (0, 2)]
SR = len(PAIRS) * HS
MR = SR + PARTS
VC = 32
QUADS = NC * (NC + 1) // 2
LOOK = 12
SLOTS = 2 * QUADS
RING = 3
E0, I0, CAP, TOPK = 64, 128, 128, 8
IS = 512
ROW0 = D + E0
E1, EZ, F1 = 8, 4, 512
ET = E1 + EZ


class Env:
    pass


def new_sem(nc, e, name):
    e.sems.append(e.layer.enter_context(nc.semaphore(name)))
    return e.sems[-1]


def recycle_semaphores(nc, e):
    with nc.Block() as block:
        @block.sync
        def _(sp):
            for s in e.sems:
                sp.sem_clear(s)
    e.layer.close()
    e.sems = []


def settle(eng):
    eng.nop(nofuse=True)


def flat(ap):
    return ap.rearrange("p o d -> p (o d)")


def setup(nc, e, a):
    with ExitStack() as ctx:
        def sb(name, shape, dt=F32):
            return ctx.enter_context(nc.sbuf_tensor(name, shape, dt))

        def sem(name):
            return new_sem(nc, e, name)

        wmod = sb("wmod", [P, 2, KD, 6 * D])
        c_col = sb("c_col", [P, 2, KD])
        c_silu = sb("c_silu", [P, 2, KD])
        c_rep = sb("c_rep", [P, 2, KD, P])
        w_out1 = sb("w_out1", [P, KD, D])
        w_out0_raw = sb("w_out0_raw", [P, KD, D])
        b_out0_raw = sb("b_out0_raw", [1, D])
        guard = sb("guard", [P, 2, D])
        rows = ctx.enter_context(nc.psum_tensor("rows", [P, 10, D], F32))
        cols = ctx.enter_context(nc.psum_tensor("cols", [P, 32], F32))
        small_loaded, wmod_loaded, x_loaded = sem("small_loaded"), sem("wmod_loaded"), sem("x_loaded")
        pool_step, const_made = sem("pool_step"), sem("const_made")
        silu_done, rep_done, mod_done = sem("silu_done"), sem("rep_done"), sem("mod_done")
        step = sem("setup_step")
        NS = 11

        with nc.Block() as block:
            @block.sync
            def _(sp):
                for l, c in enumerate((a.L0_c, a.L1_c)):
                    for k in range(KD):
                        sp.dma_start(c_col[:, l, k:k + 1], c[0:1, k * P:(k + 1) * P].rearrange("o p -> p o")).then_inc(small_loaded, 16)
                sp.dma_start(b_out0_raw[:, :], a.L0_out_b).then_inc(small_loaded, 16)
                sp.dma_start(w_out0_raw[:, :, :], a.L0_out_W.rearrange("(k p) n -> p k n", p=P)).then_inc(small_loaded, 16)
                sp.dma_start(w_out1[:, :, :], a.L1_W_out.rearrange("(k p) n -> p k n", p=P)).then_inc(small_loaded, 16)
                for s in range(2):
                    for g in range(KD):
                        sp.dma_start(e.bias_qk[:, 2 * s + g:2 * s + g + 1],
                                     a.L0_b_qkv[s:s + 1, g * P:(g + 1) * P].rearrange("o p -> p o")).then_inc(small_loaded, 16)
                for l, w in enumerate((a.L0_wmod, a.L1_wmod)):
                    sp.dma_start(wmod[:, l, :, :], w.rearrange("(k p) n -> p k n", p=P)).then_inc(wmod_loaded, 16)
                xv = a.x.rearrange("(c t p) d -> c p t d", t=TPC, p=P)
                for c in range(NC):
                    sp.dma_start(e.X[:, c * TPC:(c + 1) * TPC, :], xv[c]).then_inc(x_loaded, 16)
                sp.wait_ge(x_loaded, 16 * NC)

            @block.gpsimd
            def _(pool):
                nc.gpsimd.memset(e.ident[:, :], 0.0).then_inc(pool_step, 1)
                nc.gpsimd.memset(e.mask_k[:, :], 0.0).then_inc(pool_step, 1)
                nc.gpsimd.memset(e.mask_q[:, 0:CH], MASKED).then_inc(pool_step, 1)
                nc.gpsimd.memset(e.mask_q[:, CH:CH + P], 0.0).then_inc(pool_step, 1)
                nc.gpsimd.memset(e.ones[:, :], 1.0).then_inc(pool_step, 1)
                nc.gpsimd.memset(e.sum4[:, :], 0.0).then_inc(pool_step, 1)
                pool.wait_ge(pool_step, 6)
                nc.gpsimd.affine_select(out=e.ident[:, :], in_=e.ident[:, :], compare_op=ALU.not_equal, fill=1.0,
                                        base=0, pattern=[[-1, P]], channel_multiplier=1).then_inc(const_made, 1)
                nc.gpsimd.affine_select(out=e.mask_k[:, :], in_=e.mask_k[:, :], compare_op=ALU.is_ge, fill=MASKED,
                                        base=0, pattern=[[-1, P]], channel_multiplier=1).then_inc(const_made, 1)
                nc.gpsimd.affine_select(out=e.mask_q[:, CH:CH + P], in_=e.mask_q[:, CH:CH + P], compare_op=ALU.is_ge,
                                        fill=MASKED, base=0, pattern=[[1, P]], channel_multiplier=-1).then_inc(const_made, 1)
                for g in range(4):
                    pool.wait_ge(pool_step, 6 + g)
                    nc.gpsimd.affine_select(out=e.sum4[:, :], in_=e.sum4[:, :], compare_op=ALU.not_equal, fill=1.0,
                                            base=-VC * g, pattern=[[-1, VC]], channel_multiplier=1).then_inc(pool_step, 1)
                pool.wait_ge(const_made, 3)
                pool.wait_ge(pool_step, 10)
                nc.gpsimd.tensor_copy(e.ident_b[:, :], e.ident[:, :]).then_inc(const_made, 1)

            @block.scalar
            def _(act):
                act.wait_ge(small_loaded, 16 * NS)
                nc.scalar.activation(c_silu[:, :, :], c_col[:, :, :], ACT.Silu).then_inc(silu_done, 1)

            @block.vector
            def _(dve):
                n = [0]

                def link(ins):
                    n[0] += 1
                    ins.then_inc(step, 1)
                    dve.wait_ge(step, n[0])

                dve.wait_ge(silu_done, 1)
                dve.wait_ge(pool_step, 5)
                for l in range(2):
                    for k in range(KD):
                        nc.vector.tensor_scalar(c_rep[:, l, k, :], e.ones[:, :], c_silu[:, l, k:k + 1], None, ALU.mult).then_inc(rep_done, 1)
                dve.wait_ge(mod_done, 1)
                nc.vector.tensor_scalar(e.bias_qk[:, 0:KD], e.bias_qk[:, 0:KD], HS ** -0.5, None, ALU.mult)
                link(nc.vector.tensor_copy(e.col[:, :], cols[:, 0:24]))
                for l in range(2):
                    for w in (1, 4):
                        j = (l * 6 + w) * KD
                        link(nc.vector.tensor_scalar(e.col[:, j:j + KD], e.col[:, j:j + KD], 1.0, None, ALU.add))
                nc.vector.tensor_copy(e.row_sb0[:, :], rows[:, 2, :])
                nc.vector.tensor_scalar(e.row_cb0[:, :], rows[:, 3, :], 1.0, None, ALU.add)
                nc.vector.tensor_copy(e.row_sb1[:, :], rows[:, 6, :])
                nc.vector.tensor_scalar(e.row_cb1[:, :], rows[:, 7, :], 1.0, None, ALU.add)
                for src, dst in ((0, e.row_ga0), (1, e.row_gb0), (4, e.row_ga1), (5, e.row_gb1)):
                    link(nc.vector.tensor_scalar(guard[:, 1, :], rows[:, src, :], 0.0, 2.0, ALU.is_ge, ALU.mult))
                    link(nc.vector.tensor_scalar(guard[:, 1, :], guard[:, 1, :], 1.0, None, ALU.subtract))
                    link(nc.vector.tensor_tensor(guard[:, 0, :], guard[:, 1, :], rows[:, src, :], ALU.mult))
                    link(nc.vector.tensor_scalar(guard[:, 0, :], guard[:, 0, :], 0.25, None, ALU.max))
                    link(nc.vector.tensor_tensor(dst[:, :], guard[:, 0, :], guard[:, 1, :], ALU.mult))
                link(nc.vector.tensor_tensor(e.row_ga1[:, :], e.row_ga1[:, :], rows[:, 8, :], ALU.mult))
                for k in range(KD):
                    nc.vector.tensor_tensor(e.w_out0[:, k, :], w_out0_raw[:, k, :], e.row_ga0[:, :], ALU.mult)
                link(nc.vector.tensor_tensor(e.b_out0[:, :], b_out0_raw[:, :], e.row_ga0[0:1, :], ALU.mult))

            @block.tensor
            def _(pe):
                pe.wait_ge(wmod_loaded, 32)
                pe.wait_ge(silu_done, 1)
                for l in range(2):
                    for w in range(6):
                        for g in range(KD):
                            j = (l * 6 + w) * KD + g
                            for k in range(KD):
                                nc.tensor.matmul(cols[:, j:j + 1], wmod[:, l, k, w * D + g * P:w * D + (g + 1) * P],
                                                 c_silu[:, l, k:k + 1], start=(k == 0), stop=(k == KD - 1))
                pe.wait_ge(rep_done, 2 * KD)
                for j, (l, w) in enumerate(((0, 2), (0, 5), (0, 3), (0, 4), (1, 2), (1, 5), (1, 3), (1, 4))):
                    for k in range(KD):
                        nc.tensor.matmul(rows[:, j, :], c_rep[:, l, k, :], wmod[:, l, k, w * D:(w + 1) * D],
                                         start=(k == 0), stop=(k == KD - 1))
                for k in range(KD):
                    last = nc.tensor.matmul(rows[:, 8, :], e.ones[:, :], w_out1[:, k, :], start=(k == 0), stop=(k == KD - 1))
                last.then_inc(mod_done, 1)


def norm_stats(nc, e, dve, tag, step, stats_ready, root_done, src):
    n = 0
    for t in range(NT):
        nc.vector.bn_stats(e.bn6[:, t, :], src(t)).then_inc(step, 1)
    n += NT
    dve.wait_ge(step, n)
    for t in range(NT):
        nc.vector.bn_aggr(e.mv[:, t, :], e.bn6[:, t, :]).then_inc(step, 1)
    n += NT
    dve.wait_ge(step, n)
    nc.vector.tensor_scalar(e.var[:, :], e.mv[:, :, 1], EPS, None, ALU.add).then_inc(stats_ready, 1)
    dve.wait_ge(root_done, 1)
    nc.vector.reciprocal(e.rstd[:, :], e.root[:, :]).then_inc(step, 1)
    dve.wait_ge(step, n + 1)
    nc.vector.tensor_tensor(e.newt[:, :], e.rstd[:, :], e.rstd[:, :], ALU.mult).then_inc(step, 1)
    dve.wait_ge(step, n + 2)
    nc.vector.tensor_tensor(e.newt[:, :], e.newt[:, :], e.var[:, :], ALU.mult).then_inc(step, 1)
    dve.wait_ge(step, n + 3)
    nc.vector.tensor_scalar(e.newt[:, :], e.newt[:, :], -0.5, 1.5, ALU.mult, ALU.add).then_inc(step, 1)
    dve.wait_ge(step, n + 4)
    nc.vector.tensor_tensor(e.rstd[:, :], e.rstd[:, :], e.newt[:, :], ALU.mult).then_inc(step, 1)
    dve.wait_ge(step, n + 5)
    return n + 5


def project(nc, e, l, w_qkv, bias_v):
    with ExitStack() as ctx:
        def sb(name, shape, dt=F32):
            return ctx.enter_context(nc.sbuf_tensor(f"{name}{l}", shape, dt))

        def ps(name, shape):
            return ctx.enter_context(nc.psum_tensor(f"{name}{l}", shape, F32))

        def sem(name):
            return new_sem(nc, e, f"pr{l}_{name}")

        w = sb("w_qkv", [P, 3, KD, D])
        bv = sb("bv", [P, D])
        xn = sb("xn", [P, 2, TPC, D])
        hT = sb("hT", [P, 2, KD, CH])
        t32 = sb("t32", [P, 2, CH])
        rest = sb("rest", [P, 2, CH])
        part = sb("part", [P, 2, PARTS, CH], BF16)
        tp = ps("tp", [P, KD, CH])
        qk = ps("qk", [P, 2, CH])
        vp = ps("vp", [P, 2, TPC // 2, D])
        w_loaded, step, stats_ready, root_done = sem("w_loaded"), sem("step"), sem("stats"), sem("root")
        xn_ready, tp_ready, hT_ready = sem("xn_ready"), sem("tp_ready"), sem("hT_ready")
        qk_ready, t32_ready, first_ready, rest_ready = sem("qk_ready"), sem("t32_ready"), sem("first_ready"), sem("rest_ready")
        second_ready, third_ready = sem("second_ready"), sem("third_ready")
        v_ready, v_taken = sem("v_ready"), sem("v_taken")
        stored = [sem("stored0"), sem("stored1")]
        ca, sa = (l * 6 + 1) * KD, (l * 6) * KD
        M = 4

        with nc.Block() as block:
            @block.sync
            def _(sp):
                sp.dma_start(w[:, :, :, :], w_qkv.rearrange("(k p) s n -> p s k n", p=P)).then_inc(w_loaded, 16)
                if bias_v is not None:
                    sp.dma_start(bv[:, :], bias_v.to_broadcast([P, D])).then_inc(w_loaded, 16)

                def body(i):
                    for u in range(2):
                        for m in range(M):
                            sp.wait_ge(third_ready, i * 2 * M + u * M + m + 1)
                            sp.wait_ge(second_ready, i * 2 * M + u * M + m + 1)
                            sp.wait_ge(first_ready, i * 2 * M + u * M + m + 1)
                            dst = (e.q_dram, e.k_dram)[m // KD]
                            g = m % KD
                            sp.dma_start(dst[:, g * P:(g + 1) * P, bass.ds(i * 2 * CH + u * CH, CH)].rearrange("s r t -> r s t"),
                                         part[:, m % 2, :, :]).then_inc(stored[m % 2], 16)

                with sp.Fori(0, NC // 2, 1) as i:
                    body(i)
                for s in stored:
                    sp.wait_ge(s, NC * M // 2 * 16)

            @block.vector
            def _(dve):
                if bias_v is None:
                    nc.vector.memset(bv[:, :], 0.0).then_inc(step, 1)
                    dve.wait_ge(step, 1)
                norm_stats(nc, e, dve, l, sem("norm_step"), stats_ready, root_done, lambda t: e.X[:, t, :])
                if bias_v is not None:
                    dve.wait_ge(w_loaded, 32)

                def normalise(i, u):
                    for t in range(TPC):
                        tile = i * 2 * TPC + u * TPC + t
                        nc.vector.tensor_scalar(xn[:, u, t, :], flat(e.X[:, bass.ds(tile, 1), :]),
                                                e.mv[:, bass.ds(tile, 1), 0], e.rstd[:, bass.ds(tile, 1)],
                                                ALU.subtract, ALU.mult).then_inc(xn_ready, 1)

                def rests(i, u, m):
                    dve.wait_ge(first_ready, i * 2 * M + u * M + m + 1)
                    nc.vector.tensor_tensor(rest[:, m % 2, :], t32[:, m % 2, :], part[:, m % 2, 0, :], ALU.subtract).then_inc(rest_ready, 1)

                with dve.Fori(0, NC // 2, 1) as i:
                    for u in range(2):
                        normalise(i, u)
                        for m in range(M):
                            rests(i, u, m)
                        for q in range(TPC // 2):
                            dve.wait_ge(v_ready, i * 2 * 2 + u * 2 + q + 1)
                            for r in range(2):
                                tile = i * 2 * TPC + u * TPC + q * 2 + r
                                nc.vector.tensor_tensor(
                                    e.V[:, :, bass.ds(tile, 1), :].rearrange("p h o c -> p h (o c)"),
                                    vp[:, q, r, :].rearrange("p (h c) -> p h c", h=H),
                                    bv[:, :].rearrange("p (h c) -> p h c", h=H), ALU.add).then_inc(v_taken, 1)

            @block.scalar
            def _(act):
                act.wait_ge(stats_ready, 1)
                nc.scalar.activation(e.root[:, :], e.var[:, :], ACT.Sqrt).then_inc(root_done, 1)

                with act.Fori(0, NC // 2, 1) as i:
                    for u in range(2):
                        for k in range(KD):
                            act.wait_ge(tp_ready, i * 2 * KD + u * KD + k + 1)
                            nc.scalar.activation(hT[:, u, k, :], tp[:, k, :], ACT.Identity,
                                                 bias=e.col[:, sa + k:sa + k + 1], scale=e.col[:, ca + k:ca + k + 1]).then_inc(hT_ready, 1)
                        for m in range(M):
                            n = i * 2 * M + u * M + m
                            act.wait_ge(qk_ready, n + 1)
                            scale = HS ** -0.5 if m < KD else 1.0
                            if l == 0:
                                nc.scalar.activation(t32[:, m % 2, :], qk[:, m % 2, :], ACT.Identity,
                                                     bias=e.bias_qk[:, m:m + 1], scale=scale).then_inc(t32_ready, 1)
                            else:
                                nc.scalar.activation(t32[:, m % 2, :], qk[:, m % 2, :], ACT.Copy, scale=scale).then_inc(t32_ready, 1)
                            act.wait_ge(t32_ready, n + 1)
                            act.wait_ge(stored[m % 2], (i * M + u * (M // 2) + m // 2) * 16)
                            nc.scalar.activation(part[:, m % 2, 0, :], t32[:, m % 2, :], ACT.Copy).then_inc(first_ready, 1)
                            act.wait_ge(rest_ready, n + 1)
                            nc.scalar.activation(part[:, m % 2, 1, :], rest[:, m % 2, :], ACT.Copy).then_inc(second_ready, 1)

            @block.gpsimd
            def _(pool):
                with pool.Fori(0, NC // 2, 1) as i:
                    for u in range(2):
                        for m in range(M):
                            pool.wait_ge(second_ready, i * 2 * M + u * M + m + 1)
                            nc.gpsimd.tensor_tensor(part[:, m % 2, 2, :], rest[:, m % 2, :], part[:, m % 2, 1, :],
                                                    ALU.subtract).then_inc(third_ready, 1)

            @block.tensor
            def _(pe):
                pe.wait_ge(w_loaded, 16 if bias_v is None else 32)
                with pe.Fori(0, NC // 2, 1) as i:
                    for u in range(2):
                        for k in range(KD):
                            pe.wait_ge(xn_ready, i * 2 * TPC + (u + 1) * TPC)
                            pe.wait_ge(hT_ready, i * 2 * KD + u * KD)
                            for t in range(TPC):
                                last = nc.tensor.transpose(tp[:, k, t * P:(t + 1) * P], xn[:, u, t, k * P:(k + 1) * P], e.ident[:, :])
                            last.then_inc(tp_ready, 1)
                        pe.wait_ge(hT_ready, i * 2 * KD + (u + 1) * KD)
                        for m in range(M):
                            if m >= 2:
                                pe.wait_ge(t32_ready, i * 2 * M + u * M + m - 1)
                            else:
                                pe.wait_ge(t32_ready, i * 2 * M + u * M)
                            for k in range(KD):
                                last = nc.tensor.matmul(qk[:, m % 2, :], w[:, m // KD, k, (m % KD) * P:(m % KD + 1) * P],
                                                        hT[:, u, k, :], start=(k == 0), stop=(k == KD - 1))
                            last.then_inc(qk_ready, 1)
                        for q in range(TPC // 2):
                            pe.wait_ge(v_taken, i * 2 * TPC + u * TPC)
                            for r in range(2):
                                t = q * 2 + r
                                for k in range(KD):
                                    last = nc.tensor.matmul(vp[:, q, r, :], hT[:, u, k, t * P:(t + 1) * P], w[:, 2, k, :],
                                                            start=(k == 0), stop=(k == KD - 1))
                            last.then_inc(v_ready, 1)


def chunk_plan():
    plan = []
    for h in range(2):
        for j in reversed(range(NC)):
            for u in range(j + 1):
                plan.append((h, j, u, u == 0, u == j))
    return plan


def attention(nc, e, l):
    plan = chunk_plan()
    with ExitStack() as ctx:
        def sb(name, shape, dt=F32):
            return ctx.enter_context(nc.sbuf_tensor(f"{name}_a{l}", shape, dt))

        def ps(name, shape):
            return ctx.enter_context(nc.psum_tensor(f"{name}_a{l}", shape, F32))

        def sem(name):
            return new_sem(nc, e, f"at{l}_{name}")

        q_stack = [sb(f"q_stack{p}", [P, T], BF16) for p in range(2)]
        k_stack = [sb(f"k_stack{p}", [P, T], BF16) for p in range(2)]
        v_head = sb("v_head", [P, 2, NT, VC])
        prob = sb("prob", [P, RING, TPC, CH])
        acc_sb = sb("acc_sb", [P, CH])
        block_max = sb("block_max", [P, 2, TPC, NC])
        neg_max = sb("neg_max", [P, TPC])
        neg_rest = sb("neg_rest", [P, TPC])
        neg_part = sb("neg_part", [P, TPC, PARTS], BF16)
        recip = sb("recip", [P, TPC])
        scores = ps("scores", [P, 2, 2, CH])
        tops = ps("tops", [P, 2, CH])
        acc = ps("acc", [P, CH])
        aux = ps("aux", [P, CH])
        neg_ps = aux[:, 0:CH // 2].bitcast(BF16)
        out_ps = aux[:, CH // 2:CH // 2 + TPC * VC].rearrange("p (t c) -> p t c", t=TPC)

        loaded = [sem("loaded0"), sem("loaded1")]
        ones_set, v_staged = sem("ones_set"), sem("v_staged")
        scores_ready, exp_done, pv_done, acc_saved = sem("scores_ready"), sem("exp_done"), sem("pv_done"), sem("acc_saved")
        top_ready, top_taken = sem("top_ready"), sem("top_taken")
        neg_ready, neg_rows_ready, neg_rows_set = sem("neg_ready"), sem("neg_rows_ready"), sem("neg_rows_set")
        out_ready, out_taken = sem("out_ready"), sem("out_taken")
        recip_done, step = sem("recip_done"), sem("step")
        LOADS = 2 * len(PAIRS) * 16
        ITERS = H // 2
        CHUNKS = 2 * NC

        def chunks_before(n):
            return (n // SLOTS) * CHUNKS + sum(1 for x in plan[:n % SLOTS] if x[4])

        def chunk_of(c):
            return (c // NC) % 2, NC - 1 - c % NC

        HEAD2 = QUADS
        assert SLOTS % RING == 0 and not any(plan[LOOK - d][4] for d in (1, 2, 3))

        with nc.Block() as block:
            @block.sync
            def _(sp):
                def load(p, head):
                    for n, (a, b) in enumerate(PAIRS):
                        sp.dma_start(q_stack[p][n * HS:(n + 1) * HS, :], e.q_heads[a, bass.ds(head, 1), :, :].rearrange("o r t -> (o r) t")
                                     ).then_inc(loaded[p], 16)
                        sp.dma_start(k_stack[p][n * HS:(n + 1) * HS, :], e.k_heads[b, bass.ds(head, 1), :, :].rearrange("o r t -> (o r) t")
                                     ).then_inc(loaded[p], 16)

                load(0, 0)
                load(1, 1)
                with sp.Fori(0, ITERS - 1, 1) as i:
                    for p in range(2):
                        sp.wait_ge(scores_ready, i * 2 * SLOTS + 2 * (HEAD2 * (p + 1)))
                        load(p, i * 2 + 2 + p)
                sp.wait_ge(scores_ready, (ITERS - 1) * 2 * SLOTS + 2 * HEAD2)
                load(0, 0)
                sp.wait_ge(loaded[0], LOADS * (ITERS + 1))

            @block.gpsimd
            def _(pool):
                for p in range(2):
                    nc.gpsimd.memset(k_stack[p][SR:P, :], 1.0).then_inc(ones_set, 1)
                pool.wait_ge(ones_set, 2)
                nc.gpsimd.memset(v_head[:, :, :, HS:VC], 0.0).then_inc(ones_set, 1)
                pool.wait_ge(ones_set, 3)
                nc.gpsimd.memset(v_head[:, :, :, HS:HS + 1], 1.0).then_inc(ones_set, 1)

                def stage(p, head):
                    nc.gpsimd.tensor_copy(v_head[:, p, :, 0:HS], e.V[:, bass.ds(head, 1), :, :].rearrange("p o t c -> p (o t) c")
                                          ).then_inc(v_staged, 1)

                pool.wait_ge(ones_set, 4)
                stage(0, 0)
                stage(1, 1)
                with pool.Fori(0, ITERS - 1, 1) as i:
                    for p in range(2):
                        pool.wait_ge(pv_done, i * SLOTS + HEAD2 * (p + 1))
                        stage(p, i * 2 + 2 + p)

            @block.tensor
            def _(pe):
                def main_scores(i, n, half):
                    h, j, u, first, last = plan[n % SLOTS]
                    if n > 0:
                        pe.wait_ge(exp_done, i * 2 * SLOTS + 2 * n + half - 1)
                    if half == 0 and first:
                        pe.wait_ge(neg_rows_set, i * CHUNKS + chunks_before(n) + 1)
                    for b in range(2):
                        kb = 2 * half + b
                        diag = u == j
                        c0 = P * kb if diag and j else 0
                        last_mm = nc.tensor.matmul(scores[:, half, b, c0:CH],
                                                   k_stack[h][0:MR, u * CH + kb * P:u * CH + (kb + 1) * P],
                                                   q_stack[h][0:MR, j * CH + c0:(j + 1) * CH], start=True, stop=not diag)
                        if diag:
                            m0 = P * kb if j else 0
                            last_mm = nc.tensor.matmul(scores[:, half, b, m0:P * (kb + 1)], e.ident_b[:, :],
                                                       e.mask_q[:, CH - (P * kb - m0):CH + P], start=False, stop=True)
                    last_mm.then_inc(scores_ready, 1)

                def top_scores(i, n, t):
                    h, j, u, first, last = plan[n % SLOTS]
                    m = 4 * n + t
                    if m >= 2:
                        pe.wait_ge(top_taken, i * TPC * SLOTS + m - 1)
                    if t == 0 and j == NC - 1 and first:
                        pe.wait_ge(loaded[h], i * LOADS + (n // SLOTS + 1) * LOADS)
                    diag = u == j
                    width = P * (t + 1) if diag else CH
                    last_mm = nc.tensor.matmul(tops[:, m % 2, 0:width], q_stack[h][0:SR, j * CH + t * P:j * CH + (t + 1) * P],
                                               k_stack[h][0:SR, u * CH:u * CH + width], start=True, stop=not diag)
                    if diag:
                        last_mm = nc.tensor.matmul(tops[:, m % 2, t * P:width], e.ident_b[:, :], e.mask_k[:, :], start=False, stop=True)
                    last_mm.then_inc(top_ready, 1)

                def neg_rows(i, c, outs):
                    pe.wait_ge(neg_ready, i * CHUNKS + c + 1)
                    if c:
                        pe.wait_ge(neg_rows_set, i * CHUNKS + c)
                    if outs is not None:
                        pe.wait_ge(out_taken, i * CHUNKS + outs)
                    for t in range(TPC):
                        last_mm = nc.tensor.transpose(neg_ps[SR:SR + PARTS, t * P:(t + 1) * P], neg_part[:, t, :], e.ident_b[:, :])
                    last_mm.then_inc(neg_rows_ready, 1)

                def outputs(i, c, rows):
                    pe.wait_ge(acc_saved, i * CHUNKS + c + 1)
                    pe.wait_ge(out_taken, i * CHUNKS + c)
                    pe.wait_ge(neg_rows_set, i * CHUNKS + rows)
                    for t in range(TPC):
                        last_mm = nc.tensor.matmul(out_ps[:, t, :], acc_sb[:, t * P:(t + 1) * P], e.sum4[:, :], start=True, stop=True)
                    last_mm.then_inc(out_ready, 1)

                def weigh(i, n):
                    h, j, u, first, last = plan[n]
                    pe.wait_ge(exp_done, i * 2 * SLOTS + 2 * n + 2)
                    if first:
                        pe.wait_ge(acc_saved, i * CHUNKS + chunks_before(n))
                        if j == NC - 1:
                            pe.wait_ge(v_staged, i * 2 + h + 1)
                    for kb in range(TPC):
                        c0 = P * kb if u == j and j else 0
                        last_mm = nc.tensor.matmul(acc[VC * kb:VC * (kb + 1), c0:CH], v_head[:, h, u * TPC + kb, :],
                                                   prob[:, n % RING, kb, c0:CH], start=first, stop=last, skip_group_check=True)
                    last_mm.then_inc(pv_done, 1)

                pe.wait_ge(ones_set, 4)
                pe.wait_ge(loaded[1], LOADS)
                for n in range(LOOK):
                    for t in range(TPC):
                        top_scores(0, n, t)
                    if n >= 2 and plan[n - 2][4]:
                        neg_rows(0, chunks_before(n - 2), None)
                main_scores(0, 0, 0)
                main_scores(0, 0, 1)

                with pe.Fori(0, ITERS, 1) as i:
                    for n in range(SLOTS):
                        ahead = n + LOOK
                        main_scores(i, n + 1, 0)
                        top_scores(i, ahead, 0)
                        main_scores(i, n + 1, 1)
                        top_scores(i, ahead, 1)
                        top_scores(i, ahead, 2)
                        if plan[(ahead - 2) % SLOTS][4]:
                            neg_rows(i, chunks_before(ahead - 2), chunks_before(max(n - 1, 0)))
                        weigh(i, n)
                        top_scores(i, ahead, 3)
                        if n > 0 and plan[n - 1][4]:
                            outputs(i, chunks_before(n - 1), chunks_before(ahead - 1))
                    outputs(i, CHUNKS - 1, chunks_before(SLOTS + LOOK - 2))

            @block.scalar
            def _(act):
                def neg_rows_out(i, c):
                    act.wait_ge(neg_rows_ready, i * CHUNKS + c + 1)
                    h, j = chunk_of(c)
                    nc.scalar.activation(q_stack[h][SR:SR + PARTS, j * CH:(j + 1) * CH], neg_ps[SR:SR + PARTS, :], ACT.Copy).then_inc(neg_rows_set, 1)

                def exps(i, n, half):
                    h, j, u, first, last = plan[n % SLOTS]
                    act.wait_ge(scores_ready, i * 2 * SLOTS + 2 * n + half + 1)
                    c0 = 2 * P if u == j and j and half else 0
                    nc.scalar.activation(prob[:, n % RING, 2 * half:2 * half + 2, c0:CH], scores[:, half, :, c0:CH], ACT.Exp
                                         ).then_inc(exp_done, 1)

                def save(i, n):
                    act.wait_ge(pv_done, i * SLOTS + n + 1)
                    if chunks_before(n):
                        act.wait_ge(out_ready, i * CHUNKS + chunks_before(n))
                    nc.scalar.activation(acc_sb[:, :], acc[:, :], ACT.Copy).then_inc(acc_saved, 1)

                for n in range(LOOK - 2):
                    if plan[n][4]:
                        neg_rows_out(0, chunks_before(n))
                with act.Fori(0, ITERS, 1) as i:
                    for n in range(SLOTS):
                        if n >= RING:
                            act.wait_ge(pv_done, i * SLOTS + n - RING + 1)
                        exps(i, n, 0)
                        exps(i, n, 1)
                        if n and plan[(n + LOOK - 3) % SLOTS][4]:
                            neg_rows_out(i, chunks_before(n + LOOK - 3))
                        if n and plan[n - 1][4]:
                            save(i, n - 1)
                    save(i, SLOTS - 1)

            @block.vector
            def _(dve):
                CHAIN = 3

                def top(i, n, t):
                    h, j, u, first, last = plan[n % SLOTS]
                    m = 4 * n + t
                    dve.wait_ge(top_ready, i * TPC * SLOTS + m + 1)
                    width = P * (t + 1) if u == j else CH
                    nc.vector.tensor_reduce(block_max[:, j % 2, t, u:u + 1], tops[:, m % 2, 0:width], AX.X, ALU.max).then_inc(top_taken, 1)

                def negate(i, n, s):
                    j, c = plan[n % SLOTS][1], chunks_before(n)
                    seen = i * CHUNKS * CHAIN + CHAIN * c
                    if s == 0:
                        dve.wait_ge(top_taken, i * TPC * SLOTS + TPC * (n + 1))
                        if c:
                            dve.wait_ge(neg_rows_ready, i * CHUNKS + c)
                        nc.vector.tensor_reduce(neg_part[:, :, 0], block_max[:, j % 2, :, 0:j + 1], AX.X, ALU.max, negate=True)
                        nc.vector.tensor_reduce(neg_max[:, :], block_max[:, j % 2, :, 0:j + 1], AX.X, ALU.max, negate=True).then_inc(step, 1)
                    elif s == 1:
                        dve.wait_ge(step, seen + 1)
                        nc.vector.tensor_tensor(neg_rest[:, :], neg_max[:, :], neg_part[:, :, 0], ALU.subtract).then_inc(step, 1)
                    elif s == 2:
                        dve.wait_ge(step, seen + 2)
                        nc.vector.tensor_copy(neg_part[:, :, 1], neg_rest[:, :]).then_inc(step, 1)
                    else:
                        dve.wait_ge(step, seen + 3)
                        nc.vector.tensor_tensor(neg_part[:, :, 2], neg_rest[:, :], neg_part[:, :, 1], ALU.subtract).then_inc(neg_ready, 1)

                def normalise(i, c, s):
                    h, j = chunk_of(c)
                    if s == 0:
                        dve.wait_ge(out_ready, i * CHUNKS + c + 1)
                        nc.vector.reciprocal(recip[:, :], out_ps[:, :, HS]).then_inc(recip_done, 1)
                    else:
                        dve.wait_ge(recip_done, i * CHUNKS + c + 1)
                        nc.vector.tensor_tensor(e.O[:, j * TPC:(j + 1) * TPC, bass.ds((i * 2 + h) * HS, HS)],
                                                out_ps[:, :, 0:HS], recip[:, :].rearrange("p (t o) -> p t o", o=1).to_broadcast([P, TPC, HS]),
                                                ALU.mult).then_inc(out_taken, 1)

                def tops_down(i, n, out_chunk):
                    for t in range(TPC):
                        top(i, n, t)
                        if n and plan[(n - 1) % SLOTS][4]:
                            negate(i, n - 1, t)
                        if out_chunk is not None and t < 2:
                            normalise(i, out_chunk, t)

                for n in range(LOOK):
                    tops_down(0, n, None)
                with dve.Fori(0, ITERS, 1) as i:
                    for n in range(SLOTS):
                        tops_down(i, n + LOOK, chunks_before(n - 2) if n > 1 and plan[n - 2][4] else None)
                    for c in (CHUNKS - 2, CHUNKS - 1):
                        normalise(i, c, 0)
                        normalise(i, c, 1)


def project_out(nc, e):
    with ExitStack() as ctx:
        def sem(name):
            return new_sem(nc, e, f"po_{name}")

        o_in = ctx.enter_context(nc.sbuf_tensor("o_in", [P, 2, TPC, D], F32))
        oT = ctx.enter_context(nc.sbuf_tensor("oT", [P, 2, KD, CH], F32))
        tp = ctx.enter_context(nc.psum_tensor("po_tp", [P, KD, CH], F32))
        y = ctx.enter_context(nc.psum_tensor("po_y", [P, 2, TPC, D], F32))
        staged, turned, oT_ready, y_ready, added = sem("staged"), sem("turned"), sem("oT"), sem("y"), sem("added")

        with nc.Block() as block:
            @block.gpsimd
            def _(pool):
                with pool.Fori(0, NC // 2, 1) as i:
                    for u in range(2):
                        pool.wait_ge(turned, i * 2)
                        nc.gpsimd.tensor_copy(o_in[:, u, :, :], e.O[:, bass.ds(i * 2 * TPC + u * TPC, TPC), :]).then_inc(staged, 1)

            @block.tensor
            def _(pe):
                with pe.Fori(0, NC // 2, 1) as i:
                    for u in range(2):
                        pe.wait_ge(staged, i * 2 + u + 1)
                        pe.wait_ge(oT_ready, (i * 2 + u) * KD)
                        for k in range(KD):
                            for t in range(TPC):
                                last = nc.tensor.transpose(tp[:, k, t * P:(t + 1) * P], o_in[:, u, t, k * P:(k + 1) * P], e.ident[:, :])
                        last.then_inc(turned, 1)
                        pe.wait_ge(oT_ready, (i * 2 + u + 1) * KD)
                        pe.wait_ge(added, i * 2)
                        for t in range(TPC):
                            for k in range(KD):
                                nc.tensor.matmul(y[:, u, t, :], oT[:, u, k, t * P:(t + 1) * P], e.w_out0[:, k, :], start=(k == 0), stop=False)
                            last = nc.tensor.matmul(y[:, u, t, :], e.ones[0:1, :], e.b_out0[:, :], start=False, stop=True)
                        last.then_inc(y_ready, 1)

            @block.scalar
            def _(act):
                with act.Fori(0, NC // 2, 1) as i:
                    for u in range(2):
                        act.wait_ge(turned, i * 2 + u + 1)
                        for k in range(KD):
                            nc.scalar.activation(oT[:, u, k, :], tp[:, k, :], ACT.Copy).then_inc(oT_ready, 1)

            @block.vector
            def _(dve):
                with dve.Fori(0, NC // 2, 1) as i:
                    for u in range(2):
                        dve.wait_ge(y_ready, i * 2 + u + 1)
                        x = e.X[:, bass.ds(i * 2 * TPC + u * TPC, TPC), :]
                        nc.vector.tensor_tensor(x, y[:, u, :, :], x, ALU.add).then_inc(added, 1)


def feed_norm(nc, e, l, gate_w, gate_bias, outs):
    with ExitStack() as ctx:
        def sb(name, shape, dt=F32):
            return ctx.enter_context(nc.sbuf_tensor(f"fn{l}_{name}", shape, dt))

        def ps(name, shape):
            return ctx.enter_context(nc.psum_tensor(f"fn{l}_{name}", shape, F32))

        def sem(name):
            return new_sem(nc, e, f"fn{l}_{name}")

        G = outs
        xn = sb("xn", [P, 2, TPC, D])
        hTc = sb("hTc", [P, 2, KD, CH])
        row_h = sb("row_h", [P, 2, TPC, D]) if l == 0 else None
        gw = sb("gw", [P, KD, G])
        gb = sb("gb", [1, G])
        tp = ps("tp", [P, KD, CH])
        lg = ps("lg", [P, TPC, 128])
        turned_sel = ps("turned_sel", [P, CH])
        if l == 0:
            best = sb("best", [P, TPC, 8])
            left = sb("left", [P, TPC, E0])
            sel = sb("sel", [P, 2, TPC, E0])
            rank = sb("rank", [P, NT])
            rank_i = sb("rank_i", [P, NT], I32)
        ld, step, stats_ready, root_done = sem("ld"), sem("step"), sem("stats"), sem("root")
        xn_ready, turned, hT_ready, rows_ready, lg_ready, lg_taken = sem("xn"), sem("turned"), sem("hT"), sem("rows"), sem("lg"), sem("lg_taken")
        stored, sel_ready, sel_turned, order_ready, chain, scaled = sem("stored"), sem("sel"), sem("sel_turned"), sem("order"), sem("chain"), sem("scaled")
        rank_ready, copied = sem("rank"), sem("copied")
        cb, sb_ = (l * 6 + 4) * KD, (l * 6 + 3) * KD
        row_c, row_s = (e.row_cb0, e.row_sb0) if l == 0 else (e.row_cb1, e.row_sb1)
        NL = 1 if gate_bias is None else 2

        with nc.Block() as block:
            @block.sync
            def _(sp):
                sp.dma_start(gw[:, :, :], gate_w.rearrange("(k p) n -> p k n", p=P)).then_inc(ld, 16)
                if gate_bias is not None:
                    sp.dma_start(gb[:, :], gate_bias).then_inc(ld, 16)
                if l == 0:
                    table = e.table.rearrange("(c t p) w -> c p t w", t=TPC, p=P)
                    with sp.Fori(0, NC // 2, 1) as i:
                        for u in range(2):
                            sp.wait_ge(rows_ready, i * 2 + u + 1)
                            sp.dma_start(table[bass.ds(i * 2 + u, 1), :, :, 0:D].rearrange("o p t w -> (o p) t w"), row_h[:, u, :, :]).then_inc(stored, 16)
                    sp.wait_ge(stored, 16 * NC)

            @block.vector
            def _(dve):
                norm_stats(nc, e, dve, l, sem("norm_step"), stats_ready, root_done, lambda t: e.X[:, t, :])
                if l == 0:
                    dve.wait_ge(rank_ready, 1)
                    nc.vector.tensor_copy(rank[:, :], rank_i[:, :]).then_inc(step, 1)
                    dve.wait_ge(step, 1)
                STEPS = 2
                with dve.Fori(0, NC // 2, 1) as i:
                    for u in range(2):
                        dve.wait_ge(rows_ready, i * 2)
                        dve.wait_ge(turned, i * 2)
                        for t in range(TPC):
                            tile = i * 2 * TPC + u * TPC + t
                            nc.vector.tensor_scalar(xn[:, u, t, :], flat(e.X[:, bass.ds(tile, 1), :]), e.mv[:, bass.ds(tile, 1), 0],
                                                    e.rstd[:, bass.ds(tile, 1)], ALU.subtract, ALU.mult).then_inc(xn_ready, 1)
                        dve.wait_ge(lg_ready, i * 2 + u + 1)
                        logits = e.logits[:, bass.ds(i * 2 * TPC + u * TPC, TPC), :]
                        nc.vector.tensor_copy(logits, lg[:, :, 0:G]).then_inc(lg_taken, 1)
                        if l == 0:
                            for t in range(TPC):
                                nc.vector.max(best[:, t, :], lg[:, t, 0:E0]).then_inc(chain, 1)
                            c = i * 2 * 2 * TPC + u * 2 * TPC
                            dve.wait_ge(chain, c + TPC)
                            settle(dve)
                            for t in range(TPC):
                                nc.vector.match_replace(left[:, t, :], best[:, t, :], lg[:, t, 0:E0], MASKED).then_inc(chain, 1)
                            dve.wait_ge(chain, c + 2 * TPC)
                            nc.vector.tensor_tensor(e.chosen[:, bass.ds(i * 2 * TPC + u * TPC, TPC), :], lg[:, :, 0:E0], left[:, :, :], ALU.not_equal).then_inc(scaled, 1)
                            dve.wait_ge(scaled, i * 2 + u + 1)
                            dve.wait_ge(sel_turned, i * 2)
                            nc.vector.tensor_tensor(sel[:, u, :, :], e.chosen[:, bass.ds(i * 2 * TPC + u * TPC, TPC), :],
                                                    rank[:, bass.ds(i * 2 * TPC + u * TPC, TPC)].rearrange("p (t o) -> p t o", o=1).to_broadcast([P, TPC, E0]),
                                                    ALU.mult).then_inc(sel_ready, 1)

            @block.gpsimd
            def _(pool):
                if l == 0:
                    nc.gpsimd.iota(rank_i[:, :], [[-P, NT]], base=T, channel_multiplier=-1).then_inc(rank_ready, 1)
                with pool.Fori(0, NC // 2, 1) as i:
                    for u in range(2):
                        pool.wait_ge(xn_ready, i * 2 * TPC + (u + 1) * TPC)
                        if l == 0:
                            pool.wait_ge(stored, i * 32)
                            dst = row_h[:, u, :, :]
                        else:
                            dst = e.H[:, bass.ds(i * 2 * TPC + u * TPC, TPC), :]
                        wide = lambda row: row[:, :].rearrange("p (o d) -> p o d", o=1).to_broadcast([P, TPC, D])
                        nc.gpsimd.tensor_tensor(dst, xn[:, u, :, :], wide(row_c), ALU.mult).then_inc(copied, 1)
                        pool.wait_ge(copied, i * 2 + u + 1)
                        settle(pool)
                        nc.gpsimd.tensor_tensor(dst, dst, wide(row_s), ALU.add).then_inc(rows_ready, 1)

            @block.scalar
            def _(act):
                act.wait_ge(stats_ready, 1)
                nc.scalar.activation(e.root[:, :], e.var[:, :], ACT.Sqrt).then_inc(root_done, 1)
                with act.Fori(0, NC // 2, 1) as i:
                    for u in range(2):
                        act.wait_ge(turned, i * 2 + u + 1)
                        act.wait_ge(lg_ready, i * 2)
                        for k in range(KD):
                            nc.scalar.activation(hTc[:, u, k, :], tp[:, k, :], ACT.Identity,
                                                 bias=e.col[:, sb_ + k:sb_ + k + 1], scale=e.col[:, cb + k:cb + k + 1]).then_inc(hT_ready, 1)
                            nc.scalar.activation(e.hT[:, k, bass.ds(i * 2 * CH + u * CH, CH)], tp[:, k, :], ACT.Identity,
                                                 bias=e.col[:, sb_ + k:sb_ + k + 1], scale=e.col[:, cb + k:cb + k + 1]).then_inc(hT_ready, 1)
                        if l == 0:
                            act.wait_ge(sel_turned, i * 2 + u + 1)
                            nc.scalar.activation(e.order[E0 * u:E0 * (u + 1), bass.ds(i * CH, CH)], turned_sel[E0 * u:E0 * (u + 1), :], ACT.Copy).then_inc(order_ready, 1)

            @block.tensor
            def _(pe):
                pe.wait_ge(ld, 16 * NL)
                with pe.Fori(0, NC // 2, 1) as i:
                    for u in range(2):
                        pe.wait_ge(xn_ready, i * 2 * TPC + (u + 1) * TPC)
                        pe.wait_ge(hT_ready, (i * 2 + u) * 2 * KD)
                        for k in range(KD):
                            for t in range(TPC):
                                last = nc.tensor.transpose(tp[:, k, t * P:(t + 1) * P], xn[:, u, t, k * P:(k + 1) * P], e.ident[:, :])
                        last.then_inc(turned, 1)
                        pe.wait_ge(hT_ready, (i * 2 + u + 1) * 2 * KD)
                        pe.wait_ge(lg_taken, i * 2 + u)
                        if l == 0:
                            pe.wait_ge(scaled, i * 2 + u)
                        for t in range(TPC):
                            for k in range(KD):
                                last = nc.tensor.matmul(lg[:, t, 0:G], hTc[:, u, k, t * P:(t + 1) * P], gw[:, k, :],
                                                        start=(k == 0), stop=(k == KD - 1 and gate_bias is None))
                            if gate_bias is not None:
                                last = nc.tensor.matmul(lg[:, t, 0:G], e.ones[0:1, :], gb[:, :], start=False, stop=True)
                        last.then_inc(lg_ready, 1)
                        if l == 0:
                            pe.wait_ge(sel_ready, i * 2 + u + 1)
                            pe.wait_ge(order_ready, i * 2 + u)
                            for t in range(TPC):
                                last = nc.tensor.matmul(turned_sel[E0 * u:E0 * (u + 1), t * P:(t + 1) * P], sel[:, u, t, :], e.ident[:, :],
                                                        start=True, stop=True)
                            last.then_inc(sel_turned, 1)


def shared_expert(nc, e, a):
    with ExitStack() as ctx:
        def sb(name, shape, dt=F32):
            return ctx.enter_context(nc.sbuf_tensor(f"se_{name}", shape, dt))

        def ps(name, shape):
            return ctx.enter_context(nc.psum_tensor(f"se_{name}", shape, F32))

        def sem(name):
            return new_sem(nc, e, f"se_{name}")

        FT = IS // P
        wu = sb("wu", [P, KD, 2 * IS])
        wd = sb("wd", [P, FT, D])
        aT = sb("aT", [P, 2, FT, CH])
        silu = sb("silu", [P, 2, CH])
        weight = sb("weight", [P, NT, E0])
        small = sb("small", [P, 3, NT])
        sig = sb("sig", [P, NT])
        cand = sb("cand", [P, CAP])
        eight = sb("eight", [P, 2 * (CAP // 8 // NC), 8])
        both = sb("both", [E0, 2, CAP])
        first = sb("first", [E0, CAP])
        slot_f = sb("slot_f", [P, 2, E0])
        shared_y = sb("shared_y", [P, 2, TPC, D])
        up = ps("up", [P, 2, 2, CH])
        y = ps("y", [P, TPC, D])
        tk = ps("tk", [P, E0])
        ld, softmax_in, softmax_ex, chain, weight_ready, sig_ready, tanh_done = (sem(n) for n in ("ld", "sm_in", "sm_ex", "chain", "weight", "sig", "tanh"))
        up_ready, silu_ready, a_ready, y_ready, y_taken, x_ready, stored = (sem(n) for n in ("up", "silu", "a", "y", "y_taken", "x", "stored"))
        found, moved, tk_ready, table_stored = (sem(n) for n in ("found", "moved", "tk", "table"))
        rounds = CAP // 8 // NC

        with nc.Block() as block:
            @block.sync
            def _(sp):
                sp.dma_start(wu[:, :, :], a.L0_shared_up.rearrange("(k p) n -> p k n", p=P)).then_inc(ld, 16)
                sp.dma_start(wd[:, :, :], a.L0_shared_down.rearrange("(k p) n -> p k n", p=P)).then_inc(ld, 16)
                sp.wait_ge(weight_ready, 1)
                sp.dma_start(e.table.rearrange("(t p) w -> p t w", p=P)[:, :, D:ROW0], weight[:, :, :]).then_inc(table_stored, 16)
                xs = e.x_dram.rearrange("(c t p) d -> c p t d", t=TPC, p=P)
                with sp.Fori(0, NC, 1) as i:
                    sp.wait_ge(x_ready, i + 1)
                    sp.dma_start(xs[bass.ds(i, 1)].rearrange("o p t d -> (o p) t d"), e.X[:, bass.ds(i * TPC, TPC), :]).then_inc(stored, 16)
                sp.wait_ge(found, 3 * rounds * NC)
                sp.dma_start(both[:, 0, :], cand[0:E0, :]).then_inc(moved, 16)
                sp.dma_start(both[:, 1, :], cand[E0:P, :]).then_inc(moved, 16)
                sp.wait_ge(stored, 16 * NC)
                sp.wait_ge(table_stored, 16)

            @block.vector
            def _(dve):
                n = [0]

                def link(ins):
                    n[0] += 1
                    ins.then_inc(chain, 1)
                    dve.wait_ge(chain, n[0])

                experts = e.logits[:, :, 0:E0]
                wide = lambda s: small[:, s, :].rearrange("p (t o) -> p t o", o=1).to_broadcast([P, NT, E0])
                link(nc.vector.tensor_reduce(small[:, 0, :], experts, AX.X, ALU.max))
                nc.vector.tensor_tensor(weight[:, :, :], experts, wide(0), ALU.subtract).then_inc(softmax_in, 1)
                dve.wait_ge(softmax_ex, 1)
                link(nc.vector.tensor_tensor(weight[:, :, :], weight[:, :, :], e.chosen[:, :, :], ALU.mult))
                link(nc.vector.tensor_reduce(small[:, 1, :], weight[:, :, :], AX.X, ALU.add))
                link(nc.vector.reciprocal(small[:, 2, :], small[:, 1, :]))
                nc.vector.tensor_tensor(weight[:, :, :], weight[:, :, :], wide(2), ALU.mult).then_inc(weight_ready, 1)
                dve.wait_ge(tanh_done, 1)
                nc.vector.tensor_scalar(sig[:, :], sig[:, :], 0.5, 0.5, ALU.mult, ALU.add).then_inc(sig_ready, 1)
                dve.wait_ge(sig_ready, 1)

                with dve.Fori(0, NC // 2, 1) as i:
                    for u in range(2):
                        for f in range(FT):
                            m = u * FT + f
                            dve.wait_ge(silu_ready, i * 2 * FT + m + 1)
                            nc.vector.tensor_tensor(aT[:, u, f, :], silu[:, m % 2, :], up[:, m % 2, 1, :], ALU.mult).then_inc(a_ready, 1)
                            if f % 2 == 0:
                                r = u * rounds + f // 2
                                done = i * 6 * rounds + r * 3
                                dve.wait_ge(found, done)
                                settle(dve)
                                nc.vector.max(eight[:, r, :], e.order[:, :]).then_inc(found, 1)
                                dve.wait_ge(found, done + 1)
                                settle(dve)
                                nc.vector.match_replace(e.order[:, :], eight[:, r, :], e.order[:, :], 0.0).then_inc(found, 1)
                                nc.vector.tensor_copy(cand[:, bass.ds(i * 2 * rounds * 8 + r * 8, 8)], eight[:, r, :]).then_inc(found, 1)
                        dve.wait_ge(y_ready, i * 2 + u + 1)
                        for t in range(TPC):
                            tile = i * 2 * TPC + u * TPC + t
                            nc.vector.scalar_tensor_tensor(shared_y[:, u, t, :], y[:, t, :], sig[:, bass.ds(tile, 1)], e.row_gb0[:, :],
                                                           ALU.mult, ALU.mult).then_inc(y_taken, 1)
                        x = e.X[:, bass.ds(i * 2 * TPC + u * TPC, TPC), :]
                        dve.wait_ge(y_taken, i * 2 * TPC + (u + 1) * TPC)
                        nc.vector.tensor_tensor(x, x, shared_y[:, u, :, :], ALU.add).then_inc(x_ready, 1)
                dve.wait_ge(moved, 32)
                for r in range(CAP // 8):
                    link(nc.vector.max(first[:, r * 8:(r + 1) * 8], both[:, :, :]))
                    link(nc.vector.match_replace(both[:, :, :], first[:, r * 8:(r + 1) * 8], both[:, :, :], 0.0))
                dve.wait_ge(tk_ready, 1)
                link(nc.vector.tensor_scalar(slot_f[:, 0, :], tk[:, :], -1.0, float(T), ALU.mult, ALU.add))
                link(nc.vector.tensor_scalar(slot_f[:, 1, :], slot_f[:, 0, :], float(T - 1), None, ALU.min))
                link(nc.vector.tensor_copy(e.to_token[:, :], slot_f[:, 0, :]))
                link(nc.vector.tensor_copy(e.from_token[:, :], slot_f[:, 1, :]))

            @block.scalar
            def _(act):
                act.wait_ge(softmax_in, 1)
                nc.scalar.activation(weight[:, :, :], weight[:, :, :], ACT.Exp).then_inc(softmax_ex, 1)
                nc.scalar.activation(sig[:, :], e.logits[:, :, E0], ACT.Tanh, scale=0.5).then_inc(tanh_done, 1)
                with act.Fori(0, NC // 2, 1) as i:
                    for u in range(2):
                        for f in range(FT):
                            m = u * FT + f
                            act.wait_ge(up_ready, i * 2 * FT + m + 1)
                            act.wait_ge(a_ready, i * 2 * FT + max(m - 1, 0))
                            nc.scalar.activation(silu[:, m % 2, :], up[:, m % 2, 0, :], ACT.Silu).then_inc(silu_ready, 1)

            @block.tensor
            def _(pe):
                pe.wait_ge(ld, 32)
                with pe.Fori(0, NC // 2, 1) as i:
                    for u in range(2):
                        for f in range(FT):
                            m = u * FT + f
                            pe.wait_ge(a_ready, i * 2 * FT + max(m - 1, 0))
                            for s in range(2):
                                for k in range(KD):
                                    last = nc.tensor.matmul(up[:, m % 2, s, :], wu[:, k, s * IS + f * P:s * IS + (f + 1) * P],
                                                            e.hT[:, k, bass.ds(i * 2 * CH + u * CH, CH)], start=(k == 0), stop=(k == KD - 1))
                            last.then_inc(up_ready, 1)
                        pe.wait_ge(a_ready, i * 2 * FT + (u + 1) * FT)
                        pe.wait_ge(y_taken, i * 2 * TPC + u * TPC)
                        for t in range(TPC):
                            for f in range(FT):
                                last = nc.tensor.matmul(y[:, t, :], aT[:, u, f, t * P:(t + 1) * P], wd[:, f, :], start=(f == 0), stop=(f == FT - 1))
                        last.then_inc(y_ready, 1)
                pe.wait_ge(chain, 4 + 2 * (CAP // 8))
                nc.tensor.transpose(tk[:, :], first[:, :], e.ident[0:E0, 0:E0]).then_inc(tk_ready, 1)


def routed_experts(nc, e, a):
    R = 4
    BODIES = E0 // R
    with ExitStack() as ctx:
        def sb(name, shape, dt=F32):
            return ctx.enter_context(nc.sbuf_tensor(f"re_{name}", shape, dt))

        def ps(name, shape):
            return ctx.enter_context(nc.psum_tensor(f"re_{name}", shape, F32))

        def sem(name):
            return new_sem(nc, e, f"re_{name}")

        wu = sb("wu", [P, R, KD, 2 * I0])
        wd = sb("wd", [P, R, D])
        rows = sb("rows", [P, R, ROW0])
        read_at = sb("read_at", [P, R, 1], I32)
        add_at = sb("add_at", [P, R, 1], I32)
        w = sb("w", [P, R, 1])
        rT = sb("rT", [P, 2, KD, CAP])
        silu = sb("silu", [P, 2, I0])
        act_rows = sb("act_rows", [P, 2, I0])
        actT = sb("actT", [P, 2, CAP])
        add = sb("add", [P, R, D])
        tp = ps("tp", [P, 2, KD, CAP])
        up = ps("up", [P, 2, 2 * I0])
        ta = ps("ta", [P, 2, CAP])
        y = ps("y", [P, 2, D])
        w_loaded = [sem(f"w_loaded{r}") for r in range(R)]
        gathered = [e.kept.enter_context(nc.semaphore(f"gathered{r}")) for r in range(R)]
        scattered = e.kept.enter_context(nc.semaphore("scattered"))
        read_at_ready, add_at_ready, tp_ready, rT_ready, up_ready, silu_ready, act_ready, ta_ready, actT_ready, y_ready, add_ready, w_ready = (
            sem(n) for n in ("read_at", "add_at", "tp", "rT", "up", "silu", "act", "ta", "actT", "y", "add", "w"))

        with nc.Block() as block:
            @block.sync
            def _(sp):
                def load(i, r):
                    sp.dma_start(wu[:, r, :, :], a.L0_up[bass.ds(i * R + r, 1)].rearrange("o (k p) n -> p (o k) n", p=P)).then_inc(w_loaded[r], 16)
                    sp.dma_start(wd[:, r, :], a.L0_down[bass.ds(i * R + r, 1)].rearrange("o p n -> (o p) n")).then_inc(w_loaded[r], 16)

                for r in range(R):
                    load(0, r)
                with sp.Fori(0, BODIES - 1, 1) as i:
                    for r in range(R):
                        sp.wait_ge(y_ready, i * R + r + 1)
                        load(i + 1, r)

            @block.gpsimd
            def _(pool):
                def gather(i, r):
                    nc.gpsimd.tensor_copy(read_at[:, r, :], e.from_token[:, bass.ds(i * R + r, 1)]).then_inc(read_at_ready, 1)
                    pool.wait_ge(read_at_ready, i * R + r + 1)
                    settle(pool)
                    pool.indirect_dma_start(out=rows[:, r, :], out_offset=None, in_=e.table,
                                            in_offset=bass.IndirectOffsetOnAxis(ap=read_at[:, r, :], axis=0)).then_inc(gathered[r], 16)

                def scatter(i, r):
                    nc.gpsimd.tensor_copy(add_at[:, r, :], e.to_token[:, bass.ds(i * R + r, 1)]).then_inc(add_at_ready, 1)
                    pool.wait_ge(add_at_ready, i * R + r + 1)
                    pool.wait_ge(add_ready, i * R + r + 1)
                    pool.wait_ge(scattered, i * R * 16 + r * 16)
                    settle(pool)
                    pool.indirect_dma_start(out=e.x_dram, out_offset=bass.IndirectOffsetOnAxis(ap=add_at[:, r, :], axis=0),
                                            in_=add[:, r, :], in_offset=None, bounds_check=T - 1, oob_is_err=False,
                                            compute_op=ALU.add).then_inc(scattered, 16)

                for r in range(R):
                    gather(0, r)
                with pool.Fori(0, BODIES - 1, 1) as i:
                    for r in range(R):
                        pool.wait_ge(tp_ready, i * R + r + 1)
                        pool.wait_ge(w_ready, i * R + r + 1)
                        gather(i + 1, r)
                        scatter(i, r)
                for r in range(R):
                    scatter(BODIES - 1, r)
                pool.wait_ge(scattered, E0 * 16)

            @block.tensor
            def _(pe):
                def turn(i, r):
                    pe.wait_ge(gathered[r % R], (i + r // R) * 16 + 16)
                    if r >= 2:
                        pe.wait_ge(rT_ready, i * R + r - 1)
                    for k in range(KD):
                        last = nc.tensor.transpose(tp[:, r % 2, k, :], rows[:, r % R, k * P:(k + 1) * P], e.ident[:, :])
                    last.then_inc(tp_ready, 1)

                def products(i, peeled):
                    for r in range(R):
                        pe.wait_ge(rT_ready, i * R + r + 1)
                        pe.wait_ge(w_loaded[r], i * 32 + 32)
                        pe.wait_ge(act_ready, i * R + max(r - 1, 0))
                        for k in range(KD):
                            last = nc.tensor.matmul(up[:, r % 2, :], rT[:, r % 2, k, :], wu[:, r, k, :], start=(k == 0), stop=(k == KD - 1))
                        last.then_inc(up_ready, 1)
                        if r < R - 1 or not peeled:
                            turn(i, r + 1)
                        pe.wait_ge(act_ready, i * R + r + 1)
                        pe.wait_ge(actT_ready, i * R + max(r - 1, 0))
                        nc.tensor.transpose(ta[:, r % 2, :], act_rows[:, r % 2, :], e.ident[:, :]).then_inc(ta_ready, 1)
                        pe.wait_ge(actT_ready, i * R + r + 1)
                        pe.wait_ge(add_ready, i * R + max(r - 1, 0))
                        nc.tensor.matmul(y[:, r % 2, :], actT[:, r % 2, :], wd[:, r, :], start=True, stop=True).then_inc(y_ready, 1)

                turn(0, 0)
                with pe.Fori(0, BODIES - 1, 1) as i:
                    products(i, False)
                products(BODIES - 1, True)

            @block.scalar
            def _(act):
                def row_copy(i, r):
                    act.wait_ge(tp_ready, i * R + r + 1)
                    nc.scalar.activation(rT[:, r % 2, :, :], tp[:, r % 2, :, :], ACT.Copy).then_inc(rT_ready, 1)

                def expert(i, peeled):
                    for r in range(R):
                        act.wait_ge(up_ready, i * R + r + 1)
                        nc.scalar.activation(silu[:, r % 2, :], up[:, r % 2, 0:I0], ACT.Silu).then_inc(silu_ready, 1)
                        if r < R - 1 or not peeled:
                            row_copy(i, r + 1)
                        act.wait_ge(ta_ready, i * R + r + 1)
                        nc.scalar.activation(actT[:, r % 2, :], ta[:, r % 2, :], ACT.Copy).then_inc(actT_ready, 1)

                row_copy(0, 0)
                with act.Fori(0, BODIES - 1, 1) as i:
                    expert(i, False)
                expert(BODIES - 1, True)

            @block.vector
            def _(dve):
                def take_weight(i, r):
                    dve.wait_ge(gathered[r], i * 16 + 16)
                    nc.vector.tensor_copy(w[:, r, :], rows[:, r, bass.ds(i * R + (D + r), 1)]).then_inc(w_ready, 1)

                def experts(i, first):
                    for r in range(R):
                        take_weight(i, r)
                        dve.wait_ge(silu_ready, i * R + r + 1)
                        nc.vector.tensor_tensor(act_rows[:, r % 2, :], silu[:, r % 2, :], up[:, r % 2, I0:2 * I0], ALU.mult).then_inc(act_ready, 1)
                        dve.wait_ge(w_ready, i * R + r + 1)
                        dve.wait_ge(y_ready, i * R + r + 1)
                        if not first:
                            dve.wait_ge(scattered, i * R * 16 + (r + 1 - R) * 16)
                        nc.vector.scalar_tensor_tensor(add[:, r, :], y[:, r % 2, :], w[:, r, :], e.row_gb0[:, :], ALU.mult, ALU.mult).then_inc(add_ready, 1)

                experts(0, True)
                with dve.Fori(1, BODIES, 1) as i:
                    experts(i, False)


def reload_x(nc, e, by_sixteen):
    with nc.semaphore("reloaded%d" % by_sixteen) as reloaded, nc.Block() as block:
        @block.sync
        def _(sp):
            if by_sixteen:
                xv = e.x_dram.rearrange("(g p c) d -> p g c d", p=P, c=HS)
                for g in range(NT // HS):
                    sp.dma_start(e.X[:, g * HS:(g + 1) * HS, :], xv[:, g]).then_inc(reloaded, 16)
                sp.wait_ge(reloaded, 16 * (NT // HS))
            else:
                xv = e.x_dram.rearrange("(c t p) d -> c p t d", t=TPC, p=P)
                for c in range(NC):
                    sp.dma_start(e.X[:, c * TPC:(c + 1) * TPC, :], xv[c]).then_inc(reloaded, 16)
                sp.wait_ge(reloaded, 16 * NC)


def mixed_residual(nc, e):
    with ExitStack() as ctx:
        part = ctx.enter_context(nc.sbuf_tensor("mixed", [P, 2, HS, D], F32))
        scaled = [new_sem(nc, e, f"mix_scaled{g}") for g in range(2)]
        with nc.Block() as block:
            def work(eng, ops, g):
                o = e.O[:, :, :].rearrange("p (j g) (n c) -> p g c n j", g=2, n=H)[:, g]
                for c in range(HS):
                    row = e.row_ga1[:, :].rearrange("p (n j) -> p n j", n=H)
                    ops.tensor_tensor(part[:, g, c, :].rearrange("p (n j) -> p n j", n=H), o[:, c], row, ALU.mult).then_inc(scaled[g], 1)
                eng.wait_ge(scaled[g], HS)
                x = e.X[:, g * HS:(g + 1) * HS, :]
                ops.tensor_tensor(x, x, part[:, g], ALU.add).then_inc(scaled[g], 1)
                eng.wait_ge(scaled[g], HS + 1)

            @block.vector
            def _(dve):
                work(dve, nc.vector, 0)

            @block.gpsimd
            def _(pool):
                work(pool, nc.gpsimd, 1)


def feed_experts(nc, e, a):
    with ExitStack() as ctx:
        def sb(name, shape, dt=F32):
            return ctx.enter_context(nc.sbuf_tensor(f"fe_{name}", shape, dt))

        def ps(name, shape):
            return ctx.enter_context(nc.psum_tensor(f"fe_{name}", shape, F32))

        def sem(name):
            return new_sem(nc, e, f"fe_{name}")

        FT = F1 // P
        w1 = sb("w1", [P, 2, KD, F1])
        w2 = sb("w2", [P, 2, FT, D])
        aT = sb("aT", [P, 2, FT, CH])
        best = sb("best", [P, NT, 8])
        where = sb("where", [P, NT, 8], U32)
        where_f = sb("where_f", [P, NT, 2])
        gap = sb("gap", [P, NT])
        share = sb("share", [P, NT, 2])
        ids_i = sb("ids_i", [P, ET], I32)
        ids = sb("ids", [P, ET])
        weight = sb("weight", [P, NT, ET])
        second = sb("second", [P, NT, ET])
        zero = sb("zero", [P, NT])
        hid = ps("hid", [P, FT, CH])
        y = ps("y", [P, 2, TPC, D])
        loaded = [sem("loaded0"), sem("loaded1")]
        ids_made, chain, gap_ready, share_ready, weights_ready = sem("ids"), sem("chain"), sem("gap"), sem("share"), sem("weights")
        hid_ready, a_ready, y_ready, y_taken, done, stored = sem("hid"), sem("a"), sem("y"), sem("y_taken"), sem("done"), sem("stored")
        out_v = a.out.rearrange("(g p c) d -> p g c d", p=P, c=HS)

        with nc.Block() as block:
            @block.sync
            def _(sp):
                def load(p, ex):
                    sp.dma_start(w1[:, p, :, :], a.L1_w1[bass.ds(ex, 1)].rearrange("o (k p) f -> p (o k) f", p=P)).then_inc(loaded[p], 16)
                    sp.dma_start(w2[:, p, :, :], a.L1_w2[bass.ds(ex, 1)].rearrange("o (k p) d -> p (o k) d", p=P)).then_inc(loaded[p], 16)

                load(0, 0)
                load(1, 1)
                with sp.Fori(0, E1 // 2 - 1, 1) as i:
                    for p in range(2):
                        sp.wait_ge(y_ready, i * 2 * NC + (p + 1) * NC)
                        load(p, i * 2 + 2 + p)
                for t in range(NT // TPC):
                    g, c = (t * TPC) // HS, (t * TPC) % HS
                    sp.wait_ge(done, 2 * (t + 1))
                    sp.dma_start(out_v[:, g, c:c + TPC, :], e.H[:, t * TPC:(t + 1) * TPC, :]).then_inc(stored, 16)
                sp.wait_ge(stored, 16 * (NT // TPC))

            @block.gpsimd
            def _(pool):
                nc.gpsimd.iota(ids_i[:, :], [[1, ET]], base=0, channel_multiplier=0).then_inc(ids_made, 1)

            @block.vector
            def _(dve):
                n = [0]

                def link(ins):
                    n[0] += 1
                    ins.then_inc(chain, 1)
                    dve.wait_ge(chain, n[0])

                dve.wait_ge(ids_made, 1)
                link(nc.vector.tensor_copy(ids[:, :], ids_i[:, :]))
                for t in range(NT):
                    nc.vector.max(best[:, t, :], e.logits[:, t, :]).then_inc(chain, 1)
                n[0] += NT
                dve.wait_ge(chain, n[0])
                for t in range(NT):
                    nc.vector.max_index(where[:, t, :], best[:, t, :], e.logits[:, t, :]).then_inc(chain, 1)
                n[0] += NT
                dve.wait_ge(chain, n[0])
                nc.vector.tensor_tensor(gap[:, :], best[:, :, 0], best[:, :, 1], ALU.subtract).then_inc(gap_ready, 1)
                link(nc.vector.tensor_copy(where_f[:, :, :], where[:, :, 0:2]))
                dve.wait_ge(share_ready, 2)
                link(nc.vector.tensor_scalar(share[:, :, :], share[:, :, :], 0.5, 0.5, ALU.mult, ALU.add))
                idw = ids[:, :].rearrange("p (o n) -> p o n", o=1).to_broadcast([P, NT, ET])
                wide = lambda ap: ap.to_broadcast([P, NT, ET])
                link(nc.vector.tensor_tensor(weight[:, :, :], idw, wide(where_f[:, :, 0:1]), ALU.is_equal))
                link(nc.vector.tensor_tensor(weight[:, :, :], weight[:, :, :], wide(share[:, :, 0:1]), ALU.mult))
                link(nc.vector.tensor_tensor(second[:, :, :], idw, wide(where_f[:, :, 1:2]), ALU.is_equal))
                link(nc.vector.tensor_tensor(second[:, :, :], second[:, :, :], wide(share[:, :, 1:2]), ALU.mult))
                link(nc.vector.tensor_tensor(weight[:, :, :], weight[:, :, :], second[:, :, :], ALU.add))
                link(nc.vector.tensor_reduce(zero[:, :], weight[:, :, E1:ET], AX.X, ALU.add))
                for t in range(NT):
                    nc.vector.tensor_scalar(e.H[:, t, :], e.H[:, t, :], zero[:, t:t + 1], None, ALU.mult).then_inc(chain, 1)
                n[0] += NT
                dve.wait_ge(chain, n[0])

                with dve.Fori(0, E1 // 2, 1) as i:
                    for p in range(2):
                        for c in range(NC):
                            m = p * NC + c
                            dve.wait_ge(y_ready, i * 2 * NC + m + 1)
                            dve.wait_ge(y_taken, i * 2 * NC * TPC + max(m - NC + 1, 0) * TPC)
                            for t in range(TPC):
                                acc = e.H[:, c * TPC + t, :]
                                nc.vector.scalar_tensor_tensor(acc, y[:, c % 2, t, :], weight[:, c * TPC + t, bass.ds(i * 2 + p, 1)], acc,
                                                               ALU.mult, ALU.add).then_inc(y_taken, 1)
                dve.wait_ge(y_taken, E1 * NC * TPC)
                for c in range(NC):
                    acc = e.H[:, c * TPC:(c + 1) * TPC, :]
                    gbw = e.row_gb1[:, :].rearrange("p (o d) -> p o d", o=1).to_broadcast([P, TPC, D])
                    nc.vector.tensor_tensor(acc, acc, gbw, ALU.mult).then_inc(done, 1)
                    dve.wait_ge(done, 2 * c + 1)
                    nc.vector.tensor_tensor(acc, acc, e.X[:, c * TPC:(c + 1) * TPC, :], ALU.add).then_inc(done, 1)

            @block.scalar
            def _(act):
                act.wait_ge(gap_ready, 1)
                nc.scalar.activation(share[:, :, 0], gap[:, :], ACT.Tanh, scale=0.5).then_inc(share_ready, 1)
                nc.scalar.activation(share[:, :, 1], gap[:, :], ACT.Tanh, scale=-0.5).then_inc(share_ready, 1)
                with act.Fori(0, E1 // 2, 1) as i:
                    for p in range(2):
                        for c in range(NC):
                            m = p * NC + c
                            act.wait_ge(y_ready, i * 2 * NC + max(m - 1, 0))
                            for f in range(FT):
                                act.wait_ge(hid_ready, (i * 2 * NC + m) * FT + f + 1)
                                nc.scalar.activation(aT[:, c % 2, f, :], hid[:, f, :], ACT.Silu).then_inc(a_ready, 1)

            @block.tensor
            def _(pe):
                def hidden(i, p, c):
                    m = p * NC + c
                    for f in range(FT):
                        pe.wait_ge(a_ready, (i * 2 * NC + m - 1) * FT + f + 1 if m else i * 2 * NC * FT)
                        for k in range(KD):
                            last = nc.tensor.matmul(hid[:, f, :], w1[:, p, k, f * P:(f + 1) * P], e.hT[:, k, c * CH:(c + 1) * CH],
                                                    start=(k == 0), stop=(k == KD - 1))
                        last.then_inc(hid_ready, 1)

                def down(i, p, c):
                    m = p * NC + c
                    pe.wait_ge(a_ready, (i * 2 * NC + m + 1) * FT)
                    pe.wait_ge(y_taken, (i * 2 * NC + max(m - 1, 0)) * TPC)
                    for t in range(TPC):
                        for f in range(FT):
                            last = nc.tensor.matmul(y[:, c % 2, t, :], aT[:, c % 2, f, t * P:(t + 1) * P], w2[:, p, f, :],
                                                    start=(f == 0), stop=(f == FT - 1))
                    last.then_inc(y_ready, 1)

                with pe.Fori(0, E1 // 2, 1) as i:
                    for p in range(2):
                        pe.wait_ge(loaded[p], i * 32 + 32)
                        for c in range(NC):
                            hidden(i, p, c)
                            if c:
                                down(i, p, c - 1)
                        down(i, p, NC - 1)


def program(nc, a, stop=99):
    e = Env()
    with ExitStack() as ctx:
        e.layer = ctx.enter_context(ExitStack())
        e.sems = []
        e.kept = ctx

        def sb(name, shape, dt=F32):
            return ctx.enter_context(nc.sbuf_tensor(name, shape, dt))

        def dram(name, shape, dt=F32):
            return nc.dram_tensor(name, shape, dt, kind="Internal").ap()

        e.X = sb("X", [P, NT, D])
        e.ident, e.ident_b = sb("ident", [P, P]), sb("ident_b", [P, P], BF16)
        e.ones, e.sum4 = sb("ones", [P, P]), sb("sum4", [P, VC])
        e.mask_k, e.mask_q = sb("mask_k", [P, P], BF16), sb("mask_q", [P, CH + P], BF16)
        e.col, e.bias_qk = sb("col", [P, 24]), sb("bias_qk", [P, 4])
        e.row_ga0, e.row_gb0, e.row_sb0, e.row_cb0 = (sb(f"row_{n}", [P, D]) for n in ("ga0", "gb0", "sb0", "cb0"))
        e.row_ga1, e.row_gb1, e.row_sb1, e.row_cb1 = (sb(f"row_{n}", [P, D]) for n in ("ga1", "gb1", "sb1", "cb1"))
        e.w_out0, e.b_out0 = sb("w_out0", [P, KD, D]), sb("b_out0", [1, D])
        e.bn6, e.mv = sb("bn6", [P, NT, 6]), sb("mv", [P, NT, 2])
        e.var, e.root, e.rstd, e.newt = (sb(n, [P, NT]) for n in ("var", "root", "rstd", "newt"))
        e.q_dram, e.k_dram = dram("q_parts", (PARTS, D, T), BF16), dram("k_parts", (PARTS, D, T), BF16)
        e.table, e.x_dram = dram("table", (T, ROW0)), dram("x_after", (T, D))
        e.q_heads = e.q_dram.rearrange("s (h r) t -> s h r t", r=HS)
        e.k_heads = e.k_dram.rearrange("s (h r) t -> s h r t", r=HS)

        setup(nc, e, a)
        with ExitStack() as att:
            e.V = att.enter_context(nc.sbuf_tensor("V", [P, H, NT, HS], F32))
            e.O = att.enter_context(nc.sbuf_tensor("O", [P, NT, D], F32))
            project(nc, e, 0, a.L0_w_qkv, a.L0_b_qkv[2:3, :])
            if stop > 1:
                attention(nc, e, 0)
            if stop <= 2:
                dump(nc, e, a, e.O if stop == 2 else None)
                return
            project_out(nc, e)
        if stop == 3:
            return dump(nc, e, a, e.X)
        with ExitStack() as ffn:
            e.hT = ffn.enter_context(nc.sbuf_tensor("hT_0", [P, KD, T], F32))
            e.logits = ffn.enter_context(nc.sbuf_tensor("logits_0", [P, NT, E0 + 1], F32))
            e.chosen = ffn.enter_context(nc.sbuf_tensor("chosen", [P, NT, E0], F32))
            e.order = ffn.enter_context(nc.sbuf_tensor("order", [P, T // 2], F32))
            e.from_token = ffn.enter_context(nc.sbuf_tensor("from_token", [P, E0], I32))
            e.to_token = ffn.enter_context(nc.sbuf_tensor("to_token", [P, E0], I32))
            feed_norm(nc, e, 0, a.L0_gate_w, None, E0 + 1)
            shared_expert(nc, e, a)
            if stop == 4:
                return dump(nc, e, a, e.X)
            routed_experts(nc, e, a)
        recycle_semaphores(nc, e)
        reload_x(nc, e, False)
        if stop == 5:
            return dump(nc, e, a, e.X)
        with ExitStack() as att:
            e.V = att.enter_context(nc.sbuf_tensor("V1", [P, H, NT, HS], F32))
            e.O = att.enter_context(nc.sbuf_tensor("O1", [P, NT, D], F32))
            project(nc, e, 1, a.L1_w_qkv, None)
            attention(nc, e, 1)
            reload_x(nc, e, True)
            mixed_residual(nc, e)
        if stop == 6:
            return dump(nc, e, a, e.X, True)
        with ExitStack() as ffn:
            e.hT = ffn.enter_context(nc.sbuf_tensor("hT_1", [P, KD, T], F32))
            e.H = ffn.enter_context(nc.sbuf_tensor("H_1", [P, NT, D], F32))
            e.logits = ffn.enter_context(nc.sbuf_tensor("logits_1", [P, NT, ET], F32))
            feed_norm(nc, e, 1, a.L1_gate_w, a.L1_bias, ET)
            feed_experts(nc, e, a)


def dump(nc, e, a, src, by_sixteen=False):
    with nc.semaphore("dumped") as dumped, nc.Block() as block:
        @block.sync
        def _(sp):
            if src is None:
                sp.dma_start(a.out.rearrange("(t p) (h c) -> p h t c", p=P, h=H)[:, 0], e.V[:, 0]).then_inc(dumped, 16)
            elif by_sixteen:
                for g in range(2):
                    sp.dma_start(a.out.rearrange("(g p c) d -> p g c d", p=P, c=HS)[:, g], src[:, g * HS:(g + 1) * HS, :]).then_inc(dumped, 16)
                sp.wait_ge(dumped, 32)
            else:
                sp.dma_start(a.out.rearrange("(t p) d -> p t d", p=P), src[:, :, :]).then_inc(dumped, 16)
            sp.wait_ge(dumped, 16)


def lay_out(x):
    def qkv_heads(w):
        return np.ascontiguousarray(w.reshape(-1, H, 3, HS).transpose(0, 2, 1, 3).reshape(-1, 3, D))

    return {
        "x": np.ascontiguousarray(x["L0_attn_encodings"][0]),
        "L0_w_qkv": qkv_heads(x["L0_attn_attn_W"]),
        "L0_b_qkv": qkv_heads(x["L0_attn_attn_b"].reshape(1, -1))[0],
        "L0_out_W": x["L0_attn_out_W"], "L0_out_b": x["L0_attn_out_b"].reshape(1, D),
        "L0_gate_w": np.concatenate([x["L0_ffn_gate_w"], x["L0_ffn_shared_gate_w"]], axis=1),
        "L0_shared_up": x["L0_ffn_shared_gate_up_w"], "L0_shared_down": x["L0_ffn_shared_down_w"],
        "L0_up": x["L0_ffn_expert_gate_up_w"], "L0_down": x["L0_ffn_expert_down_w"],
        "L0_c": x["L0_c"], "L0_wmod": x["L0_wmod"],
        "L1_w_qkv": qkv_heads(np.ascontiguousarray(x["L1_attn_W_qkv"].transpose(1, 0, 2)).reshape(D, -1)),
        "L1_W_out": x["L1_attn_W_out"].reshape(D, D),
        "L1_gate_w": np.ascontiguousarray(x["L1_ffn_gate_w"].T), "L1_bias": x["L1_ffn_expert_bias"].reshape(1, ET),
        "L1_w1": np.ascontiguousarray(x["L1_ffn_w1"].transpose(0, 2, 1)),
        "L1_w2": np.ascontiguousarray(x["L1_ffn_w2"].transpose(0, 2, 1)),
        "L1_c": x["L1_c"], "L1_wmod": x["L1_wmod"],
    }


class Arguments:
    pass


def kernel(**inputs):
    import numpy as _np
    import concourse.bacc as _bacc
    from concourse import mybir as _mybir
    from concourse.bass_utils import run_bass_kernel_spmd as _run

    nc = _bacc.Bacc("TRN2", target_bir_lowering=False, num_devices=1)
    arrays = {f"in_{k}": _np.ascontiguousarray(v) for k, v in lay_out({k: _np.asarray(v) for k, v in inputs.items()}).items()}
    a = Arguments()
    a.__dict__.update({k[3:]: nc.dram_tensor(k, v.shape, _mybir.dt.from_np(v.dtype), kind="ExternalInput").ap()
                       for k, v in arrays.items()})
    a.out = nc.dram_tensor("out_0", (T, D), F32, kind="ExternalOutput").ap()
    program(nc, a)
    r = _run(nc, [arrays], core_ids=[0])
    return r.results[0]["out_0"].reshape(1, T, D)
```

```python
import concourse.bass as bass
import numpy as np
from concourse import mybir
from contextlib import ExitStack

F32 = mybir.dt.float32
BF16 = mybir.dt.bfloat16
I32 = mybir.dt.int32
U32 = mybir.dt.uint32
ALU = mybir.AluOpType
ACT = mybir.ActivationFunctionType
AX = mybir.AxisListType

P = 128
T = 4096
D = 256
KD = D // P
NT = T // P
CH = 512
NC = T // CH
TPC = CH // P
H = 16
HS = D // H
EPS = 1e-5
MASKED = -1e30
PARTS = 3
PAIRS = [(0, 0), (1, 0), (2, 0), (0, 1), (1, 1), (0, 2)]
SR = len(PAIRS) * HS
MR = SR + PARTS
VC = 32
QUADS = NC * (NC + 1) // 2
LOOK = 12
SLOTS = 2 * QUADS
RING = 3
E0, I0, CAP, TOPK = 64, 128, 128, 8
IS = 512
ROW0 = D + E0
E1, EZ, F1 = 8, 4, 512
ET = E1 + EZ


class Env:
    pass


def new_sem(nc, e, name):
    e.sems.append(e.layer.enter_context(nc.semaphore(name)))
    return e.sems[-1]


def recycle_semaphores(nc, e):
    with nc.Block() as block:
        @block.sync
        def _(sp):
            for s in e.sems:
                sp.sem_clear(s)
    e.layer.close()
    e.sems = []


def settle(eng):
    eng.nop(nofuse=True)


def flat(ap):
    return ap.rearrange("p o d -> p (o d)")


def setup(nc, e, a):
    with ExitStack() as ctx:
        def sb(name, shape, dt=F32):
            return ctx.enter_context(nc.sbuf_tensor(name, shape, dt))

        def sem(name):
            return new_sem(nc, e, name)

        wmod = sb("wmod", [P, 2, KD, 6 * D])
        c_col = sb("c_col", [P, 2, KD])
        c_silu = sb("c_silu", [P, 2, KD])
        c_rep = sb("c_rep", [P, 2, KD, P])
        w_out1 = sb("w_out1", [P, KD, D])
        w_out0_raw = sb("w_out0_raw", [P, KD, D])
        b_out0_raw = sb("b_out0_raw", [1, D])
        guard = sb("guard", [P, 2, D])
        rows = ctx.enter_context(nc.psum_tensor("rows", [P, 10, D], F32))
        cols = ctx.enter_context(nc.psum_tensor("cols", [P, 32], F32))
        small_loaded, wmod_loaded, x_loaded = sem("small_loaded"), sem("wmod_loaded"), sem("x_loaded")
        pool_step, const_made = sem("pool_step"), sem("const_made")
        silu_done, rep_done, mod_done = sem("silu_done"), sem("rep_done"), sem("mod_done")
        step = sem("setup_step")
        NS = 11

        with nc.Block() as block:
            @block.sync
            def _(sp):
                for l, c in enumerate((a.L0_c, a.L1_c)):
                    for k in range(KD):
                        sp.dma_start(c_col[:, l, k:k + 1], c[0:1, k * P:(k + 1) * P].rearrange("o p -> p o")).then_inc(small_loaded, 16)
                sp.dma_start(b_out0_raw[:, :], a.L0_out_b).then_inc(small_loaded, 16)
                sp.dma_start(w_out0_raw[:, :, :], a.L0_out_W.rearrange("(k p) n -> p k n", p=P)).then_inc(small_loaded, 16)
                sp.dma_start(w_out1[:, :, :], a.L1_W_out.rearrange("(k p) n -> p k n", p=P)).then_inc(small_loaded, 16)
                for s in range(2):
                    for g in range(KD):
                        sp.dma_start(e.bias_qk[:, 2 * s + g:2 * s + g + 1],
                                     a.L0_b_qkv[s:s + 1, g * P:(g + 1) * P].rearrange("o p -> p o")).then_inc(small_loaded, 16)
                for l, w in enumerate((a.L0_wmod, a.L1_wmod)):
                    sp.dma_start(wmod[:, l, :, :], w.rearrange("(k p) n -> p k n", p=P)).then_inc(wmod_loaded, 16)
                xv = a.x.rearrange("(c t p) d -> c p t d", t=TPC, p=P)
                for c in range(NC):
                    sp.dma_start(e.X[:, c * TPC:(c + 1) * TPC, :], xv[c]).then_inc(x_loaded, 16)
                sp.wait_ge(x_loaded, 16 * NC)

            @block.gpsimd
            def _(pool):
                nc.gpsimd.memset(e.ident[:, :], 0.0).then_inc(pool_step, 1)
                nc.gpsimd.memset(e.mask_k[:, :], 0.0).then_inc(pool_step, 1)
                nc.gpsimd.memset(e.mask_q[:, 0:CH], MASKED).then_inc(pool_step, 1)
                nc.gpsimd.memset(e.mask_q[:, CH:CH + P], 0.0).then_inc(pool_step, 1)
                nc.gpsimd.memset(e.ones[:, :], 1.0).then_inc(pool_step, 1)
                nc.gpsimd.memset(e.sum4[:, :], 0.0).then_inc(pool_step, 1)
                pool.wait_ge(pool_step, 6)
                nc.gpsimd.affine_select(out=e.ident[:, :], in_=e.ident[:, :], compare_op=ALU.not_equal, fill=1.0,
                                        base=0, pattern=[[-1, P]], channel_multiplier=1).then_inc(const_made, 1)
                nc.gpsimd.affine_select(out=e.mask_k[:, :], in_=e.mask_k[:, :], compare_op=ALU.is_ge, fill=MASKED,
                                        base=0, pattern=[[-1, P]], channel_multiplier=1).then_inc(const_made, 1)
                nc.gpsimd.affine_select(out=e.mask_q[:, CH:CH + P], in_=e.mask_q[:, CH:CH + P], compare_op=ALU.is_ge,
                                        fill=MASKED, base=0, pattern=[[1, P]], channel_multiplier=-1).then_inc(const_made, 1)
                for g in range(4):
                    pool.wait_ge(pool_step, 6 + g)
                    nc.gpsimd.affine_select(out=e.sum4[:, :], in_=e.sum4[:, :], compare_op=ALU.not_equal, fill=1.0,
                                            base=-VC * g, pattern=[[-1, VC]], channel_multiplier=1).then_inc(pool_step, 1)
                pool.wait_ge(const_made, 3)
                pool.wait_ge(pool_step, 10)
                nc.gpsimd.tensor_copy(e.ident_b[:, :], e.ident[:, :]).then_inc(const_made, 1)

            @block.scalar
            def _(act):
                act.wait_ge(small_loaded, 16 * NS)
                nc.scalar.activation(c_silu[:, :, :], c_col[:, :, :], ACT.Silu).then_inc(silu_done, 1)

            @block.vector
            def _(dve):
                n = [0]

                def link(ins):
                    n[0] += 1
                    ins.then_inc(step, 1)
                    dve.wait_ge(step, n[0])

                dve.wait_ge(silu_done, 1)
                dve.wait_ge(pool_step, 5)
                for l in range(2):
                    for k in range(KD):
                        nc.vector.tensor_scalar(c_rep[:, l, k, :], e.ones[:, :], c_silu[:, l, k:k + 1], None, ALU.mult).then_inc(rep_done, 1)
                dve.wait_ge(mod_done, 1)
                nc.vector.tensor_scalar(e.bias_qk[:, 0:KD], e.bias_qk[:, 0:KD], HS ** -0.5, None, ALU.mult)
                link(nc.vector.tensor_copy(e.col[:, :], cols[:, 0:24]))
                for l in range(2):
                    for w in (1, 4):
                        j = (l * 6 + w) * KD
                        link(nc.vector.tensor_scalar(e.col[:, j:j + KD], e.col[:, j:j + KD], 1.0, None, ALU.add))
                nc.vector.tensor_copy(e.row_sb0[:, :], rows[:, 2, :])
                nc.vector.tensor_scalar(e.row_cb0[:, :], rows[:, 3, :], 1.0, None, ALU.add)
                nc.vector.tensor_copy(e.row_sb1[:, :], rows[:, 6, :])
                nc.vector.tensor_scalar(e.row_cb1[:, :], rows[:, 7, :], 1.0, None, ALU.add)
                for src, dst in ((0, e.row_ga0), (1, e.row_gb0), (4, e.row_ga1), (5, e.row_gb1)):
                    link(nc.vector.tensor_scalar(guard[:, 1, :], rows[:, src, :], 0.0, 2.0, ALU.is_ge, ALU.mult))
                    link(nc.vector.tensor_scalar(guard[:, 1, :], guard[:, 1, :], 1.0, None, ALU.subtract))
                    link(nc.vector.tensor_tensor(guard[:, 0, :], guard[:, 1, :], rows[:, src, :], ALU.mult))
                    link(nc.vector.tensor_scalar(guard[:, 0, :], guard[:, 0, :], 0.25, None, ALU.max))
                    link(nc.vector.tensor_tensor(dst[:, :], guard[:, 0, :], guard[:, 1, :], ALU.mult))
                link(nc.vector.tensor_tensor(e.row_ga1[:, :], e.row_ga1[:, :], rows[:, 8, :], ALU.mult))
                for k in range(KD):
                    nc.vector.tensor_tensor(e.w_out0[:, k, :], w_out0_raw[:, k, :], e.row_ga0[:, :], ALU.mult)
                link(nc.vector.tensor_tensor(e.b_out0[:, :], b_out0_raw[:, :], e.row_ga0[0:1, :], ALU.mult))

            @block.tensor
            def _(pe):
                pe.wait_ge(wmod_loaded, 32)
                pe.wait_ge(silu_done, 1)
                for l in range(2):
                    for w in range(6):
                        for g in range(KD):
                            j = (l * 6 + w) * KD + g
                            for k in range(KD):
                                nc.tensor.matmul(cols[:, j:j + 1], wmod[:, l, k, w * D + g * P:w * D + (g + 1) * P],
                                                 c_silu[:, l, k:k + 1], start=(k == 0), stop=(k == KD - 1))
                pe.wait_ge(rep_done, 2 * KD)
                for j, (l, w) in enumerate(((0, 2), (0, 5), (0, 3), (0, 4), (1, 2), (1, 5), (1, 3), (1, 4))):
                    for k in range(KD):
                        nc.tensor.matmul(rows[:, j, :], c_rep[:, l, k, :], wmod[:, l, k, w * D:(w + 1) * D],
                                         start=(k == 0), stop=(k == KD - 1))
                for k in range(KD):
                    last = nc.tensor.matmul(rows[:, 8, :], e.ones[:, :], w_out1[:, k, :], start=(k == 0), stop=(k == KD - 1))
                last.then_inc(mod_done, 1)


def norm_stats(nc, e, dve, tag, step, stats_ready, root_done, src):
    n = 0
    for t in range(NT):
        nc.vector.bn_stats(e.bn6[:, t, :], src(t)).then_inc(step, 1)
    n += NT
    dve.wait_ge(step, n)
    for t in range(NT):
        nc.vector.bn_aggr(e.mv[:, t, :], e.bn6[:, t, :]).then_inc(step, 1)
    n += NT
    dve.wait_ge(step, n)
    nc.vector.tensor_scalar(e.var[:, :], e.mv[:, :, 1], EPS, None, ALU.add).then_inc(stats_ready, 1)
    dve.wait_ge(root_done, 1)
    nc.vector.reciprocal(e.rstd[:, :], e.root[:, :]).then_inc(step, 1)
    dve.wait_ge(step, n + 1)
    nc.vector.tensor_tensor(e.newt[:, :], e.rstd[:, :], e.rstd[:, :], ALU.mult).then_inc(step, 1)
    dve.wait_ge(step, n + 2)
    nc.vector.tensor_tensor(e.newt[:, :], e.newt[:, :], e.var[:, :], ALU.mult).then_inc(step, 1)
    dve.wait_ge(step, n + 3)
    nc.vector.tensor_scalar(e.newt[:, :], e.newt[:, :], -0.5, 1.5, ALU.mult, ALU.add).then_inc(step, 1)
    dve.wait_ge(step, n + 4)
    nc.vector.tensor_tensor(e.rstd[:, :], e.rstd[:, :], e.newt[:, :], ALU.mult).then_inc(step, 1)
    dve.wait_ge(step, n + 5)
    return n + 5


def project(nc, e, l, w_qkv, bias_v):
    with ExitStack() as ctx:
        def sb(name, shape, dt=F32):
            return ctx.enter_context(nc.sbuf_tensor(f"{name}{l}", shape, dt))

        def ps(name, shape):
            return ctx.enter_context(nc.psum_tensor(f"{name}{l}", shape, F32))

        def sem(name):
            return new_sem(nc, e, f"pr{l}_{name}")

        w = sb("w_qkv", [P, 3, KD, D])
        bv = sb("bv", [P, D])
        xn = sb("xn", [P, 2, TPC, D])
        hT = sb("hT", [P, 2, KD, CH])
        t32 = sb("t32", [P, 2, CH])
        rest = sb("rest", [P, 2, CH])
        part = sb("part", [P, 2, PARTS, CH], BF16)
        tp = ps("tp", [P, KD, CH])
        qk = ps("qk", [P, 2, CH])
        vp = ps("vp", [P, 2, TPC // 2, D])
        w_loaded, step, stats_ready, root_done = sem("w_loaded"), sem("step"), sem("stats"), sem("root")
        xn_ready, tp_ready, hT_ready = sem("xn_ready"), sem("tp_ready"), sem("hT_ready")
        qk_ready, t32_ready, first_ready, rest_ready = sem("qk_ready"), sem("t32_ready"), sem("first_ready"), sem("rest_ready")
        second_ready, third_ready = sem("second_ready"), sem("third_ready")
        v_ready, v_taken = sem("v_ready"), sem("v_taken")
        stored = [sem("stored0"), sem("stored1")]
        ca, sa = (l * 6 + 1) * KD, (l * 6) * KD
        M = 4

        with nc.Block() as block:
            @block.sync
            def _(sp):
                sp.dma_start(w[:, :, :, :], w_qkv.rearrange("(k p) s n -> p s k n", p=P)).then_inc(w_loaded, 16)
                if bias_v is not None:
                    sp.dma_start(bv[:, :], bias_v.to_broadcast([P, D])).then_inc(w_loaded, 16)

                def body(i):
                    for u in range(2):
                        for m in range(M):
                            sp.wait_ge(third_ready, i * 2 * M + u * M + m + 1)
                            sp.wait_ge(second_ready, i * 2 * M + u * M + m + 1)
                            sp.wait_ge(first_ready, i * 2 * M + u * M + m + 1)
                            dst = (e.q_dram, e.k_dram)[m // KD]
                            g = m % KD
                            sp.dma_start(dst[:, g * P:(g + 1) * P, bass.ds(i * 2 * CH + u * CH, CH)].rearrange("s r t -> r s t"),
                                         part[:, m % 2, :, :]).then_inc(stored[m % 2], 16)

                with sp.Fori(0, NC // 2, 1) as i:
                    body(i)
                for s in stored:
                    sp.wait_ge(s, NC * M // 2 * 16)

            @block.vector
            def _(dve):
                if bias_v is None:
                    nc.vector.memset(bv[:, :], 0.0).then_inc(step, 1)
                    dve.wait_ge(step, 1)
                norm_stats(nc, e, dve, l, sem("norm_step"), stats_ready, root_done, lambda t: e.X[:, t, :])
                if bias_v is not None:
                    dve.wait_ge(w_loaded, 32)

                def normalise(i, u):
                    for t in range(TPC):
                        tile = i * 2 * TPC + u * TPC + t
                        nc.vector.tensor_scalar(xn[:, u, t, :], flat(e.X[:, bass.ds(tile, 1), :]),
                                                e.mv[:, bass.ds(tile, 1), 0], e.rstd[:, bass.ds(tile, 1)],
                                                ALU.subtract, ALU.mult).then_inc(xn_ready, 1)

                def rests(i, u, m):
                    dve.wait_ge(first_ready, i * 2 * M + u * M + m + 1)
                    nc.vector.tensor_tensor(rest[:, m % 2, :], t32[:, m % 2, :], part[:, m % 2, 0, :], ALU.subtract).then_inc(rest_ready, 1)

                with dve.Fori(0, NC // 2, 1) as i:
                    for u in range(2):
                        normalise(i, u)
                        for m in range(M):
                            rests(i, u, m)
                        for q in range(TPC // 2):
                            dve.wait_ge(v_ready, i * 2 * 2 + u * 2 + q + 1)
                            for r in range(2):
                                tile = i * 2 * TPC + u * TPC + q * 2 + r
                                nc.vector.tensor_tensor(
                                    e.V[:, :, bass.ds(tile, 1), :].rearrange("p h o c -> p h (o c)"),
                                    vp[:, q, r, :].rearrange("p (h c) -> p h c", h=H),
                                    bv[:, :].rearrange("p (h c) -> p h c", h=H), ALU.add).then_inc(v_taken, 1)

            @block.scalar
            def _(act):
                act.wait_ge(stats_ready, 1)
                nc.scalar.activation(e.root[:, :], e.var[:, :], ACT.Sqrt).then_inc(root_done, 1)

                with act.Fori(0, NC // 2, 1) as i:
                    for u in range(2):
                        for k in range(KD):
                            act.wait_ge(tp_ready, i * 2 * KD + u * KD + k + 1)
                            nc.scalar.activation(hT[:, u, k, :], tp[:, k, :], ACT.Identity,
                                                 bias=e.col[:, sa + k:sa + k + 1], scale=e.col[:, ca + k:ca + k + 1]).then_inc(hT_ready, 1)
                        for m in range(M):
                            n = i * 2 * M + u * M + m
                            act.wait_ge(qk_ready, n + 1)
                            scale = HS ** -0.5 if m < KD else 1.0
                            if l == 0:
                                nc.scalar.activation(t32[:, m % 2, :], qk[:, m % 2, :], ACT.Identity,
                                                     bias=e.bias_qk[:, m:m + 1], scale=scale).then_inc(t32_ready, 1)
                            else:
                                nc.scalar.activation(t32[:, m % 2, :], qk[:, m % 2, :], ACT.Copy, scale=scale).then_inc(t32_ready, 1)
                            act.wait_ge(t32_ready, n + 1)
                            act.wait_ge(stored[m % 2], (i * M + u * (M // 2) + m // 2) * 16)
                            nc.scalar.activation(part[:, m % 2, 0, :], t32[:, m % 2, :], ACT.Copy).then_inc(first_ready, 1)
                            act.wait_ge(rest_ready, n + 1)
                            nc.scalar.activation(part[:, m % 2, 1, :], rest[:, m % 2, :], ACT.Copy).then_inc(second_ready, 1)

            @block.gpsimd
            def _(pool):
                with pool.Fori(0, NC // 2, 1) as i:
                    for u in range(2):
                        for m in range(M):
                            pool.wait_ge(second_ready, i * 2 * M + u * M + m + 1)
                            nc.gpsimd.tensor_tensor(part[:, m % 2, 2, :], rest[:, m % 2, :], part[:, m % 2, 1, :],
                                                    ALU.subtract).then_inc(third_ready, 1)

            @block.tensor
            def _(pe):
                pe.wait_ge(w_loaded, 16 if bias_v is None else 32)
                with pe.Fori(0, NC // 2, 1) as i:
                    for u in range(2):
                        for k in range(KD):
                            pe.wait_ge(xn_ready, i * 2 * TPC + (u + 1) * TPC)
                            pe.wait_ge(hT_ready, i * 2 * KD + u * KD)
                            for t in range(TPC):
                                last = nc.tensor.transpose(tp[:, k, t * P:(t + 1) * P], xn[:, u, t, k * P:(k + 1) * P], e.ident[:, :])
                            last.then_inc(tp_ready, 1)
                        pe.wait_ge(hT_ready, i * 2 * KD + (u + 1) * KD)
                        for m in range(M):
                            if m >= 2:
                                pe.wait_ge(t32_ready, i * 2 * M + u * M + m - 1)
                            else:
                                pe.wait_ge(t32_ready, i * 2 * M + u * M)
                            for k in range(KD):
                                last = nc.tensor.matmul(qk[:, m % 2, :], w[:, m // KD, k, (m % KD) * P:(m % KD + 1) * P],
                                                        hT[:, u, k, :], start=(k == 0), stop=(k == KD - 1))
                            last.then_inc(qk_ready, 1)
                        for q in range(TPC // 2):
                            pe.wait_ge(v_taken, i * 2 * TPC + u * TPC)
                            for r in range(2):
                                t = q * 2 + r
                                for k in range(KD):
                                    last = nc.tensor.matmul(vp[:, q, r, :], hT[:, u, k, t * P:(t + 1) * P], w[:, 2, k, :],
                                                            start=(k == 0), stop=(k == KD - 1))
                            last.then_inc(v_ready, 1)


def chunk_plan():
    plan = []
    for h in range(2):
        for j in reversed(range(NC)):
            for u in range(j + 1):
                plan.append((h, j, u, u == 0, u == j))
    return plan


def attention(nc, e, l):
    plan = chunk_plan()
    with ExitStack() as ctx:
        def sb(name, shape, dt=F32):
            return ctx.enter_context(nc.sbuf_tensor(f"{name}_a{l}", shape, dt))

        def ps(name, shape):
            return ctx.enter_context(nc.psum_tensor(f"{name}_a{l}", shape, F32))

        def sem(name):
            return new_sem(nc, e, f"at{l}_{name}")

        q_stack = [sb(f"q_stack{p}", [P, T], BF16) for p in range(2)]
        k_stack = [sb(f"k_stack{p}", [P, T], BF16) for p in range(2)]
        v_head = sb("v_head", [P, 2, NT, VC])
        prob = sb("prob", [P, RING, TPC, CH])
        acc_sb = sb("acc_sb", [P, CH])
        block_max = sb("block_max", [P, 2, TPC, NC])
        neg_max = sb("neg_max", [P, TPC])
        neg_rest = sb("neg_rest", [P, TPC])
        neg_part = sb("neg_part", [P, TPC, PARTS], BF16)
        recip = sb("recip", [P, TPC])
        scores = ps("scores", [P, 2, 2, CH])
        tops = ps("tops", [P, 2, CH])
        acc = ps("acc", [P, CH])
        aux = ps("aux", [P, CH])
        neg_ps = aux[:, 0:CH // 2].bitcast(BF16)
        out_ps = aux[:, CH // 2:CH // 2 + TPC * VC].rearrange("p (t c) -> p t c", t=TPC)

        loaded = [sem("loaded0"), sem("loaded1")]
        ones_set, v_staged = sem("ones_set"), sem("v_staged")
        scores_ready, exp_done, pv_done, acc_saved = sem("scores_ready"), sem("exp_done"), sem("pv_done"), sem("acc_saved")
        top_ready, top_taken = sem("top_ready"), sem("top_taken")
        neg_ready, neg_rows_ready, neg_rows_set = sem("neg_ready"), sem("neg_rows_ready"), sem("neg_rows_set")
        out_ready, out_taken = sem("out_ready"), sem("out_taken")
        recip_done, step = sem("recip_done"), sem("step")
        LOADS = 2 * len(PAIRS) * 16
        ITERS = H // 2
        CHUNKS = 2 * NC

        def chunks_before(n):
            return (n // SLOTS) * CHUNKS + sum(1 for x in plan[:n % SLOTS] if x[4])

        def chunk_of(c):
            return (c // NC) % 2, NC - 1 - c % NC

        HEAD2 = QUADS
        assert SLOTS % RING == 0 and not any(plan[LOOK - d][4] for d in (1, 2, 3))

        with nc.Block() as block:
            @block.sync
            def _(sp):
                def load(p, head):
                    for n, (a, b) in enumerate(PAIRS):
                        sp.dma_start(q_stack[p][n * HS:(n + 1) * HS, :], e.q_heads[a, bass.ds(head, 1), :, :].rearrange("o r t -> (o r) t")
                                     ).then_inc(loaded[p], 16)
                        sp.dma_start(k_stack[p][n * HS:(n + 1) * HS, :], e.k_heads[b, bass.ds(head, 1), :, :].rearrange("o r t -> (o r) t")
                                     ).then_inc(loaded[p], 16)

                load(0, 0)
                load(1, 1)
                with sp.Fori(0, ITERS - 1, 1) as i:
                    for p in range(2):
                        sp.wait_ge(scores_ready, i * 2 * SLOTS + 2 * (HEAD2 * (p + 1)))
                        load(p, i * 2 + 2 + p)
                sp.wait_ge(scores_ready, (ITERS - 1) * 2 * SLOTS + 2 * HEAD2)
                load(0, 0)
                sp.wait_ge(loaded[0], LOADS * (ITERS + 1))

            @block.gpsimd
            def _(pool):
                for p in range(2):
                    nc.gpsimd.memset(k_stack[p][SR:P, :], 1.0).then_inc(ones_set, 1)
                pool.wait_ge(ones_set, 2)
                nc.gpsimd.memset(v_head[:, :, :, HS:VC], 0.0).then_inc(ones_set, 1)
                pool.wait_ge(ones_set, 3)
                nc.gpsimd.memset(v_head[:, :, :, HS:HS + 1], 1.0).then_inc(ones_set, 1)

                def stage(p, head):
                    nc.gpsimd.tensor_copy(v_head[:, p, :, 0:HS], e.V[:, bass.ds(head, 1), :, :].rearrange("p o t c -> p (o t) c")
                                          ).then_inc(v_staged, 1)

                pool.wait_ge(ones_set, 4)
                stage(0, 0)
                stage(1, 1)
                with pool.Fori(0, ITERS - 1, 1) as i:
                    for p in range(2):
                        pool.wait_ge(pv_done, i * SLOTS + HEAD2 * (p + 1))
                        stage(p, i * 2 + 2 + p)

            @block.tensor
            def _(pe):
                def main_scores(i, n, half):
                    h, j, u, first, last = plan[n % SLOTS]
                    if n > 0:
                        pe.wait_ge(exp_done, i * 2 * SLOTS + 2 * n + half - 1)
                    if half == 0 and first:
                        pe.wait_ge(neg_rows_set, i * CHUNKS + chunks_before(n) + 1)
                    for b in range(2):
                        kb = 2 * half + b
                        diag = u == j
                        c0 = P * kb if diag and j else 0
                        last_mm = nc.tensor.matmul(scores[:, half, b, c0:CH],
                                                   k_stack[h][0:MR, u * CH + kb * P:u * CH + (kb + 1) * P],
                                                   q_stack[h][0:MR, j * CH + c0:(j + 1) * CH], start=True, stop=not diag)
                        if diag:
                            m0 = P * kb if j else 0
                            last_mm = nc.tensor.matmul(scores[:, half, b, m0:P * (kb + 1)], e.ident_b[:, :],
                                                       e.mask_q[:, CH - (P * kb - m0):CH + P], start=False, stop=True)
                    last_mm.then_inc(scores_ready, 1)

                def top_scores(i, n, t):
                    h, j, u, first, last = plan[n % SLOTS]
                    m = 4 * n + t
                    if m >= 2:
                        pe.wait_ge(top_taken, i * TPC * SLOTS + m - 1)
                    if t == 0 and j == NC - 1 and first:
                        pe.wait_ge(loaded[h], i * LOADS + (n // SLOTS + 1) * LOADS)
                    diag = u == j
                    width = P * (t + 1) if diag else CH
                    last_mm = nc.tensor.matmul(tops[:, m % 2, 0:width], q_stack[h][0:SR, j * CH + t * P:j * CH + (t + 1) * P],
                                               k_stack[h][0:SR, u * CH:u * CH + width], start=True, stop=not diag)
                    if diag:
                        last_mm = nc.tensor.matmul(tops[:, m % 2, t * P:width], e.ident_b[:, :], e.mask_k[:, :], start=False, stop=True)
                    last_mm.then_inc(top_ready, 1)

                def neg_rows(i, c, outs):
                    pe.wait_ge(neg_ready, i * CHUNKS + c + 1)
                    if c:
                        pe.wait_ge(neg_rows_set, i * CHUNKS + c)
                    if outs is not None:
                        pe.wait_ge(out_taken, i * CHUNKS + outs)
                    for t in range(TPC):
                        last_mm = nc.tensor.transpose(neg_ps[SR:SR + PARTS, t * P:(t + 1) * P], neg_part[:, t, :], e.ident_b[:, :])
                    last_mm.then_inc(neg_rows_ready, 1)

                def outputs(i, c, rows):
                    pe.wait_ge(acc_saved, i * CHUNKS + c + 1)
                    pe.wait_ge(out_taken, i * CHUNKS + c)
                    pe.wait_ge(neg_rows_set, i * CHUNKS + rows)
                    for t in range(TPC):
                        last_mm = nc.tensor.matmul(out_ps[:, t, :], acc_sb[:, t * P:(t + 1) * P], e.sum4[:, :], start=True, stop=True)
                    last_mm.then_inc(out_ready, 1)

                def weigh(i, n):
                    h, j, u, first, last = plan[n]
                    pe.wait_ge(exp_done, i * 2 * SLOTS + 2 * n + 2)
                    if first:
                        pe.wait_ge(acc_saved, i * CHUNKS + chunks_before(n))
                        if j == NC - 1:
                            pe.wait_ge(v_staged, i * 2 + h + 1)
                    for kb in range(TPC):
                        c0 = P * kb if u == j and j else 0
                        last_mm = nc.tensor.matmul(acc[VC * kb:VC * (kb + 1), c0:CH], v_head[:, h, u * TPC + kb, :],
                                                   prob[:, n % RING, kb, c0:CH], start=first, stop=last, skip_group_check=True)
                    last_mm.then_inc(pv_done, 1)

                pe.wait_ge(ones_set, 4)
                pe.wait_ge(loaded[1], LOADS)
                for n in range(LOOK):
                    for t in range(TPC):
                        top_scores(0, n, t)
                    if n >= 2 and plan[n - 2][4]:
                        neg_rows(0, chunks_before(n - 2), None)
                main_scores(0, 0, 0)
                main_scores(0, 0, 1)

                with pe.Fori(0, ITERS, 1) as i:
                    for n in range(SLOTS):
                        ahead = n + LOOK
                        main_scores(i, n + 1, 0)
                        top_scores(i, ahead, 0)
                        main_scores(i, n + 1, 1)
                        top_scores(i, ahead, 1)
                        top_scores(i, ahead, 2)
                        if plan[(ahead - 2) % SLOTS][4]:
                            neg_rows(i, chunks_before(ahead - 2), chunks_before(max(n - 1, 0)))
                        weigh(i, n)
                        top_scores(i, ahead, 3)
                        if n > 0 and plan[n - 1][4]:
                            outputs(i, chunks_before(n - 1), chunks_before(ahead - 1))
                    outputs(i, CHUNKS - 1, chunks_before(SLOTS + LOOK - 2))

            @block.scalar
            def _(act):
                def neg_rows_out(i, c):
                    act.wait_ge(neg_rows_ready, i * CHUNKS + c + 1)
                    h, j = chunk_of(c)
                    nc.scalar.activation(q_stack[h][SR:SR + PARTS, j * CH:(j + 1) * CH], neg_ps[SR:SR + PARTS, :], ACT.Copy).then_inc(neg_rows_set, 1)

                def exps(i, n, half):
                    h, j, u, first, last = plan[n % SLOTS]
                    act.wait_ge(scores_ready, i * 2 * SLOTS + 2 * n + half + 1)
                    c0 = 2 * P if u == j and j and half else 0
                    nc.scalar.activation(prob[:, n % RING, 2 * half:2 * half + 2, c0:CH], scores[:, half, :, c0:CH], ACT.Exp
                                         ).then_inc(exp_done, 1)

                def save(i, n):
                    act.wait_ge(pv_done, i * SLOTS + n + 1)
                    if chunks_before(n):
                        act.wait_ge(out_ready, i * CHUNKS + chunks_before(n))
                    nc.scalar.activation(acc_sb[:, :], acc[:, :], ACT.Copy).then_inc(acc_saved, 1)

                for n in range(LOOK - 2):
                    if plan[n][4]:
                        neg_rows_out(0, chunks_before(n))
                with act.Fori(0, ITERS, 1) as i:
                    for n in range(SLOTS):
                        if n >= RING:
                            act.wait_ge(pv_done, i * SLOTS + n - RING + 1)
                        exps(i, n, 0)
                        exps(i, n, 1)
                        if n and plan[(n + LOOK - 3) % SLOTS][4]:
                            neg_rows_out(i, chunks_before(n + LOOK - 3))
                        if n and plan[n - 1][4]:
                            save(i, n - 1)
                    save(i, SLOTS - 1)

            @block.vector
            def _(dve):
                CHAIN = 3

                def top(i, n, t):
                    h, j, u, first, last = plan[n % SLOTS]
                    m = 4 * n + t
                    dve.wait_ge(top_ready, i * TPC * SLOTS + m + 1)
                    width = P * (t + 1) if u == j else CH
                    nc.vector.tensor_reduce(block_max[:, j % 2, t, u:u + 1], tops[:, m % 2, 0:width], AX.X, ALU.max).then_inc(top_taken, 1)

                def negate(i, n, s):
                    j, c = plan[n % SLOTS][1], chunks_before(n)
                    seen = i * CHUNKS * CHAIN + CHAIN * c
                    if s == 0:
                        dve.wait_ge(top_taken, i * TPC * SLOTS + TPC * (n + 1))
                        if c:
                            dve.wait_ge(neg_rows_ready, i * CHUNKS + c)
                        nc.vector.tensor_reduce(neg_part[:, :, 0], block_max[:, j % 2, :, 0:j + 1], AX.X, ALU.max, negate=True)
                        nc.vector.tensor_reduce(neg_max[:, :], block_max[:, j % 2, :, 0:j + 1], AX.X, ALU.max, negate=True).then_inc(step, 1)
                    elif s == 1:
                        dve.wait_ge(step, seen + 1)
                        nc.vector.tensor_tensor(neg_rest[:, :], neg_max[:, :], neg_part[:, :, 0], ALU.subtract).then_inc(step, 1)
                    elif s == 2:
                        dve.wait_ge(step, seen + 2)
                        nc.vector.tensor_copy(neg_part[:, :, 1], neg_rest[:, :]).then_inc(step, 1)
                    else:
                        dve.wait_ge(step, seen + 3)
                        nc.vector.tensor_tensor(neg_part[:, :, 2], neg_rest[:, :], neg_part[:, :, 1], ALU.subtract).then_inc(neg_ready, 1)

                def normalise(i, c, s):
                    h, j = chunk_of(c)
                    if s == 0:
                        dve.wait_ge(out_ready, i * CHUNKS + c + 1)
                        nc.vector.reciprocal(recip[:, :], out_ps[:, :, HS]).then_inc(recip_done, 1)
                    else:
                        dve.wait_ge(recip_done, i * CHUNKS + c + 1)
                        nc.vector.tensor_tensor(e.O[:, j * TPC:(j + 1) * TPC, bass.ds((i * 2 + h) * HS, HS)],
                                                out_ps[:, :, 0:HS], recip[:, :].rearrange("p (t o) -> p t o", o=1).to_broadcast([P, TPC, HS]),
                                                ALU.mult).then_inc(out_taken, 1)

                def tops_down(i, n, out_chunk):
                    for t in range(TPC):
                        top(i, n, t)
                        if n and plan[(n - 1) % SLOTS][4]:
                            negate(i, n - 1, t)
                        if out_chunk is not None and t < 2:
                            normalise(i, out_chunk, t)

                for n in range(LOOK):
                    tops_down(0, n, None)
                with dve.Fori(0, ITERS, 1) as i:
                    for n in range(SLOTS):
                        tops_down(i, n + LOOK, chunks_before(n - 2) if n > 1 and plan[n - 2][4] else None)
                    for c in (CHUNKS - 2, CHUNKS - 1):
                        normalise(i, c, 0)
                        normalise(i, c, 1)


def project_out(nc, e):
    with ExitStack() as ctx:
        def sem(name):
            return new_sem(nc, e, f"po_{name}")

        o_in = ctx.enter_context(nc.sbuf_tensor("o_in", [P, 2, TPC, D], F32))
        oT = ctx.enter_context(nc.sbuf_tensor("oT", [P, 2, KD, CH], F32))
        tp = ctx.enter_context(nc.psum_tensor("po_tp", [P, KD, CH], F32))
        y = ctx.enter_context(nc.psum_tensor("po_y", [P, 2, TPC, D], F32))
        staged, turned, oT_ready, y_ready, added = sem("staged"), sem("turned"), sem("oT"), sem("y"), sem("added")

        with nc.Block() as block:
            @block.gpsimd
            def _(pool):
                with pool.Fori(0, NC // 2, 1) as i:
                    for u in range(2):
                        pool.wait_ge(turned, i * 2)
                        nc.gpsimd.tensor_copy(o_in[:, u, :, :], e.O[:, bass.ds(i * 2 * TPC + u * TPC, TPC), :]).then_inc(staged, 1)

            @block.tensor
            def _(pe):
                with pe.Fori(0, NC // 2, 1) as i:
                    for u in range(2):
                        pe.wait_ge(staged, i * 2 + u + 1)
                        pe.wait_ge(oT_ready, (i * 2 + u) * KD)
                        for k in range(KD):
                            for t in range(TPC):
                                last = nc.tensor.transpose(tp[:, k, t * P:(t + 1) * P], o_in[:, u, t, k * P:(k + 1) * P], e.ident[:, :])
                        last.then_inc(turned, 1)
                        pe.wait_ge(oT_ready, (i * 2 + u + 1) * KD)
                        pe.wait_ge(added, i * 2)
                        for t in range(TPC):
                            for k in range(KD):
                                nc.tensor.matmul(y[:, u, t, :], oT[:, u, k, t * P:(t + 1) * P], e.w_out0[:, k, :], start=(k == 0), stop=False)
                            last = nc.tensor.matmul(y[:, u, t, :], e.ones[0:1, :], e.b_out0[:, :], start=False, stop=True)
                        last.then_inc(y_ready, 1)

            @block.scalar
            def _(act):
                with act.Fori(0, NC // 2, 1) as i:
                    for u in range(2):
                        act.wait_ge(turned, i * 2 + u + 1)
                        for k in range(KD):
                            nc.scalar.activation(oT[:, u, k, :], tp[:, k, :], ACT.Copy).then_inc(oT_ready, 1)

            @block.vector
            def _(dve):
                with dve.Fori(0, NC // 2, 1) as i:
                    for u in range(2):
                        dve.wait_ge(y_ready, i * 2 + u + 1)
                        x = e.X[:, bass.ds(i * 2 * TPC + u * TPC, TPC), :]
                        nc.vector.tensor_tensor(x, y[:, u, :, :], x, ALU.add).then_inc(added, 1)


def feed_norm(nc, e, l, gate_w, gate_bias, outs):
    with ExitStack() as ctx:
        def sb(name, shape, dt=F32):
            return ctx.enter_context(nc.sbuf_tensor(f"fn{l}_{name}", shape, dt))

        def ps(name, shape):
            return ctx.enter_context(nc.psum_tensor(f"fn{l}_{name}", shape, F32))

        def sem(name):
            return new_sem(nc, e, f"fn{l}_{name}")

        G = outs
        xn = sb("xn", [P, 2, TPC, D])
        hTc = sb("hTc", [P, 2, KD, CH])
        row_h = sb("row_h", [P, 2, TPC, D]) if l == 0 else None
        gw = sb("gw", [P, KD, G])
        gb = sb("gb", [1, G])
        tp = ps("tp", [P, KD, CH])
        lg = ps("lg", [P, TPC, 128])
        turned_sel = ps("turned_sel", [P, CH])
        if l == 0:
            best = sb("best", [P, TPC, 8])
            left = sb("left", [P, TPC, E0])
            sel = sb("sel", [P, 2, TPC, E0])
            rank = sb("rank", [P, NT])
            rank_i = sb("rank_i", [P, NT], I32)
        ld, step, stats_ready, root_done = sem("ld"), sem("step"), sem("stats"), sem("root")
        xn_ready, turned, hT_ready, rows_ready, lg_ready, lg_taken = sem("xn"), sem("turned"), sem("hT"), sem("rows"), sem("lg"), sem("lg_taken")
        stored, sel_ready, sel_turned, order_ready, chain, scaled = sem("stored"), sem("sel"), sem("sel_turned"), sem("order"), sem("chain"), sem("scaled")
        rank_ready, copied = sem("rank"), sem("copied")
        cb, sb_ = (l * 6 + 4) * KD, (l * 6 + 3) * KD
        row_c, row_s = (e.row_cb0, e.row_sb0) if l == 0 else (e.row_cb1, e.row_sb1)
        NL = 1 if gate_bias is None else 2
        COPIES = 2 * KD if l == 0 else KD
        if l == 1:
            nil = sb("nil", [P, D])
            nil_set, cleared = sem("nil_set"), sem("cleared")

        with nc.Block() as block:
            @block.sync
            def _(sp):
                sp.dma_start(gw[:, :, :], gate_w.rearrange("(k p) n -> p k n", p=P)).then_inc(ld, 16)
                if gate_bias is not None:
                    sp.dma_start(gb[:, :], gate_bias).then_inc(ld, 16)
                if l == 1:
                    sp.wait_ge(nil_set, 1)
                    rows = e.queue.rearrange("(n t p) d -> n p t d", p=P, t=E1)
                    for n in range(e.queue.shape[0] // (P * E1)):
                        sp.dma_start(rows[n], nil[:, :].rearrange("p (o d) -> p o d", o=1).to_broadcast([P, E1, D])).then_inc(cleared, 16)
                    sp.wait_ge(cleared, 16 * (e.queue.shape[0] // (P * E1)))
                if l == 0:
                    table = e.table.rearrange("(c t p) w -> c p t w", t=TPC, p=P)
                    with sp.Fori(0, NC // 2, 1) as i:
                        for u in range(2):
                            sp.wait_ge(rows_ready, i * 2 + u + 1)
                            sp.dma_start(table[bass.ds(i * 2 + u, 1), :, :, 0:D].rearrange("o p t w -> (o p) t w"), row_h[:, u, :, :]).then_inc(stored, 16)
                    sp.wait_ge(stored, 16 * NC)

            @block.vector
            def _(dve):
                norm_stats(nc, e, dve, l, sem("norm_step"), stats_ready, root_done, lambda t: e.X[:, t, :])
                if l == 0:
                    dve.wait_ge(rank_ready, 1)
                    nc.vector.tensor_copy(rank[:, :], rank_i[:, :]).then_inc(step, 1)
                    dve.wait_ge(step, 1)
                STEPS = 2
                with dve.Fori(0, NC // 2, 1) as i:
                    for u in range(2):
                        dve.wait_ge(rows_ready, i * 2)
                        dve.wait_ge(turned, i * 2)
                        for t in range(TPC):
                            tile = i * 2 * TPC + u * TPC + t
                            nc.vector.tensor_scalar(xn[:, u, t, :], flat(e.X[:, bass.ds(tile, 1), :]), e.mv[:, bass.ds(tile, 1), 0],
                                                    e.rstd[:, bass.ds(tile, 1)], ALU.subtract, ALU.mult).then_inc(xn_ready, 1)
                        dve.wait_ge(lg_ready, i * 2 + u + 1)
                        logits = e.logits[:, bass.ds(i * 2 * TPC + u * TPC, TPC), :]
                        nc.vector.tensor_copy(logits, lg[:, :, 0:G]).then_inc(lg_taken, 1)
                        if l == 0:
                            for t in range(TPC):
                                nc.vector.max(best[:, t, :], lg[:, t, 0:E0]).then_inc(chain, 1)
                            c = i * 2 * 2 * TPC + u * 2 * TPC
                            dve.wait_ge(chain, c + TPC)
                            settle(dve)
                            for t in range(TPC):
                                nc.vector.match_replace(left[:, t, :], best[:, t, :], lg[:, t, 0:E0], MASKED).then_inc(chain, 1)
                            dve.wait_ge(chain, c + 2 * TPC)
                            nc.vector.tensor_tensor(e.chosen[:, bass.ds(i * 2 * TPC + u * TPC, TPC), :], lg[:, :, 0:E0], left[:, :, :], ALU.not_equal).then_inc(scaled, 1)
                            dve.wait_ge(scaled, i * 2 + u + 1)
                            dve.wait_ge(sel_turned, i * 2)
                            nc.vector.tensor_tensor(sel[:, u, :, :], e.chosen[:, bass.ds(i * 2 * TPC + u * TPC, TPC), :],
                                                    rank[:, bass.ds(i * 2 * TPC + u * TPC, TPC)].rearrange("p (t o) -> p t o", o=1).to_broadcast([P, TPC, E0]),
                                                    ALU.mult).then_inc(sel_ready, 1)

            @block.gpsimd
            def _(pool):
                if l == 1:
                    nc.gpsimd.memset(nil[:, :], 0.0).then_inc(nil_set, 1)
                if l == 0:
                    nc.gpsimd.iota(rank_i[:, :], [[-P, NT]], base=T, channel_multiplier=-1).then_inc(rank_ready, 1)
                with pool.Fori(0, NC // 2, 1) as i:
                    for u in range(2):
                        pool.wait_ge(xn_ready, i * 2 * TPC + (u + 1) * TPC)
                        if l == 0:
                            pool.wait_ge(stored, i * 32)
                            dst = row_h[:, u, :, :]
                        else:
                            dst = e.H[:, bass.ds(i * 2 * TPC + u * TPC, TPC), :]
                        wide = lambda row: row[:, :].rearrange("p (o d) -> p o d", o=1).to_broadcast([P, TPC, D])
                        nc.gpsimd.tensor_tensor(dst, xn[:, u, :, :], wide(row_c), ALU.mult).then_inc(copied, 1)
                        pool.wait_ge(copied, i * 2 + u + 1)
                        settle(pool)
                        nc.gpsimd.tensor_tensor(dst, dst, wide(row_s), ALU.add).then_inc(rows_ready, 1)

            @block.scalar
            def _(act):
                act.wait_ge(stats_ready, 1)
                nc.scalar.activation(e.root[:, :], e.var[:, :], ACT.Sqrt).then_inc(root_done, 1)
                with act.Fori(0, NC // 2, 1) as i:
                    for u in range(2):
                        act.wait_ge(turned, i * 2 + u + 1)
                        act.wait_ge(lg_ready, i * 2)
                        for k in range(KD):
                            nc.scalar.activation(hTc[:, u, k, :], tp[:, k, :], ACT.Identity,
                                                 bias=e.col[:, sb_ + k:sb_ + k + 1], scale=e.col[:, cb + k:cb + k + 1]).then_inc(hT_ready, 1)
                            if l == 0:
                                nc.scalar.activation(e.hT[:, k, bass.ds(i * 2 * CH + u * CH, CH)], tp[:, k, :], ACT.Identity,
                                                     bias=e.col[:, sb_ + k:sb_ + k + 1], scale=e.col[:, cb + k:cb + k + 1]).then_inc(hT_ready, 1)
                        if l == 0:
                            act.wait_ge(sel_turned, i * 2 + u + 1)
                            nc.scalar.activation(e.order[E0 * u:E0 * (u + 1), bass.ds(i * CH, CH)], turned_sel[E0 * u:E0 * (u + 1), :], ACT.Copy).then_inc(order_ready, 1)

            @block.tensor
            def _(pe):
                pe.wait_ge(ld, 16 * NL)
                with pe.Fori(0, NC // 2, 1) as i:
                    for u in range(2):
                        pe.wait_ge(xn_ready, i * 2 * TPC + (u + 1) * TPC)
                        pe.wait_ge(hT_ready, (i * 2 + u) * COPIES)
                        for k in range(KD):
                            for t in range(TPC):
                                last = nc.tensor.transpose(tp[:, k, t * P:(t + 1) * P], xn[:, u, t, k * P:(k + 1) * P], e.ident[:, :])
                        last.then_inc(turned, 1)
                        pe.wait_ge(hT_ready, (i * 2 + u + 1) * COPIES)
                        pe.wait_ge(lg_taken, i * 2 + u)
                        if l == 0:
                            pe.wait_ge(scaled, i * 2 + u)
                        for t in range(TPC):
                            for k in range(KD):
                                last = nc.tensor.matmul(lg[:, t, 0:G], hTc[:, u, k, t * P:(t + 1) * P], gw[:, k, :],
                                                        start=(k == 0), stop=(k == KD - 1 and gate_bias is None))
                            if gate_bias is not None:
                                last = nc.tensor.matmul(lg[:, t, 0:G], e.ones[0:1, :], gb[:, :], start=False, stop=True)
                        last.then_inc(lg_ready, 1)
                        if l == 0:
                            pe.wait_ge(sel_ready, i * 2 + u + 1)
                            pe.wait_ge(order_ready, i * 2 + u)
                            for t in range(TPC):
                                last = nc.tensor.matmul(turned_sel[E0 * u:E0 * (u + 1), t * P:(t + 1) * P], sel[:, u, t, :], e.ident[:, :],
                                                        start=True, stop=True)
                            last.then_inc(sel_turned, 1)


def shared_expert(nc, e, a):
    with ExitStack() as ctx:
        def sb(name, shape, dt=F32):
            return ctx.enter_context(nc.sbuf_tensor(f"se_{name}", shape, dt))

        def ps(name, shape):
            return ctx.enter_context(nc.psum_tensor(f"se_{name}", shape, F32))

        def sem(name):
            return new_sem(nc, e, f"se_{name}")

        FT = IS // P
        wu = sb("wu", [P, KD, 2 * IS])
        wd = sb("wd", [P, FT, D])
        aT = sb("aT", [P, 2, FT, CH])
        silu = sb("silu", [P, 2, CH])
        weight = sb("weight", [P, NT, E0])
        small = sb("small", [P, 3, NT])
        sig = sb("sig", [P, NT])
        cand = sb("cand", [P, CAP])
        eight = sb("eight", [P, 2 * (CAP // 8 // NC), 8])
        both = sb("both", [E0, 2, CAP])
        first = sb("first", [E0, CAP])
        slot_f = sb("slot_f", [P, 2, E0])
        shared_y = sb("shared_y", [P, 2, TPC, D])
        up = ps("up", [P, 2, 2, CH])
        y = ps("y", [P, TPC, D])
        tk = ps("tk", [P, E0])
        ld, softmax_in, softmax_ex, chain, weight_ready, sig_ready, tanh_done = (sem(n) for n in ("ld", "sm_in", "sm_ex", "chain", "weight", "sig", "tanh"))
        up_ready, silu_ready, a_ready, y_ready, y_taken, x_ready, stored = (sem(n) for n in ("up", "silu", "a", "y", "y_taken", "x", "stored"))
        found, moved, tk_ready, table_stored = (sem(n) for n in ("found", "moved", "tk", "table"))
        rounds = CAP // 8 // NC

        with nc.Block() as block:
            @block.sync
            def _(sp):
                sp.dma_start(wu[:, :, :], a.L0_shared_up.rearrange("(k p) n -> p k n", p=P)).then_inc(ld, 16)
                sp.dma_start(wd[:, :, :], a.L0_shared_down.rearrange("(k p) n -> p k n", p=P)).then_inc(ld, 16)
                sp.wait_ge(weight_ready, 1)
                sp.dma_start(e.table.rearrange("(t p) w -> p t w", p=P)[:, :, D:ROW0], weight[:, :, :]).then_inc(table_stored, 16)
                xs = e.x_dram.rearrange("(c t p) d -> c p t d", t=TPC, p=P)
                with sp.Fori(0, NC, 1) as i:
                    sp.wait_ge(x_ready, i + 1)
                    sp.dma_start(xs[bass.ds(i, 1)].rearrange("o p t d -> (o p) t d"), e.X[:, bass.ds(i * TPC, TPC), :]).then_inc(stored, 16)
                sp.wait_ge(found, 3 * rounds * NC)
                sp.dma_start(both[:, 0, :], cand[0:E0, :]).then_inc(moved, 16)
                sp.dma_start(both[:, 1, :], cand[E0:P, :]).then_inc(moved, 16)
                sp.wait_ge(stored, 16 * NC)
                sp.wait_ge(table_stored, 16)

            @block.vector
            def _(dve):
                n = [0]

                def link(ins):
                    n[0] += 1
                    ins.then_inc(chain, 1)
                    dve.wait_ge(chain, n[0])

                experts = e.logits[:, :, 0:E0]
                wide = lambda s: small[:, s, :].rearrange("p (t o) -> p t o", o=1).to_broadcast([P, NT, E0])
                link(nc.vector.tensor_reduce(small[:, 0, :], experts, AX.X, ALU.max))
                nc.vector.tensor_tensor(weight[:, :, :], experts, wide(0), ALU.subtract).then_inc(softmax_in, 1)
                dve.wait_ge(softmax_ex, 1)
                link(nc.vector.tensor_tensor(weight[:, :, :], weight[:, :, :], e.chosen[:, :, :], ALU.mult))
                link(nc.vector.tensor_reduce(small[:, 1, :], weight[:, :, :], AX.X, ALU.add))
                link(nc.vector.reciprocal(small[:, 2, :], small[:, 1, :]))
                nc.vector.tensor_tensor(weight[:, :, :], weight[:, :, :], wide(2), ALU.mult).then_inc(weight_ready, 1)
                dve.wait_ge(tanh_done, 1)
                nc.vector.tensor_scalar(sig[:, :], sig[:, :], 0.5, 0.5, ALU.mult, ALU.add).then_inc(sig_ready, 1)
                dve.wait_ge(sig_ready, 1)

                with dve.Fori(0, NC // 2, 1) as i:
                    for u in range(2):
                        for f in range(FT):
                            m = u * FT + f
                            dve.wait_ge(silu_ready, i * 2 * FT + m + 1)
                            nc.vector.tensor_tensor(aT[:, u, f, :], silu[:, m % 2, :], up[:, m % 2, 1, :], ALU.mult).then_inc(a_ready, 1)
                            if f % 2 == 0:
                                r = u * rounds + f // 2
                                done = i * 6 * rounds + r * 3
                                dve.wait_ge(found, done)
                                settle(dve)
                                nc.vector.max(eight[:, r, :], e.order[:, :]).then_inc(found, 1)
                                dve.wait_ge(found, done + 1)
                                settle(dve)
                                nc.vector.match_replace(e.order[:, :], eight[:, r, :], e.order[:, :], 0.0).then_inc(found, 1)
                                nc.vector.tensor_copy(cand[:, bass.ds(i * 2 * rounds * 8 + r * 8, 8)], eight[:, r, :]).then_inc(found, 1)
                        dve.wait_ge(y_ready, i * 2 + u + 1)
                        for t in range(TPC):
                            tile = i * 2 * TPC + u * TPC + t
                            nc.vector.scalar_tensor_tensor(shared_y[:, u, t, :], y[:, t, :], sig[:, bass.ds(tile, 1)], e.row_gb0[:, :],
                                                           ALU.mult, ALU.mult).then_inc(y_taken, 1)
                        x = e.X[:, bass.ds(i * 2 * TPC + u * TPC, TPC), :]
                        dve.wait_ge(y_taken, i * 2 * TPC + (u + 1) * TPC)
                        nc.vector.tensor_tensor(x, x, shared_y[:, u, :, :], ALU.add).then_inc(x_ready, 1)
                dve.wait_ge(moved, 32)
                for r in range(CAP // 8):
                    link(nc.vector.max(first[:, r * 8:(r + 1) * 8], both[:, :, :]))
                    link(nc.vector.match_replace(both[:, :, :], first[:, r * 8:(r + 1) * 8], both[:, :, :], 0.0))
                dve.wait_ge(tk_ready, 1)
                link(nc.vector.tensor_scalar(slot_f[:, 0, :], tk[:, :], -1.0, float(T), ALU.mult, ALU.add))
                link(nc.vector.tensor_scalar(slot_f[:, 1, :], slot_f[:, 0, :], float(T - 1), None, ALU.min))
                link(nc.vector.tensor_copy(e.to_token[:, :], slot_f[:, 0, :]))
                link(nc.vector.tensor_copy(e.from_token[:, :], slot_f[:, 1, :]))

            @block.scalar
            def _(act):
                act.wait_ge(softmax_in, 1)
                nc.scalar.activation(weight[:, :, :], weight[:, :, :], ACT.Exp).then_inc(softmax_ex, 1)
                nc.scalar.activation(sig[:, :], e.logits[:, :, E0], ACT.Tanh, scale=0.5).then_inc(tanh_done, 1)
                with act.Fori(0, NC // 2, 1) as i:
                    for u in range(2):
                        for f in range(FT):
                            m = u * FT + f
                            act.wait_ge(up_ready, i * 2 * FT + m + 1)
                            act.wait_ge(a_ready, i * 2 * FT + max(m - 1, 0))
                            nc.scalar.activation(silu[:, m % 2, :], up[:, m % 2, 0, :], ACT.Silu).then_inc(silu_ready, 1)

            @block.tensor
            def _(pe):
                pe.wait_ge(ld, 32)
                with pe.Fori(0, NC // 2, 1) as i:
                    for u in range(2):
                        for f in range(FT):
                            m = u * FT + f
                            pe.wait_ge(a_ready, i * 2 * FT + max(m - 1, 0))
                            for s in range(2):
                                for k in range(KD):
                                    last = nc.tensor.matmul(up[:, m % 2, s, :], wu[:, k, s * IS + f * P:s * IS + (f + 1) * P],
                                                            e.hT[:, k, bass.ds(i * 2 * CH + u * CH, CH)], start=(k == 0), stop=(k == KD - 1))
                            last.then_inc(up_ready, 1)
                        pe.wait_ge(a_ready, i * 2 * FT + (u + 1) * FT)
                        pe.wait_ge(y_taken, i * 2 * TPC + u * TPC)
                        for t in range(TPC):
                            for f in range(FT):
                                last = nc.tensor.matmul(y[:, t, :], aT[:, u, f, t * P:(t + 1) * P], wd[:, f, :], start=(f == 0), stop=(f == FT - 1))
                        last.then_inc(y_ready, 1)
                pe.wait_ge(chain, 4 + 2 * (CAP // 8))
                nc.tensor.transpose(tk[:, :], first[:, :], e.ident[0:E0, 0:E0]).then_inc(tk_ready, 1)


def routed_experts(nc, e, a):
    R = 4
    BODIES = E0 // R
    with ExitStack() as ctx:
        def sb(name, shape, dt=F32):
            return ctx.enter_context(nc.sbuf_tensor(f"re_{name}", shape, dt))

        def ps(name, shape):
            return ctx.enter_context(nc.psum_tensor(f"re_{name}", shape, F32))

        def sem(name):
            return new_sem(nc, e, f"re_{name}")

        wu = sb("wu", [P, R, KD, 2 * I0])
        wd = sb("wd", [P, R, D])
        rows = sb("rows", [P, R, ROW0])
        read_at = sb("read_at", [P, R, 1], I32)
        add_at = sb("add_at", [P, R, 1], I32)
        w = sb("w", [P, R, 1])
        rT = sb("rT", [P, 2, KD, CAP])
        silu = sb("silu", [P, 2, I0])
        act_rows = sb("act_rows", [P, 2, I0])
        actT = sb("actT", [P, 2, CAP])
        add = sb("add", [P, R, D])
        tp = ps("tp", [P, 2, KD, CAP])
        up = ps("up", [P, 2, 2 * I0])
        ta = ps("ta", [P, 2, CAP])
        y = ps("y", [P, 2, D])
        w_loaded = [sem(f"w_loaded{r}") for r in range(R)]
        gathered = [e.kept.enter_context(nc.semaphore(f"gathered{r}")) for r in range(R)]
        scattered = e.kept.enter_context(nc.semaphore("scattered"))
        read_at_ready, add_at_ready, tp_ready, rT_ready, up_ready, silu_ready, act_ready, ta_ready, actT_ready, y_ready, add_ready, w_ready = (
            sem(n) for n in ("read_at", "add_at", "tp", "rT", "up", "silu", "act", "ta", "actT", "y", "add", "w"))

        with nc.Block() as block:
            @block.sync
            def _(sp):
                def load(i, r):
                    sp.dma_start(wu[:, r, :, :], a.L0_up[bass.ds(i * R + r, 1)].rearrange("o (k p) n -> p (o k) n", p=P)).then_inc(w_loaded[r], 16)
                    sp.dma_start(wd[:, r, :], a.L0_down[bass.ds(i * R + r, 1)].rearrange("o p n -> (o p) n")).then_inc(w_loaded[r], 16)

                for r in range(R):
                    load(0, r)
                with sp.Fori(0, BODIES - 1, 1) as i:
                    for r in range(R):
                        sp.wait_ge(y_ready, i * R + r + 1)
                        load(i + 1, r)

            @block.gpsimd
            def _(pool):
                def gather(i, r):
                    nc.gpsimd.tensor_copy(read_at[:, r, :], e.from_token[:, bass.ds(i * R + r, 1)]).then_inc(read_at_ready, 1)
                    pool.wait_ge(read_at_ready, i * R + r + 1)
                    settle(pool)
                    pool.indirect_dma_start(out=rows[:, r, :], out_offset=None, in_=e.table,
                                            in_offset=bass.IndirectOffsetOnAxis(ap=read_at[:, r, :], axis=0)).then_inc(gathered[r], 16)

                def scatter(i, r):
                    nc.gpsimd.tensor_copy(add_at[:, r, :], e.to_token[:, bass.ds(i * R + r, 1)]).then_inc(add_at_ready, 1)
                    pool.wait_ge(add_at_ready, i * R + r + 1)
                    pool.wait_ge(add_ready, i * R + r + 1)
                    pool.wait_ge(scattered, i * R * 16 + r * 16)
                    settle(pool)
                    pool.indirect_dma_start(out=e.x_dram, out_offset=bass.IndirectOffsetOnAxis(ap=add_at[:, r, :], axis=0),
                                            in_=add[:, r, :], in_offset=None, bounds_check=T - 1, oob_is_err=False,
                                            compute_op=ALU.add).then_inc(scattered, 16)

                for r in range(R):
                    gather(0, r)
                with pool.Fori(0, BODIES - 1, 1) as i:
                    for r in range(R):
                        pool.wait_ge(tp_ready, i * R + r + 1)
                        pool.wait_ge(w_ready, i * R + r + 1)
                        gather(i + 1, r)
                        scatter(i, r)
                for r in range(R):
                    scatter(BODIES - 1, r)
                pool.wait_ge(scattered, E0 * 16)

            @block.tensor
            def _(pe):
                def turn(i, r):
                    pe.wait_ge(gathered[r % R], (i + r // R) * 16 + 16)
                    if r >= 2:
                        pe.wait_ge(rT_ready, i * R + r - 1)
                    for k in range(KD):
                        last = nc.tensor.transpose(tp[:, r % 2, k, :], rows[:, r % R, k * P:(k + 1) * P], e.ident[:, :])
                    last.then_inc(tp_ready, 1)

                def products(i, peeled):
                    for r in range(R):
                        pe.wait_ge(rT_ready, i * R + r + 1)
                        pe.wait_ge(w_loaded[r], i * 32 + 32)
                        pe.wait_ge(act_ready, i * R + max(r - 1, 0))
                        for k in range(KD):
                            last = nc.tensor.matmul(up[:, r % 2, :], rT[:, r % 2, k, :], wu[:, r, k, :], start=(k == 0), stop=(k == KD - 1))
                        last.then_inc(up_ready, 1)
                        if r < R - 1 or not peeled:
                            turn(i, r + 1)
                        pe.wait_ge(act_ready, i * R + r + 1)
                        pe.wait_ge(actT_ready, i * R + max(r - 1, 0))
                        nc.tensor.transpose(ta[:, r % 2, :], act_rows[:, r % 2, :], e.ident[:, :]).then_inc(ta_ready, 1)
                        pe.wait_ge(actT_ready, i * R + r + 1)
                        pe.wait_ge(add_ready, i * R + max(r - 1, 0))
                        nc.tensor.matmul(y[:, r % 2, :], actT[:, r % 2, :], wd[:, r, :], start=True, stop=True).then_inc(y_ready, 1)

                turn(0, 0)
                with pe.Fori(0, BODIES - 1, 1) as i:
                    products(i, False)
                products(BODIES - 1, True)

            @block.scalar
            def _(act):
                def row_copy(i, r):
                    act.wait_ge(tp_ready, i * R + r + 1)
                    nc.scalar.activation(rT[:, r % 2, :, :], tp[:, r % 2, :, :], ACT.Copy).then_inc(rT_ready, 1)

                def expert(i, peeled):
                    for r in range(R):
                        act.wait_ge(up_ready, i * R + r + 1)
                        nc.scalar.activation(silu[:, r % 2, :], up[:, r % 2, 0:I0], ACT.Silu).then_inc(silu_ready, 1)
                        if r < R - 1 or not peeled:
                            row_copy(i, r + 1)
                        act.wait_ge(ta_ready, i * R + r + 1)
                        nc.scalar.activation(actT[:, r % 2, :], ta[:, r % 2, :], ACT.Copy).then_inc(actT_ready, 1)

                row_copy(0, 0)
                with act.Fori(0, BODIES - 1, 1) as i:
                    expert(i, False)
                expert(BODIES - 1, True)

            @block.vector
            def _(dve):
                def take_weight(i, r):
                    dve.wait_ge(gathered[r], i * 16 + 16)
                    nc.vector.tensor_copy(w[:, r, :], rows[:, r, bass.ds(i * R + (D + r), 1)]).then_inc(w_ready, 1)

                def experts(i, first):
                    for r in range(R):
                        take_weight(i, r)
                        dve.wait_ge(silu_ready, i * R + r + 1)
                        nc.vector.tensor_tensor(act_rows[:, r % 2, :], silu[:, r % 2, :], up[:, r % 2, I0:2 * I0], ALU.mult).then_inc(act_ready, 1)
                        dve.wait_ge(w_ready, i * R + r + 1)
                        dve.wait_ge(y_ready, i * R + r + 1)
                        if not first:
                            dve.wait_ge(scattered, i * R * 16 + (r + 1 - R) * 16)
                        nc.vector.scalar_tensor_tensor(add[:, r, :], y[:, r % 2, :], w[:, r, :], e.row_gb0[:, :], ALU.mult, ALU.mult).then_inc(add_ready, 1)

                experts(0, True)
                with dve.Fori(1, BODIES, 1) as i:
                    experts(i, False)


def reload_x(nc, e, by_sixteen):
    with nc.semaphore("reloaded%d" % by_sixteen) as reloaded, nc.Block() as block:
        @block.sync
        def _(sp):
            if by_sixteen:
                xv = e.x_dram.rearrange("(g p c) d -> p g c d", p=P, c=HS)
                for g in range(NT // HS):
                    sp.dma_start(e.X[:, g * HS:(g + 1) * HS, :], xv[:, g]).then_inc(reloaded, 16)
                sp.wait_ge(reloaded, 16 * (NT // HS))
            else:
                xv = e.x_dram.rearrange("(c t p) d -> c p t d", t=TPC, p=P)
                for c in range(NC):
                    sp.dma_start(e.X[:, c * TPC:(c + 1) * TPC, :], xv[c]).then_inc(reloaded, 16)
                sp.wait_ge(reloaded, 16 * NC)


def mixed_residual(nc, e):
    with ExitStack() as ctx:
        part = ctx.enter_context(nc.sbuf_tensor("mixed", [P, 2, HS, D], F32))
        scaled = [new_sem(nc, e, f"mix_scaled{g}") for g in range(2)]
        with nc.Block() as block:
            def work(eng, ops, g):
                o = e.O[:, :, :].rearrange("p (j g) (n c) -> p g c n j", g=2, n=H)[:, g]
                for c in range(HS):
                    row = e.row_ga1[:, :].rearrange("p (n j) -> p n j", n=H)
                    ops.tensor_tensor(part[:, g, c, :].rearrange("p (n j) -> p n j", n=H), o[:, c], row, ALU.mult).then_inc(scaled[g], 1)
                eng.wait_ge(scaled[g], HS)
                x = e.X[:, g * HS:(g + 1) * HS, :]
                ops.tensor_tensor(x, x, part[:, g], ALU.add).then_inc(scaled[g], 1)
                eng.wait_ge(scaled[g], HS + 1)

            @block.vector
            def _(dve):
                work(dve, nc.vector, 0)

            @block.gpsimd
            def _(pool):
                work(pool, nc.gpsimd, 1)


def feed_experts(nc, e, a):
    FT = F1 // P
    TILES = 2 * NT + E1
    R = 4
    BODIES = TILES // R
    ROWS = TILES * P
    with ExitStack() as ctx:
        def sb(name, shape, dt=F32):
            return ctx.enter_context(nc.sbuf_tensor(f"fe_{name}", shape, dt))

        def ps(name, shape):
            return ctx.enter_context(nc.psum_tensor(f"fe_{name}", shape, F32))

        def sem(name):
            return new_sem(nc, e, f"fe_{name}")

        w1 = sb("w1", [P, KD, E1, F1])
        w2 = sb("w2", [P, FT, E1, D])
        best, where = sb("best", [P, NT, 8]), sb("where", [P, NT, 8], U32)
        where_f, gap, share = sb("where_f", [P, NT, 2]), sb("gap", [P, NT]), sb("share", [P, NT, 2])
        ids_i, ids = sb("ids_i", [P, ET], I32), sb("ids", [P, ET])
        starts_i, starts = sb("starts_i", [P, NT], I32), sb("starts", [P, NT])
        tile_i, tile_no = sb("tile_i", [P, TILES], I32), sb("tile_no", [P, TILES])
        earlier = sb("earlier", [P, P])
        hit = sb("hit", [P, 2, NT, ET])
        sel = sb("sel", [P, NT, E1])
        tot = sb("tot", [P, NT, E1])
        run = sb("run", [P, 2, NT, E1])
        past = sb("past", [P, E1, NT])
        tiles_e = sb("tiles_e", [P, E1])
        ends = sb("ends", [P, 2, E1])
        base = sb("base", [P, E1])
        pos = sb("pos", [P, NT, E1])
        picked = sb("picked", [P, NT, E1])
        slot, none, dead = sb("slot", [P, 2, NT]), sb("none", [P, 2, NT]), sb("dead", [P, 2, NT])
        keep, zero_w = sb("keep", [P, 2, NT]), sb("zero_w", [P, NT])
        over = sb("over", [P, TILES, E1])
        owner_f, owner = sb("owner_f", [P, TILES]), sb("owner", [P, TILES], I32)
        put_i, get_i = sb("put_i", [P, 2, NT], I32), sb("get_i", [P, 2, NT], I32)
        x_row = sb("x_row", [P, 2 * TPC, D])
        put_at, get_at = sb("put_at", [P, 2 * TPC, 1], I32), sb("get_at", [P, 2 * TPC, 1], I32)
        x_in, xT = sb("x_in", [P, R, D]), sb("xT", [P, 2, KD, P])
        act_rows, aT = sb("act_rows", [P, 2, F1]), sb("aT", [P, 2, FT, P])
        y_sb = sb("y_sb", [P, R, D])
        got = sb("got", [P, 2 * TPC, D])
        mixed = sb("mixed", [P, TPC, D])
        hid, ta, y = ps("hid", [P, 2, F1]), ps("ta", [P, 2, FT, P]), ps("y", [P, 2, CH])
        tp = ps("tp", [P, 2 * KD, P])
        rt = ps("rt", [P, 2, NT, E1])
        w_loaded, made, chain, gap_ready, share_ready, sel_ready, rt_ready = (
            sem(n) for n in ("w_loaded", "made", "chain", "gap", "share", "sel", "rt"))
        lists_ready, put_ready, get_ready, owner_ready, keep_ready = (sem(n) for n in ("lists", "put", "get", "owner", "keep"))
        x_loaded = [sem(f"x_loaded{r}") for r in range(R)]
        y_stored = [sem(f"y_stored{r}") for r in range(R)]
        turned, xT_ready, hid_ready, act_ready, flipped, aT_ready, y_ready, y_saved, part_done, mixed_ready, done, stored = (
            sem(n) for n in ("turned", "xT", "hid", "act", "flipped", "aT", "y", "y_saved", "part", "mixed", "done", "stored"))
        scattered = e.kept.enter_context(nc.semaphore("fe_scattered"))
        fetched = [e.kept.enter_context(nc.semaphore(f"fe_fetched{r}")) for r in range(2 * TPC)]
        out_v = a.out.rearrange("(g p c) d -> p g c d", p=P, c=HS)
        queue = e.queue.rearrange("(n p) d -> n p d", p=P)
        results = e.results.rearrange("(n p) d -> n p d", p=P)

        with nc.Block() as block:
            @block.sync
            def _(sp):
                for k in range(KD):
                    sp.dma_start(w1[:, k, :, :], a.L1_w1[:, k * P:(k + 1) * P, :].rearrange("e p f -> p e f")).then_inc(w_loaded, 16)
                for f in range(FT):
                    sp.dma_start(w2[:, f, :, :], a.L1_w2[:, f * P:(f + 1) * P, :].rearrange("e p d -> p e d")).then_inc(w_loaded, 16)

                def load(i, r):
                    sp.dma_start(x_in[:, r, :], queue[bass.ds(i * R + r, 1)].rearrange("o p d -> (o p) d")).then_inc(x_loaded[r], 16)

                def store(i, r):
                    sp.wait_ge(y_saved, i * R + r + 1)
                    sp.dma_start(results[bass.ds(i * R + r, 1)].rearrange("o p d -> (o p) d"), y_sb[:, r, :]).then_inc(y_stored[r], 16)

                sp.wait_ge(scattered, 2 * NT * 16)
                for r in range(R):
                    load(0, r)
                with sp.Fori(0, BODIES - 1, 1) as i:
                    for r in range(R):
                        sp.wait_ge(turned, i * R + r + 1)
                        load(i + 1, r)
                        store(i, r)
                for r in range(R):
                    store(BODIES - 1, r)
                for c in range(NT // TPC):
                    g, t = (c * TPC) // HS, (c * TPC) % HS
                    sp.wait_ge(done, c + 1)
                    sp.dma_start(out_v[:, g, t:t + TPC, :], e.X[:, c * TPC:(c + 1) * TPC, :]).then_inc(stored, 16)
                sp.wait_ge(stored, 16 * (NT // TPC))

            @block.gpsimd
            def _(pool):
                nc.gpsimd.iota(ids_i[:, :], [[1, ET]], base=0, channel_multiplier=0).then_inc(made, 1)
                nc.gpsimd.iota(starts_i[:, :], [[P, NT]], base=0, channel_multiplier=0).then_inc(made, 1)
                nc.gpsimd.iota(tile_i[:, :], [[1, TILES]], base=0, channel_multiplier=0).then_inc(made, 1)
                nc.gpsimd.memset(earlier[:, :], 1.0).then_inc(made, 1)
                pool.wait_ge(made, 4)
                nc.gpsimd.affine_select(out=earlier[:, :], in_=earlier[:, :], compare_op=ALU.is_gt, fill=0.0,
                                        base=0, pattern=[[1, P]], channel_multiplier=-1).then_inc(made, 1)
                pool.wait_ge(lists_ready, 1)
                with pool.Fori(0, NC, 1) as i:
                    for r in range(2 * TPC):
                        nc.gpsimd.tensor_copy(put_at[:, r, :], put_i[:, r % 2, bass.ds(i * TPC + r // 2, 1)]).then_inc(put_ready, 1)
                        nc.gpsimd.tensor_copy(x_row[:, r, :], e.H[:, bass.ds(i * TPC + r // 2, 1), :].rearrange("p o d -> p (o d)")).then_inc(put_ready, 1)
                        pool.wait_ge(put_ready, i * 4 * TPC + 2 * r + 2)
                        settle(pool)
                        pool.indirect_dma_start(out=e.queue, out_offset=bass.IndirectOffsetOnAxis(ap=put_at[:, r, :], axis=0),
                                                in_=x_row[:, r, :], in_offset=None, bounds_check=ROWS - 1, oob_is_err=False).then_inc(scattered, 16)
                    pool.wait_ge(scattered, i * 2 * TPC * 16 + 2 * TPC * 16)

                for s in y_stored:
                    pool.wait_ge(s, 16 * BODIES)

                def fetch(i, r):
                    nc.gpsimd.tensor_copy(get_at[:, r, :], get_i[:, r % 2, bass.ds(i * TPC + r // 2, 1)]).then_inc(get_ready, 1)
                    pool.wait_ge(get_ready, i * 2 * TPC + r + 1)
                    settle(pool)
                    pool.indirect_dma_start(out=got[:, r, :], out_offset=None, in_=e.results,
                                            in_offset=bass.IndirectOffsetOnAxis(ap=get_at[:, r, :], axis=0)).then_inc(fetched[r], 16)

                for r in range(2 * TPC):
                    fetch(0, r)
                with pool.Fori(1, NC, 1) as i:
                    for r in range(2 * TPC):
                        pool.wait_ge(part_done, i * 2 * TPC - 2 * TPC + r + 1)
                        fetch(i, r)

            @block.vector
            def _(dve):
                n = [0]

                def link(ins):
                    n[0] += 1
                    ins.then_inc(chain, 1)
                    dve.wait_ge(chain, n[0])

                def all_of(instructions):
                    for ins in instructions:
                        ins.then_inc(chain, 1)
                        n[0] += 1
                    dve.wait_ge(chain, n[0])

                tt, flat2 = nc.vector.tensor_tensor, lambda ap: ap.rearrange("p (o n) -> p o n", o=1)
                dve.wait_ge(made, 5)
                link(nc.vector.tensor_copy(ids[:, :], ids_i[:, :]))
                link(nc.vector.tensor_copy(starts[:, :], starts_i[:, :]))
                link(nc.vector.tensor_copy(tile_no[:, :], tile_i[:, :]))
                all_of([nc.vector.max(best[:, t, :], e.logits[:, t, :]) for t in range(NT)])
                all_of([nc.vector.max_index(where[:, t, :], best[:, t, :], e.logits[:, t, :]) for t in range(NT)])
                tt(gap[:, :], best[:, :, 0], best[:, :, 1], ALU.subtract).then_inc(gap_ready, 1)
                link(nc.vector.tensor_copy(where_f[:, :, :], where[:, :, 0:2]))
                for k in range(2):
                    link(tt(hit[:, k, :, :], flat2(ids[:, :]).to_broadcast([P, NT, ET]),
                            where_f[:, :, k:k + 1].to_broadcast([P, NT, ET]), ALU.is_equal))
                tt(sel[:, :, :], hit[:, 0, :, 0:E1], hit[:, 1, :, 0:E1], ALU.add).then_inc(sel_ready, 1)
                dve.wait_ge(rt_ready, 1)
                link(nc.vector.tensor_copy(tot[:, :, :], rt[:, 1, :, :]))
                src, step = tot[:, :, :], 1
                for s in range(5):
                    dst = run[:, s % 2, :, :]
                    all_of([nc.vector.tensor_copy(dst[:, 0:step, :], src[:, 0:step, :]),
                            tt(dst[:, step:NT, :], src[:, step:NT, :], src[:, 0:NT - step, :], ALU.add)])
                    src, step = dst, step * 2
                assert step == NT
                link(tt(past[:, :, :], src[:, NT - 1:NT, :].rearrange("p o (e q) -> p (o e) q", q=1).to_broadcast([P, E1, NT]),
                        flat2(starts[:, :]).to_broadcast([P, E1, NT]), ALU.is_gt))
                link(nc.vector.tensor_reduce(tiles_e[:, :], past[:, :, :], AX.X, ALU.add))
                before, step = tiles_e[:, :], 1
                for s in range(3):
                    dst = ends[:, s % 2, :]
                    all_of([nc.vector.tensor_copy(dst[:, 0:step], before[:, 0:step]),
                            tt(dst[:, step:E1], before[:, step:E1], before[:, 0:E1 - step], ALU.add)])
                    before, step = dst, step * 2
                assert step == E1
                link(tt(base[:, :], before, tiles_e[:, :], ALU.subtract))
                link(nc.vector.tensor_scalar(base[:, :], base[:, :], float(P), None, ALU.mult))
                link(tt(pos[:, :, :], src, tot[:, :, :], ALU.subtract))
                link(tt(pos[:, :, :], rt[:, 0, :, :], pos[:, :, :], ALU.add))
                link(tt(pos[:, :, :], pos[:, :, :], flat2(base[:, :]).to_broadcast([P, NT, E1]), ALU.add))
                for k in range(2):
                    link(tt(picked[:, :, :], hit[:, k, :, 0:E1], pos[:, :, :], ALU.mult))
                    link(nc.vector.tensor_reduce(slot[:, k, :], picked[:, :, :], AX.X, ALU.add))
                    link(nc.vector.tensor_reduce(none[:, k, :], hit[:, k, :, E1:ET], AX.X, ALU.add))
                link(nc.vector.scalar_tensor_tensor(dead[:, :, :], none[:, :, :], float(ROWS), slot[:, :, :], ALU.mult, ALU.add))
                link(nc.vector.tensor_copy(get_i[:, :, :], slot[:, :, :]))
                nc.vector.tensor_copy(put_i[:, :, :], dead[:, :, :]).then_inc(lists_ready, 1)
                link(tt(over[:, :, :], flat2(before).to_broadcast([P, TILES, E1]),
                        tile_no[:, :].rearrange("p (t o) -> p t o", o=1).to_broadcast([P, TILES, E1]), ALU.is_le))
                link(nc.vector.tensor_reduce(owner_f[:, :], over[:, :, :], AX.X, ALU.add))
                link(nc.vector.tensor_scalar(owner_f[:, :], owner_f[:, :], float(E1 - 1), None, ALU.min))
                nc.vector.tensor_copy(owner[:, :], owner_f[:, :]).then_inc(owner_ready, 1)
                dve.wait_ge(share_ready, 2)
                link(nc.vector.tensor_scalar(share[:, :, :], share[:, :, :], 0.5, 0.5, ALU.mult, ALU.add))
                share_k = share[:, :, :].rearrange("p t k -> p k t")
                link(tt(none[:, :, :], share_k, none[:, :, :], ALU.mult))
                link(tt(keep[:, :, :], share_k, none[:, :, :], ALU.subtract))
                link(tt(zero_w[:, :], none[:, 0, :], none[:, 1, :], ALU.add))
                gbw = flat2(e.row_gb1[:, :]).to_broadcast([P, TPC, D])
                for c in range(NC):
                    all_of([nc.vector.scalar_tensor_tensor(mixed[:, t, :], e.H[:, c * TPC + t, :], zero_w[:, c * TPC + t:c * TPC + t + 1],
                                                           e.row_gb1[:, :], ALU.mult, ALU.mult) for t in range(TPC)])
                    x = e.X[:, c * TPC:(c + 1) * TPC, :]
                    link(tt(x, x, mixed[:, :, :], ALU.add))

                def flip_copy(i, r):
                    dve.wait_ge(flipped, i * R + r + 1)
                    nc.vector.tensor_copy(aT[:, r % 2, :, :], ta[:, r % 2, :, :]).then_inc(aT_ready, 1)

                def save(i, r, first):
                    dve.wait_ge(y_ready, i * R + r + 1)
                    if not first:
                        dve.wait_ge(y_stored[r], i * 16)
                    nc.vector.tensor_copy(y_sb[:, r, :], y[:, r % 2, 0:D]).then_inc(y_saved, 1)

                def tiles(i, first):
                    for r in range(R):
                        flip_copy(i, r)
                        save(i, r, first)

                tiles(0, True)
                with dve.Fori(1, BODIES, 1) as i:
                    tiles(i, False)

                with dve.Fori(0, NC, 1) as i:
                    for t in range(TPC):
                        dve.wait_ge(fetched[2 * t], i * 16 + 16)
                        nc.vector.tensor_scalar(mixed[:, t, :], got[:, 2 * t, :], keep[:, 0, bass.ds(i * TPC + t, 1)], None, ALU.mult).then_inc(part_done, 1)
                        dve.wait_ge(fetched[2 * t + 1], i * 16 + 16)
                        dve.wait_ge(part_done, i * 2 * TPC + 2 * t + 1)
                        nc.vector.scalar_tensor_tensor(mixed[:, t, :], got[:, 2 * t + 1, :], keep[:, 1, bass.ds(i * TPC + t, 1)], mixed[:, t, :],
                                                       ALU.mult, ALU.add).then_inc(part_done, 1)
                    dve.wait_ge(part_done, i * 2 * TPC + 2 * TPC)
                    nc.vector.tensor_tensor(mixed[:, :, :], mixed[:, :, :], gbw, ALU.mult).then_inc(mixed_ready, 1)
                    dve.wait_ge(mixed_ready, i + 1)
                    x = e.X[:, bass.ds(i * TPC, TPC), :]
                    nc.vector.tensor_tensor(x, x, mixed[:, :, :], ALU.add).then_inc(done, 1)
                    dve.wait_ge(done, i + 1)

            @block.scalar
            def _(act):
                act.wait_ge(gap_ready, 1)
                nc.scalar.activation(share[:, :, 0], gap[:, :], ACT.Tanh, scale=0.5).then_inc(share_ready, 1)
                nc.scalar.activation(share[:, :, 1], gap[:, :], ACT.Tanh, scale=-0.5).then_inc(share_ready, 1)

                def row_copy(i, r):
                    act.wait_ge(turned, i * R + r + 1)
                    nc.scalar.activation(xT[:, r % 2, :, :], tp[:, 0:KD, :], ACT.Copy).then_inc(xT_ready, 1)

                def tiles(i, last):
                    for r in range(R):
                        act.wait_ge(hid_ready, i * R + r + 1)
                        nc.scalar.activation(act_rows[:, r % 2, :], hid[:, r % 2, :], ACT.Silu).then_inc(act_ready, 1)
                        if r < R - 1 or not last:
                            row_copy(i, r + 1)

                row_copy(0, 0)
                with act.Fori(0, BODIES - 1, 1) as i:
                    tiles(i, False)
                tiles(BODIES - 1, True)

            @block.tensor
            def _(pe):
                pe.wait_ge(sel_ready, 1)
                sel_flat = sel[:, :, :].rearrange("p t e -> p (t e)")
                nc.tensor.matmul(rt[:, 0, :, :].rearrange("p t e -> p (t e)"), earlier[:, :], sel_flat, start=True, stop=True)
                nc.tensor.matmul(rt[:, 1, :, :].rearrange("p t e -> p (t e)"), e.ones[:, :], sel_flat, start=True, stop=True).then_inc(rt_ready, 1)
                pe.wait_ge(owner_ready, 1)
                pe.wait_ge(w_loaded, 16 * (KD + FT))

                def expert_of(i, r):
                    return pe.value_load(owner[0:1, bass.ds(i * R + r, 1)], min_val=0, max_val=E1 - 1)

                def turn(i, r):
                    pe.wait_ge(x_loaded[r % R], (i + r // R) * 16 + 16)
                    if r:
                        pe.wait_ge(xT_ready, i * R + r)
                    for k in range(KD):
                        last = nc.tensor.transpose(tp[:, k, :], x_in[:, r % R, k * P:(k + 1) * P], e.ident[:, :])
                    last.then_inc(turned, 1)

                def hidden(i, r, ex):
                    pe.wait_ge(xT_ready, i * R + r + 1)
                    for k in range(KD):
                        last = nc.tensor.matmul(hid[:, r % 2, :], xT[:, r % 2, k, :], w1[:, k, bass.ds(ex, 1), :].rearrange("p o f -> p (o f)"),
                                                start=(k == 0), stop=(k == KD - 1))
                    last.then_inc(hid_ready, 1)

                def flip(i, r):
                    pe.wait_ge(act_ready, i * R + r + 1)
                    for f in range(FT):
                        last = nc.tensor.transpose(ta[:, r % 2, f, :], act_rows[:, r % 2, f * P:(f + 1) * P], e.ident[:, :])
                    last.then_inc(flipped, 1)

                def down(i, r, ex):
                    pe.wait_ge(aT_ready, i * R + r + 1)
                    if r >= 2 or not isinstance(i, int) or i:
                        pe.wait_ge(y_saved, i * R + r - 1)
                    for f in range(FT):
                        last = nc.tensor.matmul(y[:, r % 2, 0:D], aT[:, r % 2, f, :], w2[:, f, bass.ds(ex, 1), :].rearrange("p o d -> p (o d)"),
                                                start=(f == 0), stop=(f == FT - 1))
                    last.then_inc(y_ready, 1)

                def tiles(i, first, last):
                    for r in range(R):
                        hidden(i, r, expert_of(i, r))
                        if r < R - 1 or not last:
                            turn(i, r + 1)
                        if r or not first:
                            if r:
                                down(i, r - 1, expert_of(i, r - 1))
                            else:
                                down(i - 1, R - 1, expert_of(i - 1, R - 1))
                        flip(i, r)

                turn(0, 0)
                tiles(0, True, False)
                with pe.Fori(1, BODIES - 1, 1) as i:
                    tiles(i, False, False)
                tiles(BODIES - 1, False, True)
                down(BODIES - 1, R - 1, expert_of(BODIES - 1, R - 1))


def program(nc, a, stop=99):
    e = Env()
    with ExitStack() as ctx:
        e.layer = ctx.enter_context(ExitStack())
        e.sems = []
        e.kept = ctx

        def sb(name, shape, dt=F32):
            return ctx.enter_context(nc.sbuf_tensor(name, shape, dt))

        def dram(name, shape, dt=F32):
            return nc.dram_tensor(name, shape, dt, kind="Internal").ap()

        e.X = sb("X", [P, NT, D])
        e.ident, e.ident_b = sb("ident", [P, P]), sb("ident_b", [P, P], BF16)
        e.ones, e.sum4 = sb("ones", [P, P]), sb("sum4", [P, VC])
        e.mask_k, e.mask_q = sb("mask_k", [P, P], BF16), sb("mask_q", [P, CH + P], BF16)
        e.col, e.bias_qk = sb("col", [P, 24]), sb("bias_qk", [P, 4])
        e.row_ga0, e.row_gb0, e.row_sb0, e.row_cb0 = (sb(f"row_{n}", [P, D]) for n in ("ga0", "gb0", "sb0", "cb0"))
        e.row_ga1, e.row_gb1, e.row_sb1, e.row_cb1 = (sb(f"row_{n}", [P, D]) for n in ("ga1", "gb1", "sb1", "cb1"))
        e.w_out0, e.b_out0 = sb("w_out0", [P, KD, D]), sb("b_out0", [1, D])
        e.bn6, e.mv = sb("bn6", [P, NT, 6]), sb("mv", [P, NT, 2])
        e.var, e.root, e.rstd, e.newt = (sb(n, [P, NT]) for n in ("var", "root", "rstd", "newt"))
        e.q_dram, e.k_dram = dram("q_parts", (PARTS, D, T), BF16), dram("k_parts", (PARTS, D, T), BF16)
        e.table, e.x_dram = dram("table", (T, ROW0)), dram("x_after", (T, D))
        e.queue, e.results = dram("queue", ((2 * NT + E1) * P, D)), dram("results", ((2 * NT + E1) * P, D))
        e.q_heads = e.q_dram.rearrange("s (h r) t -> s h r t", r=HS)
        e.k_heads = e.k_dram.rearrange("s (h r) t -> s h r t", r=HS)

        setup(nc, e, a)
        with ExitStack() as att:
            e.V = att.enter_context(nc.sbuf_tensor("V", [P, H, NT, HS], F32))
            e.O = att.enter_context(nc.sbuf_tensor("O", [P, NT, D], F32))
            project(nc, e, 0, a.L0_w_qkv, a.L0_b_qkv[2:3, :])
            if stop > 1:
                attention(nc, e, 0)
            if stop <= 2:
                dump(nc, e, a, e.O if stop == 2 else None)
                return
            project_out(nc, e)
        if stop == 3:
            return dump(nc, e, a, e.X)
        with ExitStack() as ffn:
            e.hT = ffn.enter_context(nc.sbuf_tensor("hT_0", [P, KD, T], F32))
            e.logits = ffn.enter_context(nc.sbuf_tensor("logits_0", [P, NT, E0 + 1], F32))
            e.chosen = ffn.enter_context(nc.sbuf_tensor("chosen", [P, NT, E0], F32))
            e.order = ffn.enter_context(nc.sbuf_tensor("order", [P, T // 2], F32))
            e.from_token = ffn.enter_context(nc.sbuf_tensor("from_token", [P, E0], I32))
            e.to_token = ffn.enter_context(nc.sbuf_tensor("to_token", [P, E0], I32))
            feed_norm(nc, e, 0, a.L0_gate_w, None, E0 + 1)
            shared_expert(nc, e, a)
            if stop == 4:
                return dump(nc, e, a, e.X)
            routed_experts(nc, e, a)
        recycle_semaphores(nc, e)
        reload_x(nc, e, False)
        if stop == 5:
            return dump(nc, e, a, e.X)
        with ExitStack() as att:
            e.V = att.enter_context(nc.sbuf_tensor("V1", [P, H, NT, HS], F32))
            e.O = att.enter_context(nc.sbuf_tensor("O1", [P, NT, D], F32))
            project(nc, e, 1, a.L1_w_qkv, None)
            attention(nc, e, 1)
            reload_x(nc, e, True)
            mixed_residual(nc, e)
        if stop == 6:
            return dump(nc, e, a, e.X, True)
        with ExitStack() as ffn:
            e.H = ffn.enter_context(nc.sbuf_tensor("H_1", [P, NT, D], F32))
            e.logits = ffn.enter_context(nc.sbuf_tensor("logits_1", [P, NT, ET], F32))
            feed_norm(nc, e, 1, a.L1_gate_w, a.L1_bias, ET)
            feed_experts(nc, e, a)


def dump(nc, e, a, src, by_sixteen=False):
    with nc.semaphore("dumped") as dumped, nc.Block() as block:
        @block.sync
        def _(sp):
            if src is None:
                sp.dma_start(a.out.rearrange("(t p) (h c) -> p h t c", p=P, h=H)[:, 0], e.V[:, 0]).then_inc(dumped, 16)
            elif by_sixteen:
                for g in range(2):
                    sp.dma_start(a.out.rearrange("(g p c) d -> p g c d", p=P, c=HS)[:, g], src[:, g * HS:(g + 1) * HS, :]).then_inc(dumped, 16)
                sp.wait_ge(dumped, 32)
            else:
                sp.dma_start(a.out.rearrange("(t p) d -> p t d", p=P), src[:, :, :]).then_inc(dumped, 16)
            sp.wait_ge(dumped, 16)


def lay_out(x):
    def qkv_heads(w):
        return np.ascontiguousarray(w.reshape(-1, H, 3, HS).transpose(0, 2, 1, 3).reshape(-1, 3, D))

    return {
        "x": np.ascontiguousarray(x["L0_attn_encodings"][0]),
        "L0_w_qkv": qkv_heads(x["L0_attn_attn_W"]),
        "L0_b_qkv": qkv_heads(x["L0_attn_attn_b"].reshape(1, -1))[0],
        "L0_out_W": x["L0_attn_out_W"], "L0_out_b": x["L0_attn_out_b"].reshape(1, D),
        "L0_gate_w": np.concatenate([x["L0_ffn_gate_w"], x["L0_ffn_shared_gate_w"]], axis=1),
        "L0_shared_up": x["L0_ffn_shared_gate_up_w"], "L0_shared_down": x["L0_ffn_shared_down_w"],
        "L0_up": x["L0_ffn_expert_gate_up_w"], "L0_down": x["L0_ffn_expert_down_w"],
        "L0_c": x["L0_c"], "L0_wmod": x["L0_wmod"],
        "L1_w_qkv": qkv_heads(np.ascontiguousarray(x["L1_attn_W_qkv"].transpose(1, 0, 2)).reshape(D, -1)),
        "L1_W_out": x["L1_attn_W_out"].reshape(D, D),
        "L1_gate_w": np.ascontiguousarray(x["L1_ffn_gate_w"].T), "L1_bias": x["L1_ffn_expert_bias"].reshape(1, ET),
        "L1_w1": np.ascontiguousarray(x["L1_ffn_w1"].transpose(0, 2, 1)),
        "L1_w2": np.ascontiguousarray(x["L1_ffn_w2"].transpose(0, 2, 1)),
        "L1_c": x["L1_c"], "L1_wmod": x["L1_wmod"],
    }


class Arguments:
    pass


def kernel(**inputs):
    import numpy as _np
    import concourse.bacc as _bacc
    from concourse import mybir as _mybir
    from concourse.bass_utils import run_bass_kernel_spmd as _run

    nc = _bacc.Bacc("TRN2", target_bir_lowering=False, num_devices=1)
    arrays = {f"in_{k}": _np.ascontiguousarray(v) for k, v in lay_out({k: _np.asarray(v) for k, v in inputs.items()}).items()}
    a = Arguments()
    a.__dict__.update({k[3:]: nc.dram_tensor(k, v.shape, _mybir.dt.from_np(v.dtype), kind="ExternalInput").ap()
                       for k, v in arrays.items()})
    a.out = nc.dram_tensor("out_0", (T, D), F32, kind="ExternalOutput").ap()
    program(nc, a)
    r = _run(nc, [arrays], core_ids=[0])
    return r.results[0]["out_0"].reshape(1, T, D)
```

```python
import concourse.bass as bass
import numpy as np
from concourse import mybir
from contextlib import ExitStack

F32 = mybir.dt.float32
BF16 = mybir.dt.bfloat16
I32 = mybir.dt.int32
U32 = mybir.dt.uint32
ALU = mybir.AluOpType
ACT = mybir.ActivationFunctionType
AX = mybir.AxisListType

P = 128
T = 4096
D = 256
KD = D // P
NT = T // P
CH = 512
NC = T // CH
TPC = CH // P
H = 16
HS = D // H
EPS = 1e-5
MASKED = -1e30
PARTS = 3
PAIRS = [(0, 0), (1, 0), (2, 0), (0, 1), (1, 1), (0, 2)]
SR = len(PAIRS) * HS
MR = SR + PARTS
VC = 32
QUADS = NC * (NC + 1) // 2
LOOK = 12
SLOTS = 2 * QUADS
RING = 3
E0, I0, CAP, TOPK = 64, 128, 128, 8
IS = 512
ROW0 = D + E0
E1, EZ, F1 = 8, 4, 512
ET = E1 + EZ


class Env:
    pass


def new_sem(nc, e, name):
    e.sems.append(e.layer.enter_context(nc.semaphore(name)))
    return e.sems[-1]


def recycle_semaphores(nc, e):
    with nc.Block() as block:
        @block.sync
        def _(sp):
            for s in e.sems:
                sp.sem_clear(s)
    e.layer.close()
    e.sems = []


def settle(eng):
    eng.nop(nofuse=True)


def past(eng, sem, value):
    if not isinstance(value, int) or value > 0:
        eng.wait_ge(sem, value)


def flat(ap):
    return ap.rearrange("p o d -> p (o d)")


def setup(nc, e, a):
    with ExitStack() as ctx:
        def sb(name, shape, dt=F32):
            return ctx.enter_context(nc.sbuf_tensor(name, shape, dt))

        def sem(name):
            return new_sem(nc, e, name)

        wmod = sb("wmod", [P, 2, KD, 6 * D])
        c_col = sb("c_col", [P, 2, KD])
        c_silu = sb("c_silu", [P, 2, KD])
        c_rep = sb("c_rep", [P, 2, KD, P])
        w_out1 = sb("w_out1", [P, KD, D])
        w_out0_raw = sb("w_out0_raw", [P, KD, D])
        b_out0_raw = sb("b_out0_raw", [1, D])
        guard = sb("guard", [P, 2, D])
        rows = ctx.enter_context(nc.psum_tensor("rows", [P, 10, D], F32))
        cols = ctx.enter_context(nc.psum_tensor("cols", [P, 32], F32))
        small_loaded, wmod_loaded = sem("small_loaded"), sem("wmod_loaded")
        e.x_loaded = [sem(f"x_loaded{c}") for c in range(NC)]
        pool_step, const_made = sem("pool_step"), sem("const_made")
        silu_done, rep_done, mod_done = sem("silu_done"), sem("rep_done"), sem("mod_done")
        step = sem("setup_step")
        NS = 11

        with nc.Block() as block:
            @block.sync
            def _(sp):
                for l, c in enumerate((a.L0_c, a.L1_c)):
                    for k in range(KD):
                        sp.dma_start(c_col[:, l, k:k + 1], c[0:1, k * P:(k + 1) * P].rearrange("o p -> p o")).then_inc(small_loaded, 16)
                sp.dma_start(b_out0_raw[:, :], a.L0_out_b).then_inc(small_loaded, 16)
                sp.dma_start(w_out0_raw[:, :, :], a.L0_out_W.rearrange("(k p) n -> p k n", p=P)).then_inc(small_loaded, 16)
                sp.dma_start(w_out1[:, :, :], a.L1_W_out.rearrange("(k p) n -> p k n", p=P)).then_inc(small_loaded, 16)
                for s in range(2):
                    for g in range(KD):
                        sp.dma_start(e.bias_qk[:, 2 * s + g:2 * s + g + 1],
                                     a.L0_b_qkv[s:s + 1, g * P:(g + 1) * P].rearrange("o p -> p o")).then_inc(small_loaded, 16)
                for l, w in enumerate((a.L0_wmod, a.L1_wmod)):
                    sp.dma_start(wmod[:, l, :, :], w.rearrange("(k p) n -> p k n", p=P)).then_inc(wmod_loaded, 16)
                xv = a.x.rearrange("(c t p) d -> c p t d", t=TPC, p=P)
                for c in range(NC):
                    sp.dma_start(e.X[:, c * TPC:(c + 1) * TPC, :], xv[c]).then_inc(e.x_loaded[c], 16)

            @block.gpsimd
            def _(pool):
                nc.gpsimd.memset(e.ident[:, :], 0.0).then_inc(pool_step, 1)
                nc.gpsimd.memset(e.mask_k[:, :], 0.0).then_inc(pool_step, 1)
                nc.gpsimd.memset(e.mask_q[:, 0:CH], MASKED).then_inc(pool_step, 1)
                nc.gpsimd.memset(e.mask_q[:, CH:CH + P], 0.0).then_inc(pool_step, 1)
                nc.gpsimd.memset(e.ones[:, :], 1.0).then_inc(pool_step, 1)
                pool.wait_ge(pool_step, 5)
                nc.gpsimd.affine_select(out=e.ident[:, :], in_=e.ident[:, :], compare_op=ALU.not_equal, fill=1.0,
                                        base=0, pattern=[[-1, P]], channel_multiplier=1).then_inc(const_made, 1)
                nc.gpsimd.affine_select(out=e.mask_k[:, :], in_=e.mask_k[:, :], compare_op=ALU.is_ge, fill=MASKED,
                                        base=0, pattern=[[-1, P]], channel_multiplier=1).then_inc(const_made, 1)
                nc.gpsimd.affine_select(out=e.mask_q[:, CH:CH + P], in_=e.mask_q[:, CH:CH + P], compare_op=ALU.is_ge,
                                        fill=MASKED, base=0, pattern=[[1, P]], channel_multiplier=-1).then_inc(const_made, 1)
                pool.wait_ge(const_made, 3)
                nc.gpsimd.tensor_copy(e.ident_b[:, :], e.ident[:, :]).then_inc(const_made, 1)

            @block.scalar
            def _(act):
                act.wait_ge(small_loaded, 16 * NS)
                nc.scalar.activation(c_silu[:, :, :], c_col[:, :, :], ACT.Silu).then_inc(silu_done, 1)

            @block.vector
            def _(dve):
                n = [0]

                def link(ins):
                    n[0] += 1
                    ins.then_inc(step, 1)
                    dve.wait_ge(step, n[0])

                dve.wait_ge(silu_done, 1)
                dve.wait_ge(pool_step, 5)
                for l in range(2):
                    for k in range(KD):
                        nc.vector.tensor_scalar(c_rep[:, l, k, :], e.ones[:, :], c_silu[:, l, k:k + 1], None, ALU.mult).then_inc(rep_done, 1)
                dve.wait_ge(mod_done, 1)
                nc.vector.tensor_scalar(e.bias_qk[:, 0:KD], e.bias_qk[:, 0:KD], HS ** -0.5, None, ALU.mult)
                link(nc.vector.tensor_copy(e.col[:, :], cols[:, 0:24]))
                for l in range(2):
                    for w in (1, 4):
                        j = (l * 6 + w) * KD
                        link(nc.vector.tensor_scalar(e.col[:, j:j + KD], e.col[:, j:j + KD], 1.0, None, ALU.add))
                nc.vector.tensor_copy(e.row_sb0[:, :], rows[:, 2, :])
                nc.vector.tensor_scalar(e.row_cb0[:, :], rows[:, 3, :], 1.0, None, ALU.add)
                nc.vector.tensor_copy(e.row_sb1[:, :], rows[:, 6, :])
                nc.vector.tensor_scalar(e.row_cb1[:, :], rows[:, 7, :], 1.0, None, ALU.add)
                for src, dst in ((0, e.row_ga0), (1, e.row_gb0), (4, e.row_ga1), (5, e.row_gb1)):
                    link(nc.vector.tensor_scalar(guard[:, 1, :], rows[:, src, :], 0.0, 2.0, ALU.is_ge, ALU.mult))
                    link(nc.vector.tensor_scalar(guard[:, 1, :], guard[:, 1, :], 1.0, None, ALU.subtract))
                    link(nc.vector.tensor_tensor(guard[:, 0, :], guard[:, 1, :], rows[:, src, :], ALU.mult))
                    link(nc.vector.tensor_scalar(guard[:, 0, :], guard[:, 0, :], 0.25, None, ALU.max))
                    link(nc.vector.tensor_tensor(dst[:, :], guard[:, 0, :], guard[:, 1, :], ALU.mult))
                link(nc.vector.tensor_tensor(e.row_ga1[:, :], e.row_ga1[:, :], rows[:, 8, :], ALU.mult))
                for k in range(KD):
                    nc.vector.tensor_tensor(e.w_out0[:, k, :], w_out0_raw[:, k, :], e.row_ga0[:, :], ALU.mult)
                link(nc.vector.tensor_tensor(e.b_out0[:, :], b_out0_raw[:, :], e.row_ga0[0:1, :], ALU.mult))

            @block.tensor
            def _(pe):
                pe.wait_ge(wmod_loaded, 32)
                pe.wait_ge(silu_done, 1)
                for l in range(2):
                    for w in range(6):
                        for g in range(KD):
                            j = (l * 6 + w) * KD + g
                            for k in range(KD):
                                nc.tensor.matmul(cols[:, j:j + 1], wmod[:, l, k, w * D + g * P:w * D + (g + 1) * P],
                                                 c_silu[:, l, k:k + 1], start=(k == 0), stop=(k == KD - 1))
                pe.wait_ge(rep_done, 2 * KD)
                for j, (l, w) in enumerate(((0, 2), (0, 5), (0, 3), (0, 4), (1, 2), (1, 5), (1, 3), (1, 4))):
                    for k in range(KD):
                        nc.tensor.matmul(rows[:, j, :], c_rep[:, l, k, :], wmod[:, l, k, w * D:(w + 1) * D],
                                         start=(k == 0), stop=(k == KD - 1))
                for k in range(KD):
                    last = nc.tensor.matmul(rows[:, 8, :], e.ones[:, :], w_out1[:, k, :], start=(k == 0), stop=(k == KD - 1))
                last.then_inc(mod_done, 1)


def norm_stats(nc, e, dve, tag, step, stats_ready, root_done, src):
    n = 0
    for t in range(NT):
        nc.vector.bn_stats(e.bn6[:, t, :], src(t)).then_inc(step, 1)
    n += NT
    dve.wait_ge(step, n)
    for t in range(NT):
        nc.vector.bn_aggr(e.mv[:, t, :], e.bn6[:, t, :]).then_inc(step, 1)
    n += NT
    dve.wait_ge(step, n)
    nc.vector.tensor_scalar(e.var[:, :], e.mv[:, :, 1], EPS, None, ALU.add).then_inc(stats_ready, 1)
    dve.wait_ge(root_done, 1)
    nc.vector.reciprocal(e.rstd[:, :], e.root[:, :]).then_inc(step, 1)
    dve.wait_ge(step, n + 1)
    nc.vector.tensor_tensor(e.newt[:, :], e.rstd[:, :], e.rstd[:, :], ALU.mult).then_inc(step, 1)
    dve.wait_ge(step, n + 2)
    nc.vector.tensor_tensor(e.newt[:, :], e.newt[:, :], e.var[:, :], ALU.mult).then_inc(step, 1)
    dve.wait_ge(step, n + 3)
    nc.vector.tensor_scalar(e.newt[:, :], e.newt[:, :], -0.5, 1.5, ALU.mult, ALU.add).then_inc(step, 1)
    dve.wait_ge(step, n + 4)
    nc.vector.tensor_tensor(e.rstd[:, :], e.rstd[:, :], e.newt[:, :], ALU.mult).then_inc(step, 1)
    dve.wait_ge(step, n + 5)
    return n + 5


def project(nc, e, l, w_qkv, bias_v):
    with ExitStack() as ctx:
        def sb(name, shape, dt=F32):
            return ctx.enter_context(nc.sbuf_tensor(f"{name}{l}", shape, dt))

        def ps(name, shape):
            return ctx.enter_context(nc.psum_tensor(f"{name}{l}", shape, F32))

        def sem(name):
            return new_sem(nc, e, f"pr{l}_{name}")

        w = sb("w_qkv", [P, 3, KD, D])
        bv = sb("bv", [P, D])
        xn = sb("xn", [P, 2, TPC, D])
        hT = sb("hT", [P, 2, KD, CH])
        t32 = sb("t32", [P, 2, CH])
        rest = sb("rest", [P, 4, CH])
        part = sb("part", [P, 4, PARTS, CH], BF16)
        tp = ps("tp", [P, KD, CH])
        qk = ps("qk", [P, 2, CH])
        vp = ps("vp", [P, 2, TPC // 2, D])
        w_loaded, step, stats_ready, root_done = sem("w_loaded"), sem("step"), sem("stats"), sem("root")
        if l == 1:
            e.x_loaded = [sem(f"x_loaded{c}") for c in range(NC)]
        xn_ready, tp_ready, hT_ready = sem("xn_ready"), sem("tp_ready"), sem("hT_ready")
        qk_ready, t32_ready, first_ready, rest_ready = sem("qk_ready"), sem("t32_ready"), sem("first_ready"), sem("rest_ready")
        second_ready, third_ready = sem("second_ready"), sem("third_ready")
        v_ready, v_taken = sem("v_ready"), sem("v_taken")
        M = 4
        stored = [sem(f"stored{m}") for m in range(M)]
        ca, sa = (l * 6 + 1) * KD, (l * 6) * KD

        with nc.Block() as block:
            @block.sync
            def _(sp):
                if l == 1:
                    xv = e.x_dram.rearrange("(c t p) d -> c p t d", t=TPC, p=P)
                    for c in range(NC):
                        sp.dma_start(e.X[:, c * TPC:(c + 1) * TPC, :], xv[c]).then_inc(e.x_loaded[c], 16)
                sp.dma_start(w[:, :, :, :], w_qkv.rearrange("(k p) s n -> p s k n", p=P)).then_inc(w_loaded, 16)
                if bias_v is not None:
                    sp.dma_start(bv[:, :], bias_v.to_broadcast([P, D])).then_inc(w_loaded, 16)

                def body(i):
                    for u in range(2):
                        for m in range(M):
                            sp.wait_ge(third_ready, i * 2 * M + u * M + m + 1)
                            sp.wait_ge(second_ready, i * 2 * M + u * M + m + 1)
                            sp.wait_ge(first_ready, i * 2 * M + u * M + m + 1)
                            dst = (e.q_dram, e.k_dram)[m // KD]
                            g = m % KD
                            sp.dma_start(dst[:, g * P:(g + 1) * P, bass.ds(i * 2 * CH + u * CH, CH)].rearrange("s r t -> r s t"),
                                         part[:, m, :, :]).then_inc(stored[m], 16)

                with sp.Fori(0, NC // 2, 1) as i:
                    body(i)
                for s in stored:
                    sp.wait_ge(s, NC * 16)

            @block.vector
            def _(dve):
                if bias_v is None:
                    nc.vector.memset(bv[:, :], 0.0).then_inc(step, 1)
                    dve.wait_ge(step, 1)
                def x_tile(t):
                    if t % TPC == 0:
                        dve.wait_ge(e.x_loaded[t // TPC], 16)
                    return e.X[:, t, :]

                norm_stats(nc, e, dve, l, sem("norm_step"), stats_ready, root_done, x_tile)
                if bias_v is not None:
                    dve.wait_ge(w_loaded, 32)

                def normalise(i, u):
                    for t in range(TPC):
                        tile = i * 2 * TPC + u * TPC + t
                        nc.vector.tensor_scalar(xn[:, u, t, :], flat(e.X[:, bass.ds(tile, 1), :]),
                                                e.mv[:, bass.ds(tile, 1), 0], e.rstd[:, bass.ds(tile, 1)],
                                                ALU.subtract, ALU.mult).then_inc(xn_ready, 1)

                def rests(i, u, m):
                    dve.wait_ge(first_ready, i * 2 * M + u * M + m + 1)
                    nc.vector.tensor_tensor(rest[:, m, :], t32[:, m % 2, :], part[:, m, 0, :], ALU.subtract).then_inc(rest_ready, 1)

                def chunks(i, last):
                    for u in range(2):
                        if u == 0 or not last:
                            normalise(i + u, 1 - u)
                        for m in range(M):
                            rests(i, u, m)
                        for q in range(TPC // 2):
                            dve.wait_ge(v_ready, i * 2 * 2 + u * 2 + q + 1)
                            for r in range(2):
                                tile = i * 2 * TPC + u * TPC + q * 2 + r
                                nc.vector.tensor_tensor(
                                    e.V[:, :, bass.ds(tile, 1), :].rearrange("p h o c -> p h (o c)"),
                                    vp[:, q, r, :].rearrange("p (h c) -> p h c", h=H),
                                    bv[:, :].rearrange("p (h c) -> p h c", h=H), ALU.add).then_inc(v_taken, 1)

                normalise(0, 0)
                chunks(0, False)
                with dve.Fori(1, NC // 2 - 1, 1) as i:
                    chunks(i, False)
                chunks(NC // 2 - 1, True)

            @block.scalar
            def _(act):
                act.wait_ge(stats_ready, 1)
                nc.scalar.activation(e.root[:, :], e.var[:, :], ACT.Sqrt).then_inc(root_done, 1)

                def modulate(i, u):
                    for k in range(KD):
                        act.wait_ge(tp_ready, i * 2 * KD + u * KD + k + 1)
                        nc.scalar.activation(hT[:, u, k, :], tp[:, k, :], ACT.Identity,
                                             bias=e.col[:, sa + k:sa + k + 1], scale=e.col[:, ca + k:ca + k + 1]).then_inc(hT_ready, 1)

                def second(i, u, m):
                    act.wait_ge(rest_ready, i * 2 * M + u * M + m + 1)
                    nc.scalar.activation(part[:, m, 1, :], rest[:, m, :], ACT.Copy).then_inc(second_ready, 1)

                def chunks(i, last):
                    for u in range(2):
                        for m in range(M):
                            n = i * 2 * M + u * M + m
                            act.wait_ge(qk_ready, n + 1)
                            scale = HS ** -0.5 if m < KD else 1.0
                            if l == 0:
                                nc.scalar.activation(t32[:, m % 2, :], qk[:, m % 2, :], ACT.Identity,
                                                     bias=e.bias_qk[:, m:m + 1], scale=scale).then_inc(t32_ready, 1)
                            else:
                                nc.scalar.activation(t32[:, m % 2, :], qk[:, m % 2, :], ACT.Copy, scale=scale).then_inc(t32_ready, 1)
                            act.wait_ge(t32_ready, n + 1)
                            past(act, stored[m], (i * 2 + u) * 16)
                            nc.scalar.activation(part[:, m, 0, :], t32[:, m % 2, :], ACT.Copy).then_inc(first_ready, 1)
                            if m:
                                second(i, u, m - 1)
                        second(i, u, M - 1)
                        if u == 0 or not last:
                            modulate(i + u, 1 - u)

                modulate(0, 0)
                chunks(0, False)
                with act.Fori(1, NC // 2 - 1, 1) as i:
                    chunks(i, False)
                chunks(NC // 2 - 1, True)

            @block.gpsimd
            def _(pool):
                with pool.Fori(0, NC // 2, 1) as i:
                    for u in range(2):
                        for m in range(M):
                            pool.wait_ge(second_ready, i * 2 * M + u * M + m + 1)
                            nc.gpsimd.tensor_tensor(part[:, m, 2, :], rest[:, m, :], part[:, m, 1, :],
                                                    ALU.subtract).then_inc(third_ready, 1)

            @block.tensor
            def _(pe):
                def turn(i, u, first):
                    pe.wait_ge(xn_ready, i * 2 * TPC + (u + 1) * TPC)
                    if not first:
                        past(pe, hT_ready, i * 2 * KD + u * KD)
                    for k in range(KD):
                        for t in range(TPC):
                            last = nc.tensor.transpose(tp[:, k, t * P:(t + 1) * P], xn[:, u, t, k * P:(k + 1) * P], e.ident[:, :])
                        last.then_inc(tp_ready, 1)

                def chunks(i, last_body):
                    for u in range(2):
                        pe.wait_ge(hT_ready, i * 2 * KD + (u + 1) * KD)
                        for m in range(M):
                            if m >= 2:
                                pe.wait_ge(t32_ready, i * 2 * M + u * M + m - 1)
                            else:
                                past(pe, t32_ready, i * 2 * M + u * M)
                            for k in range(KD):
                                last = nc.tensor.matmul(qk[:, m % 2, :], w[:, m // KD, k, (m % KD) * P:(m % KD + 1) * P],
                                                        hT[:, u, k, :], start=(k == 0), stop=(k == KD - 1))
                            last.then_inc(qk_ready, 1)
                        if u == 0 or not last_body:
                            turn(i + u, 1 - u, False)
                        for q in range(TPC // 2):
                            past(pe, v_taken, i * 2 * TPC + u * TPC)
                            for r in range(2):
                                t = q * 2 + r
                                for k in range(KD):
                                    last = nc.tensor.matmul(vp[:, q, r, :], hT[:, u, k, t * P:(t + 1) * P], w[:, 2, k, :],
                                                            start=(k == 0), stop=(k == KD - 1))
                            last.then_inc(v_ready, 1)

                turn(0, 0, True)
                pe.wait_ge(w_loaded, 16 if bias_v is None else 32)
                chunks(0, False)
                with pe.Fori(1, NC // 2 - 1, 1) as i:
                    chunks(i, False)
                chunks(NC // 2 - 1, True)


def chunk_plan():
    plan = []
    for h in range(2):
        for j in reversed(range(NC)):
            for u in range(j + 1):
                plan.append((h, j, u, u == 0, u == j))
    return plan


def attention(nc, e, l):
    plan = chunk_plan()
    with ExitStack() as ctx:
        def sb(name, shape, dt=F32):
            return ctx.enter_context(nc.sbuf_tensor(f"{name}_a{l}", shape, dt))

        def ps(name, shape):
            return ctx.enter_context(nc.psum_tensor(f"{name}_a{l}", shape, F32))

        def sem(name):
            return new_sem(nc, e, f"at{l}_{name}")

        q_stack = [sb(f"q_stack{p}", [P, T], BF16) for p in range(2)]
        k_stack = [sb(f"k_stack{p}", [P, T], BF16) for p in range(2)]
        v_head = sb("v_head", [P, 2, NT, VC])
        prob = sb("prob", [P, RING, TPC, CH])
        acc_sb = sb("acc_sb", [P, CH])
        block_max = sb("block_max", [P, 2, TPC, NC])
        neg_max = sb("neg_max", [P, TPC])
        neg_rest = sb("neg_rest", [P, TPC])
        neg_part = sb("neg_part", [P, TPC, PARTS], BF16)
        total = sb("total", [P, 2, TPC, HS + 1])
        recip = sb("recip", [P, TPC])
        scores = ps("scores", [P, 2, 2, CH])
        tops = ps("tops", [P, 2, CH])
        acc = ps("acc", [P, CH])
        aux = ps("aux", [P, CH])
        neg_ps = aux[:, 0:CH // 2].bitcast(BF16)
        out_ps = aux[:, :].rearrange("p (t g c) -> p t g c", t=TPC, g=TPC)

        loaded = [sem("loaded0"), sem("loaded1")]
        ones_set, v_staged, x_loaded = sem("ones_set"), sem("v_staged"), sem("x_loaded")
        scores_ready, exp_done, pv_done, acc_saved = sem("scores_ready"), sem("exp_done"), sem("pv_done"), sem("acc_saved")
        top_ready, top_taken = sem("top_ready"), sem("top_taken")
        neg_ready, neg_rows_ready, neg_rows_set = sem("neg_ready"), sem("neg_rows_ready"), sem("neg_rows_set")
        out_ready, out_taken = sem("out_ready"), sem("out_taken")
        recip_done, step = sem("recip_done"), sem("step")
        LOADS = 2 * len(PAIRS) * 16
        ITERS = H // 2
        CHUNKS = 2 * NC

        def chunks_before(n):
            return (n // SLOTS) * CHUNKS + sum(1 for x in plan[:n % SLOTS] if x[4])

        def chunk_of(c):
            return (c // NC) % 2, NC - 1 - c % NC

        HEAD2 = QUADS
        assert SLOTS % RING == 0 and not any(plan[LOOK - d][4] for d in (1, 2, 3))

        with nc.Block() as block:
            @block.sync
            def _(sp):
                def load(p, head):
                    for n, (a, b) in enumerate(PAIRS):
                        sp.dma_start(q_stack[p][n * HS:(n + 1) * HS, :], e.q_heads[a, bass.ds(head, 1), :, :].rearrange("o r t -> (o r) t")
                                     ).then_inc(loaded[p], 16)
                        sp.dma_start(k_stack[p][n * HS:(n + 1) * HS, :], e.k_heads[b, bass.ds(head, 1), :, :].rearrange("o r t -> (o r) t")
                                     ).then_inc(loaded[p], 16)

                load(0, 0)
                load(1, 1)
                if l == 1:
                    xv = e.x_dram.rearrange("(g p c) d -> p g c d", p=P, c=HS)
                    for g in range(NT // HS):
                        sp.dma_start(e.X[:, g * HS:(g + 1) * HS, :], xv[:, g]).then_inc(x_loaded, 16)
                with sp.Fori(0, ITERS - 1, 1) as i:
                    for p in range(2):
                        sp.wait_ge(scores_ready, i * 2 * SLOTS + 2 * (HEAD2 * (p + 1)))
                        load(p, i * 2 + 2 + p)
                sp.wait_ge(scores_ready, (ITERS - 1) * 2 * SLOTS + 2 * HEAD2)
                load(0, 0)
                sp.wait_ge(loaded[0], LOADS * (ITERS + 1))
                if l == 1:
                    sp.wait_ge(x_loaded, 16 * (NT // HS))

            @block.gpsimd
            def _(pool):
                for p in range(2):
                    nc.gpsimd.memset(k_stack[p][SR:P, :], 1.0).then_inc(ones_set, 1)
                pool.wait_ge(ones_set, 2)
                nc.gpsimd.memset(v_head[:, :, :, HS:VC], 0.0).then_inc(ones_set, 1)
                pool.wait_ge(ones_set, 3)
                nc.gpsimd.memset(v_head[:, :, :, HS:HS + 1], 1.0).then_inc(ones_set, 1)

                def stage(p, head):
                    nc.gpsimd.tensor_copy(v_head[:, p, :, 0:HS], e.V[:, bass.ds(head, 1), :, :].rearrange("p o t c -> p (o t) c")
                                          ).then_inc(v_staged, 1)

                pool.wait_ge(ones_set, 4)
                stage(0, 0)
                stage(1, 1)
                with pool.Fori(0, ITERS - 1, 1) as i:
                    for p in range(2):
                        pool.wait_ge(pv_done, i * SLOTS + HEAD2 * (p + 1))
                        stage(p, i * 2 + 2 + p)

            @block.tensor
            def _(pe):
                def main_scores(i, n, kb):
                    h, j, u, first, last = plan[n % SLOTS]
                    half, b = kb // 2, kb % 2
                    if n > 0 and b == 0:
                        pe.wait_ge(exp_done, i * 2 * SLOTS + 2 * n + half - 1)
                    if kb == 0 and first:
                        pe.wait_ge(neg_rows_set, i * CHUNKS + chunks_before(n) + 1)
                    diag = u == j
                    c0 = P * kb if diag and j else 0
                    last_mm = nc.tensor.matmul(scores[:, half, b, c0:CH],
                                               k_stack[h][0:MR, u * CH + kb * P:u * CH + (kb + 1) * P],
                                               q_stack[h][0:MR, j * CH + c0:(j + 1) * CH], start=True, stop=not diag)
                    if diag:
                        m0 = P * kb if j else 0
                        last_mm = nc.tensor.matmul(scores[:, half, b, m0:P * (kb + 1)], e.ident_b[:, :],
                                                   e.mask_q[:, CH - (P * kb - m0):CH + P], start=False, stop=True)
                    if b:
                        last_mm.then_inc(scores_ready, 1)

                def top_scores(i, n, t):
                    h, j, u, first, last = plan[n % SLOTS]
                    m = 4 * n + t
                    if m >= 2:
                        pe.wait_ge(top_taken, i * TPC * SLOTS + m - 1)
                    if t == 0 and j == NC - 1 and first:
                        pe.wait_ge(loaded[h], i * LOADS + (n // SLOTS + 1) * LOADS)
                    diag = u == j
                    width = P * (t + 1) if diag else CH
                    last_mm = nc.tensor.matmul(tops[:, m % 2, 0:width], q_stack[h][0:SR, j * CH + t * P:j * CH + (t + 1) * P],
                                               k_stack[h][0:SR, u * CH:u * CH + width], start=True, stop=not diag)
                    if diag:
                        last_mm = nc.tensor.matmul(tops[:, m % 2, t * P:width], e.ident_b[:, :], e.mask_k[:, :], start=False, stop=True)
                    last_mm.then_inc(top_ready, 1)

                def neg_rows(i, c, outs):
                    pe.wait_ge(neg_ready, i * CHUNKS + c + 1)
                    if c:
                        pe.wait_ge(neg_rows_set, i * CHUNKS + c)
                    if outs is not None:
                        pe.wait_ge(out_taken, i * CHUNKS + outs + 1)
                    for t in range(TPC):
                        last_mm = nc.tensor.transpose(neg_ps[SR:SR + PARTS, t * P:(t + 1) * P], neg_part[:, t, :], e.ident_b[:, :])
                    last_mm.then_inc(neg_rows_ready, 1)

                def outputs(i, c, rows):
                    pe.wait_ge(acc_saved, i * CHUNKS + c + 2)
                    pe.wait_ge(out_taken, i * CHUNKS + c + 1)
                    pe.wait_ge(neg_rows_set, i * CHUNKS + rows)
                    for t in range(TPC):
                        last_mm = nc.tensor.transpose(out_ps[:, t, :, :].rearrange("p g c -> p (g c)"), acc_sb[:, t * P:(t + 1) * P], e.ident[:, :])
                    last_mm.then_inc(out_ready, 1)

                def weigh(i, n):
                    h, j, u, first, last = plan[n]
                    pe.wait_ge(exp_done, i * 2 * SLOTS + 2 * n + 2)
                    if first:
                        pe.wait_ge(acc_saved, i * CHUNKS + chunks_before(n) + 1)
                        if j == NC - 1:
                            pe.wait_ge(v_staged, i * 2 + h + 1)
                    for kb in range(TPC):
                        c0 = P * kb if u == j and j else 0
                        last_mm = nc.tensor.matmul(acc[VC * kb:VC * (kb + 1), c0:CH], v_head[:, h, u * TPC + kb, :],
                                                   prob[:, n % RING, kb, c0:CH], start=first, stop=last, skip_group_check=True)
                    last_mm.then_inc(pv_done, 1)

                pe.wait_ge(ones_set, 4)
                for n in range(LOOK):
                    for t in range(TPC):
                        top_scores(0, n, t)
                    if n >= 2 and plan[n - 2][4]:
                        neg_rows(0, chunks_before(n - 2), None)
                for kb in range(TPC):
                    main_scores(0, 0, kb)

                with pe.Fori(0, ITERS, 1) as i:
                    for n in range(SLOTS):
                        ahead = n + LOOK
                        main_scores(i, n + 1, 0)
                        top_scores(i, ahead, 0)
                        main_scores(i, n + 1, 1)
                        main_scores(i, n + 1, 2)
                        top_scores(i, ahead, 1)
                        main_scores(i, n + 1, 3)
                        top_scores(i, ahead, 2)
                        if plan[(ahead - 2) % SLOTS][4]:
                            neg_rows(i, chunks_before(ahead - 2), chunks_before(max(n - 1, 0)))
                        weigh(i, n)
                        top_scores(i, ahead, 3)
                        if n > 0 and plan[n - 1][4]:
                            outputs(i, chunks_before(n - 1), chunks_before(ahead - 1))
                    outputs(i, CHUNKS - 1, chunks_before(SLOTS + LOOK - 2))

            @block.scalar
            def _(act):
                def neg_rows_out(i, c):
                    act.wait_ge(neg_rows_ready, i * CHUNKS + c + 1)
                    h, j = chunk_of(c)
                    nc.scalar.activation(q_stack[h][SR:SR + PARTS, j * CH:(j + 1) * CH], neg_ps[SR:SR + PARTS, :], ACT.Copy).then_inc(neg_rows_set, 1)

                def exps(i, n, half):
                    h, j, u, first, last = plan[n % SLOTS]
                    act.wait_ge(scores_ready, i * 2 * SLOTS + 2 * n + half + 1)
                    c0 = 2 * P if u == j and j and half else 0
                    nc.scalar.activation(prob[:, n % RING, 2 * half:2 * half + 2, c0:CH], scores[:, half, :, c0:CH], ACT.Exp
                                         ).then_inc(exp_done, 1)

                def save(i, n):
                    act.wait_ge(pv_done, i * SLOTS + n + 1)
                    if chunks_before(n):
                        act.wait_ge(out_ready, i * CHUNKS + chunks_before(n))
                    nc.scalar.activation(acc_sb[:, :], acc[:, :], ACT.Copy).then_inc(acc_saved, 1)

                nc.scalar.activation(acc_sb[:, :], e.mask_q[:, 0:CH], ACT.Copy).then_inc(acc_saved, 1)
                for n in range(LOOK - 2):
                    if plan[n][4]:
                        neg_rows_out(0, chunks_before(n))
                with act.Fori(0, ITERS, 1) as i:
                    for n in range(SLOTS):
                        if n >= RING:
                            act.wait_ge(pv_done, i * SLOTS + n - RING + 1)
                        exps(i, n, 0)
                        exps(i, n, 1)
                        if n and plan[(n + LOOK - 3) % SLOTS][4]:
                            neg_rows_out(i, chunks_before(n + LOOK - 3))
                        if n and plan[n - 1][4]:
                            save(i, n - 1)
                    save(i, SLOTS - 1)

            @block.vector
            def _(dve):
                CHAIN = 3

                def top(i, n, t):
                    h, j, u, first, last = plan[n % SLOTS]
                    m = 4 * n + t
                    dve.wait_ge(top_ready, i * TPC * SLOTS + m + 1)
                    width = P * (t + 1) if u == j else CH
                    nc.vector.tensor_reduce(block_max[:, j % 2, t, u:u + 1], tops[:, m % 2, 0:width], AX.X, ALU.max).then_inc(top_taken, 1)

                def negate(i, n, s):
                    j, c = plan[n % SLOTS][1], chunks_before(n)
                    seen = i * CHUNKS * CHAIN + CHAIN * c
                    if s == 0:
                        dve.wait_ge(top_taken, i * TPC * SLOTS + TPC * (n + 1))
                        if c:
                            dve.wait_ge(neg_rows_ready, i * CHUNKS + c)
                        nc.vector.tensor_reduce(neg_part[:, :, 0], block_max[:, j % 2, :, 0:j + 1], AX.X, ALU.max, negate=True)
                        nc.vector.tensor_reduce(neg_max[:, :], block_max[:, j % 2, :, 0:j + 1], AX.X, ALU.max, negate=True).then_inc(step, 1)
                    elif s == 1:
                        dve.wait_ge(step, seen + 1)
                        nc.vector.tensor_tensor(neg_rest[:, :], neg_max[:, :], neg_part[:, :, 0], ALU.subtract).then_inc(step, 1)
                    elif s == 2:
                        dve.wait_ge(step, seen + 2)
                        nc.vector.tensor_copy(neg_part[:, :, 1], neg_rest[:, :]).then_inc(step, 1)
                    else:
                        dve.wait_ge(step, seen + 3)
                        nc.vector.tensor_tensor(neg_part[:, :, 2], neg_rest[:, :], neg_part[:, :, 1], ALU.subtract).then_inc(neg_ready, 1)

                def normalise(i, c, s):
                    h, j = chunk_of(c)
                    if s == 0:
                        dve.wait_ge(out_ready, i * CHUNKS + c + 1)
                        nc.vector.tensor_reduce(total[:, c % 2, :, :], out_ps[:, :, :, 0:HS + 1].rearrange("p t g c -> p t c g"), AX.X, ALU.add
                                                ).then_inc(out_taken, 1)
                    elif s == 1:
                        dve.wait_ge(out_taken, i * CHUNKS + c + 2)
                        nc.vector.reciprocal(recip[:, :], total[:, c % 2, :, HS]).then_inc(recip_done, 1)
                    else:
                        dve.wait_ge(recip_done, i * CHUNKS + c + 1)
                        nc.vector.tensor_tensor(e.O[:, j * TPC:(j + 1) * TPC, bass.ds((i * 2 + h) * HS, HS)],
                                                total[:, c % 2, :, 0:HS], recip[:, :].rearrange("p (t o) -> p t o", o=1).to_broadcast([P, TPC, HS]),
                                                ALU.mult)

                def tops_down(i, n, out_chunk):
                    for t in range(TPC):
                        top(i, n, t)
                        if n and plan[(n - 1) % SLOTS][4]:
                            negate(i, n - 1, t)
                        if out_chunk is not None and t < 3:
                            normalise(i, out_chunk, t)

                nc.vector.memset(recip[:, :], 0.0).then_inc(out_taken, 1)
                for n in range(LOOK):
                    tops_down(0, n, None)
                with dve.Fori(0, ITERS, 1) as i:
                    for n in range(SLOTS):
                        tops_down(i, n + LOOK, chunks_before(n - 2) if n > 1 and plan[n - 2][4] else None)
                    for c in (CHUNKS - 2, CHUNKS - 1):
                        for s in range(3):
                            normalise(i, c, s)


def project_out(nc, e):
    with ExitStack() as ctx:
        def sem(name):
            return new_sem(nc, e, f"po_{name}")

        o_in = ctx.enter_context(nc.sbuf_tensor("o_in", [P, 2, TPC, D], F32))
        oT = ctx.enter_context(nc.sbuf_tensor("oT", [P, 2, KD, CH], F32))
        tp = ctx.enter_context(nc.psum_tensor("po_tp", [P, KD, CH], F32))
        y = ctx.enter_context(nc.psum_tensor("po_y", [P, 2, TPC, D], F32))
        staged, turned, oT_ready, y_ready, added = sem("staged"), sem("turned"), sem("oT"), sem("y"), sem("added")

        with nc.Block() as block:
            @block.gpsimd
            def _(pool):
                def one_round(i):
                    for u in range(2):
                        past(pool, turned, i * 2)
                        nc.gpsimd.tensor_copy(o_in[:, u, :, :], e.O[:, bass.ds(i * 2 * TPC + u * TPC, TPC), :]).then_inc(staged, 1)

                one_round(0)
                with pool.Fori(1, NC // 2, 1) as i:
                    one_round(i)

            @block.tensor
            def _(pe):
                def one_round(i):
                    for u in range(2):
                        pe.wait_ge(staged, i * 2 + u + 1)
                        past(pe, oT_ready, (i * 2 + u) * KD)
                        for k in range(KD):
                            for t in range(TPC):
                                last = nc.tensor.transpose(tp[:, k, t * P:(t + 1) * P], o_in[:, u, t, k * P:(k + 1) * P], e.ident[:, :])
                        last.then_inc(turned, 1)
                        pe.wait_ge(oT_ready, (i * 2 + u + 1) * KD)
                        past(pe, added, i * 2)
                        for t in range(TPC):
                            for k in range(KD):
                                nc.tensor.matmul(y[:, u, t, :], oT[:, u, k, t * P:(t + 1) * P], e.w_out0[:, k, :], start=(k == 0), stop=False)
                            last = nc.tensor.matmul(y[:, u, t, :], e.ones[0:1, :], e.b_out0[:, :], start=False, stop=True)
                        last.then_inc(y_ready, 1)

                one_round(0)
                with pe.Fori(1, NC // 2, 1) as i:
                    one_round(i)

            @block.scalar
            def _(act):
                with act.Fori(0, NC // 2, 1) as i:
                    for u in range(2):
                        act.wait_ge(turned, i * 2 + u + 1)
                        for k in range(KD):
                            nc.scalar.activation(oT[:, u, k, :], tp[:, k, :], ACT.Copy).then_inc(oT_ready, 1)

            @block.vector
            def _(dve):
                with dve.Fori(0, NC // 2, 1) as i:
                    for u in range(2):
                        dve.wait_ge(y_ready, i * 2 + u + 1)
                        x = e.X[:, bass.ds(i * 2 * TPC + u * TPC, TPC), :]
                        nc.vector.tensor_tensor(x, y[:, u, :, :], x, ALU.add).then_inc(added, 1)


def feed_norm(nc, e, l, gate_w, gate_bias, outs):
    with ExitStack() as ctx:
        def sb(name, shape, dt=F32):
            return ctx.enter_context(nc.sbuf_tensor(f"fn{l}_{name}", shape, dt))

        def ps(name, shape):
            return ctx.enter_context(nc.psum_tensor(f"fn{l}_{name}", shape, F32))

        def sem(name):
            return new_sem(nc, e, f"fn{l}_{name}")

        G = outs
        xn = sb("xn", [P, 2, TPC, D])
        hTc = sb("hTc", [P, 2, KD, CH])
        row_h = sb("row_h", [P, 2, TPC, D]) if l == 0 else None
        gw = sb("gw", [P, KD, G])
        gb = sb("gb", [P, G])
        tp = ps("tp", [P, KD, CH])
        lg = ps("lg", [P, TPC, 128])
        turned_sel = ps("turned_sel", [P, CH])
        if l == 0:
            best = sb("best", [P, TPC, 8])
            left = sb("left", [P, TPC, E0])
            sel = sb("sel", [P, 2, TPC, E0])
            rank = sb("rank", [P, NT])
            rank_i = sb("rank_i", [P, NT], I32)
        ld, step, stats_ready, root_done = sem("ld"), sem("step"), sem("stats"), sem("root")
        xn_ready, turned, hT_ready, rows_ready, lg_ready, lg_taken = sem("xn"), sem("turned"), sem("hT"), sem("rows"), sem("lg"), sem("lg_taken")
        stored, sel_ready, sel_turned, order_ready, chain, scaled = sem("stored"), sem("sel"), sem("sel_turned"), sem("order"), sem("chain"), sem("scaled")
        rank_ready, copied = sem("rank"), sem("copied")
        cb, sb_ = (l * 6 + 4) * KD, (l * 6 + 3) * KD
        row_c, row_s = (e.row_cb0, e.row_sb0) if l == 0 else (e.row_cb1, e.row_sb1)
        NL = 1 if gate_bias is None else 2
        COPIES = 2 * KD if l == 0 else KD
        if l == 1:
            nil = sb("nil", [P, D])
            nil_set, cleared = sem("nil_set"), sem("cleared")

        with nc.Block() as block:
            @block.sync
            def _(sp):
                sp.dma_start(gw[:, :, :], gate_w.rearrange("(k p) n -> p k n", p=P)).then_inc(ld, 16)
                if gate_bias is not None:
                    sp.dma_start(gb[:, :], gate_bias.to_broadcast([P, G])).then_inc(ld, 16)
                if l == 1:
                    sp.wait_ge(nil_set, 1)
                    rows = e.queue.rearrange("(n t p) d -> n p t d", p=P, t=E1)
                    for n in range(e.queue.shape[0] // (P * E1)):
                        sp.dma_start(rows[n], nil[:, :].rearrange("p (o d) -> p o d", o=1).to_broadcast([P, E1, D])).then_inc(cleared, 16)
                    sp.wait_ge(cleared, 16 * (e.queue.shape[0] // (P * E1)))
                if l == 0:
                    table = e.table.rearrange("(c t p) w -> c p t w", t=TPC, p=P)
                    with sp.Fori(0, NC // 2, 1) as i:
                        for u in range(2):
                            sp.wait_ge(rows_ready, i * 2 + u + 1)
                            sp.dma_start(table[bass.ds(i * 2 + u, 1), :, :, 0:D].rearrange("o p t w -> (o p) t w"), row_h[:, u, :, :]).then_inc(stored, 16)
                    sp.wait_ge(stored, 16 * NC)

            @block.vector
            def _(dve):
                norm_stats(nc, e, dve, l, sem("norm_step"), stats_ready, root_done, lambda t: e.X[:, t, :])
                if l == 0:
                    dve.wait_ge(rank_ready, 1)
                    nc.vector.tensor_copy(rank[:, :], rank_i[:, :]).then_inc(step, 1)
                    dve.wait_ge(step, 1)

                if gate_bias is not None:
                    dve.wait_ge(ld, 16 * NL)

                def normalise(i, u):
                    for t in range(TPC):
                        tile = i * 2 * TPC + u * TPC + t
                        nc.vector.tensor_scalar(xn[:, u, t, :], flat(e.X[:, bass.ds(tile, 1), :]), e.mv[:, bass.ds(tile, 1), 0],
                                                e.rstd[:, bass.ds(tile, 1)], ALU.subtract, ALU.mult).then_inc(xn_ready, 1)

                def chunks(i, last):
                    for u in range(2):
                        if u == 0 or not last:
                            past(dve, rows_ready, i * 2 + u)
                            past(dve, turned, i * 2 + u)
                            normalise(i + u, 1 - u)
                        dve.wait_ge(lg_ready, i * 2 + u + 1)
                        logits = e.logits[:, bass.ds(i * 2 * TPC + u * TPC, TPC), :]
                        if gate_bias is None:
                            nc.vector.tensor_copy(logits, lg[:, :, 0:G]).then_inc(lg_taken, 1)
                        else:
                            nc.vector.tensor_tensor(logits, lg[:, :, 0:G], gb[:, :].rearrange("p (o g) -> p o g", o=1).to_broadcast([P, TPC, G]),
                                                    ALU.add).then_inc(lg_taken, 1)
                        if l == 0:
                            for t in range(TPC):
                                nc.vector.max(best[:, t, :], lg[:, t, 0:E0]).then_inc(chain, 1)
                            c = i * 2 * 2 * TPC + u * 2 * TPC
                            dve.wait_ge(chain, c + TPC)
                            settle(dve)
                            for t in range(TPC):
                                nc.vector.match_replace(left[:, t, :], best[:, t, :], lg[:, t, 0:E0], MASKED).then_inc(chain, 1)
                            dve.wait_ge(chain, c + 2 * TPC)
                            nc.vector.tensor_tensor(e.chosen[:, bass.ds(i * 2 * TPC + u * TPC, TPC), :], lg[:, :, 0:E0], left[:, :, :], ALU.not_equal).then_inc(scaled, 1)
                            dve.wait_ge(scaled, i * 2 + u + 1)
                            past(dve, sel_turned, i * 2)
                            nc.vector.tensor_tensor(sel[:, u, :, :], e.chosen[:, bass.ds(i * 2 * TPC + u * TPC, TPC), :],
                                                    rank[:, bass.ds(i * 2 * TPC + u * TPC, TPC)].rearrange("p (t o) -> p t o", o=1).to_broadcast([P, TPC, E0]),
                                                    ALU.mult).then_inc(sel_ready, 1)

                normalise(0, 0)
                chunks(0, False)
                with dve.Fori(1, NC // 2 - 1, 1) as i:
                    chunks(i, False)
                chunks(NC // 2 - 1, True)

            @block.gpsimd
            def _(pool):
                if l == 1:
                    nc.gpsimd.memset(nil[:, :], 0.0).then_inc(nil_set, 1)
                if l == 0:
                    nc.gpsimd.iota(rank_i[:, :], [[-P, NT]], base=T, channel_multiplier=-1).then_inc(rank_ready, 1)
                def one_round(i):
                    for u in range(2):
                        pool.wait_ge(xn_ready, i * 2 * TPC + (u + 1) * TPC)
                        if l == 0:
                            past(pool, stored, i * 32)
                            dst = row_h[:, u, :, :]
                        else:
                            dst = e.H[:, bass.ds(i * 2 * TPC + u * TPC, TPC), :]
                        wide = lambda row: row[:, :].rearrange("p (o d) -> p o d", o=1).to_broadcast([P, TPC, D])
                        nc.gpsimd.tensor_tensor(dst, xn[:, u, :, :], wide(row_c), ALU.mult).then_inc(copied, 1)
                        pool.wait_ge(copied, i * 2 + u + 1)
                        settle(pool)
                        nc.gpsimd.tensor_tensor(dst, dst, wide(row_s), ALU.add).then_inc(rows_ready, 1)

                one_round(0)
                with pool.Fori(1, NC // 2, 1) as i:
                    one_round(i)

            @block.scalar
            def _(act):
                act.wait_ge(stats_ready, 1)
                nc.scalar.activation(e.root[:, :], e.var[:, :], ACT.Sqrt).then_inc(root_done, 1)

                def modulate(i, u):
                    act.wait_ge(turned, i * 2 + u + 1)
                    for k in range(KD):
                        nc.scalar.activation(hTc[:, u, k, :], tp[:, k, :], ACT.Identity,
                                             bias=e.col[:, sb_ + k:sb_ + k + 1], scale=e.col[:, cb + k:cb + k + 1]).then_inc(hT_ready, 1)
                        if l == 0:
                            nc.scalar.activation(e.hT[:, k, bass.ds(i * 2 * CH + u * CH, CH)], tp[:, k, :], ACT.Identity,
                                                 bias=e.col[:, sb_ + k:sb_ + k + 1], scale=e.col[:, cb + k:cb + k + 1]).then_inc(hT_ready, 1)

                def chunks(i, last):
                    for u in range(2):
                        if u == 0 or not last:
                            modulate(i + u, 1 - u)
                        if l == 0:
                            act.wait_ge(sel_turned, i * 2 + u + 1)
                            nc.scalar.activation(e.order[E0 * u:E0 * (u + 1), bass.ds(i * CH, CH)], turned_sel[E0 * u:E0 * (u + 1), :], ACT.Copy).then_inc(order_ready, 1)

                modulate(0, 0)
                chunks(0, False)
                with act.Fori(1, NC // 2 - 1, 1) as i:
                    chunks(i, False)
                chunks(NC // 2 - 1, True)

            @block.tensor
            def _(pe):
                def turn(i, u):
                    pe.wait_ge(xn_ready, i * 2 * TPC + (u + 1) * TPC)
                    for k in range(KD):
                        for t in range(TPC):
                            last_mm = nc.tensor.transpose(tp[:, k, t * P:(t + 1) * P], xn[:, u, t, k * P:(k + 1) * P], e.ident[:, :])
                    last_mm.then_inc(turned, 1)

                def chunks(i, last):
                    for u in range(2):
                        pe.wait_ge(hT_ready, (i * 2 + u + 1) * COPIES)
                        if l == 1 and (u == 0 or not last):
                            turn(i + u, 1 - u)
                        past(pe, lg_taken, i * 2 + u)
                        if l == 0:
                            past(pe, scaled, i * 2 + u)
                        for t in range(TPC):
                            for k in range(KD):
                                last_mm = nc.tensor.matmul(lg[:, t, 0:G], hTc[:, u, k, t * P:(t + 1) * P], gw[:, k, :],
                                                           start=(k == 0), stop=(k == KD - 1))
                        last_mm.then_inc(lg_ready, 1)
                        if l == 0 and (u == 0 or not last):
                            turn(i + u, 1 - u)
                        if l == 0:
                            pe.wait_ge(sel_ready, i * 2 + u + 1)
                            past(pe, order_ready, i * 2 + u)
                            for t in range(TPC):
                                last_mm = nc.tensor.matmul(turned_sel[E0 * u:E0 * (u + 1), t * P:(t + 1) * P], sel[:, u, t, :], e.ident[:, :],
                                                           start=True, stop=True)
                            last_mm.then_inc(sel_turned, 1)

                turn(0, 0)
                pe.wait_ge(ld, 16 * NL)
                chunks(0, False)
                with pe.Fori(1, NC // 2 - 1, 1) as i:
                    chunks(i, False)
                chunks(NC // 2 - 1, True)


def shared_expert(nc, e, a):
    with ExitStack() as ctx:
        def sb(name, shape, dt=F32):
            return ctx.enter_context(nc.sbuf_tensor(f"se_{name}", shape, dt))

        def ps(name, shape):
            return ctx.enter_context(nc.psum_tensor(f"se_{name}", shape, F32))

        def sem(name):
            return new_sem(nc, e, f"se_{name}")

        FT = IS // P
        wu = sb("wu", [P, KD, 2 * IS])
        wd = sb("wd", [P, FT, D])
        aT = sb("aT", [P, 2, FT, CH])
        silu = sb("silu", [P, 2, CH])
        weight = sb("weight", [P, NT, E0])
        small = sb("small", [P, 3, NT])
        sig = sb("sig", [P, NT])
        cand = sb("cand", [P, CAP])
        eight = sb("eight", [P, 2 * (CAP // 8 // NC), 8])
        both = sb("both", [E0, 2, CAP])
        first = sb("first", [E0, CAP])
        slot_f, empty = sb("slot_f", [P, 2, E0]), sb("empty", [P, E0])
        lane_i, lane = sb("lane_i", [P, 1], I32), sb("lane", [P, 1])
        shared_y = sb("shared_y", [P, 2, TPC, D])
        up = ps("up", [P, 2, 2, CH])
        y = ps("y", [P, TPC, D])
        tk = ps("tk", [P, E0])
        ld, softmax_in, softmax_ex, chain, weight_ready, sig_ready, tanh_done = (sem(n) for n in ("ld", "sm_in", "sm_ex", "chain", "weight", "sig", "tanh"))
        up_ready, silu_ready, a_ready, y_ready, y_taken, x_ready, stored = (sem(n) for n in ("up", "silu", "a", "y", "y_taken", "x", "stored"))
        found, moved, tk_ready, table_stored, lane_made, padded = (sem(n) for n in ("found", "moved", "tk", "table", "lane", "padded"))
        rounds = CAP // 8 // NC

        with nc.Block() as block:
            @block.sync
            def _(sp):
                sp.dma_start(wu[:, :, :], a.L0_shared_up.rearrange("(k p) n -> p k n", p=P)).then_inc(ld, 16)
                sp.dma_start(wd[:, :, :], a.L0_shared_down.rearrange("(k p) n -> p k n", p=P)).then_inc(ld, 16)
                sp.dma_start(e.x_padded[T:T + CAP, :], e.row_gb0[:, :]).then_inc(padded, 16)
                sp.wait_ge(weight_ready, 1)
                sp.dma_start(e.table.rearrange("(t p) w -> p t w", p=P)[:, :, D:ROW0], weight[:, :, :]).then_inc(table_stored, 16)
                xs = e.x_dram.rearrange("(c t p) d -> c p t d", t=TPC, p=P)
                with sp.Fori(0, NC, 1) as i:
                    sp.wait_ge(x_ready, i + 1)
                    sp.dma_start(xs[bass.ds(i, 1)].rearrange("o p t d -> (o p) t d"), e.X[:, bass.ds(i * TPC, TPC), :]).then_inc(stored, 16)
                sp.wait_ge(found, 3 * rounds * NC)
                sp.dma_start(both[:, 0, :], cand[0:E0, :]).then_inc(moved, 16)
                sp.dma_start(both[:, 1, :], cand[E0:P, :]).then_inc(moved, 16)
                sp.wait_ge(stored, 16 * NC)
                sp.wait_ge(table_stored, 16)
                sp.wait_ge(padded, 16)

            @block.gpsimd
            def _(pool):
                nc.gpsimd.iota(lane_i[:, :], [[0, 1]], base=0, channel_multiplier=1).then_inc(lane_made, 1)

            @block.vector
            def _(dve):
                n = [0]

                def link(ins):
                    n[0] += 1
                    ins.then_inc(chain, 1)
                    dve.wait_ge(chain, n[0])

                experts = e.logits[:, :, 0:E0]
                wide = lambda s: small[:, s, :].rearrange("p (t o) -> p t o", o=1).to_broadcast([P, NT, E0])
                link(nc.vector.tensor_reduce(small[:, 0, :], experts, AX.X, ALU.max))
                nc.vector.tensor_tensor(weight[:, :, :], experts, wide(0), ALU.subtract).then_inc(softmax_in, 1)
                dve.wait_ge(softmax_ex, 1)
                link(nc.vector.tensor_tensor(weight[:, :, :], weight[:, :, :], e.chosen[:, :, :], ALU.mult))
                link(nc.vector.tensor_reduce(small[:, 1, :], weight[:, :, :], AX.X, ALU.add))
                link(nc.vector.reciprocal(small[:, 2, :], small[:, 1, :]))
                nc.vector.tensor_tensor(weight[:, :, :], weight[:, :, :], wide(2), ALU.mult).then_inc(weight_ready, 1)
                dve.wait_ge(tanh_done, 1)
                nc.vector.tensor_scalar(sig[:, :], sig[:, :], 0.5, 0.5, ALU.mult, ALU.add).then_inc(sig_ready, 1)
                dve.wait_ge(sig_ready, 1)

                def one_round(i):
                    for u in range(2):
                        for f in range(FT):
                            m = u * FT + f
                            dve.wait_ge(silu_ready, i * 2 * FT + m + 1)
                            nc.vector.tensor_tensor(aT[:, u, f, :], silu[:, m % 2, :], up[:, m % 2, 1, :], ALU.mult).then_inc(a_ready, 1)
                            if f % 2 == 0:
                                r = u * rounds + f // 2
                                done = i * 6 * rounds + r * 3
                                past(dve, found, done)
                                settle(dve)
                                nc.vector.max(eight[:, r, :], e.order[:, :]).then_inc(found, 1)
                                dve.wait_ge(found, done + 1)
                                settle(dve)
                                nc.vector.match_replace(e.order[:, :], eight[:, r, :], e.order[:, :], 0.0).then_inc(found, 1)
                                nc.vector.tensor_copy(cand[:, bass.ds(i * 2 * rounds * 8 + r * 8, 8)], eight[:, r, :]).then_inc(found, 1)
                        dve.wait_ge(y_ready, i * 2 + u + 1)
                        for t in range(TPC):
                            tile = i * 2 * TPC + u * TPC + t
                            nc.vector.scalar_tensor_tensor(shared_y[:, u, t, :], y[:, t, :], sig[:, bass.ds(tile, 1)], e.row_gb0[:, :],
                                                           ALU.mult, ALU.mult).then_inc(y_taken, 1)
                        x = e.X[:, bass.ds(i * 2 * TPC + u * TPC, TPC), :]
                        dve.wait_ge(y_taken, i * 2 * TPC + (u + 1) * TPC)
                        nc.vector.tensor_tensor(x, x, shared_y[:, u, :, :], ALU.add).then_inc(x_ready, 1)

                one_round(0)
                with dve.Fori(1, NC // 2, 1) as i:
                    one_round(i)
                dve.wait_ge(moved, 32)
                for r in range(CAP // 8):
                    link(nc.vector.max(first[:, r * 8:(r + 1) * 8], both[:, :, :]))
                    link(nc.vector.match_replace(both[:, :, :], first[:, r * 8:(r + 1) * 8], both[:, :, :], 0.0))
                dve.wait_ge(tk_ready, 1)
                dve.wait_ge(lane_made, 1)
                link(nc.vector.tensor_copy(lane[:, :], lane_i[:, :]))
                link(nc.vector.tensor_scalar(slot_f[:, 0, :], tk[:, :], -1.0, float(T), ALU.mult, ALU.add))
                link(nc.vector.tensor_scalar(slot_f[:, 1, :], slot_f[:, 0, :], float(T - 1), None, ALU.min))
                link(nc.vector.tensor_scalar(empty[:, :], slot_f[:, 0, :], float(T), None, ALU.is_ge))
                link(nc.vector.scalar_tensor_tensor(slot_f[:, 0, :], empty[:, :], lane[:, :], slot_f[:, 0, :], ALU.mult, ALU.add))
                link(nc.vector.tensor_copy(e.to_token[:, :], slot_f[:, 0, :]))
                link(nc.vector.tensor_copy(e.from_token[:, :], slot_f[:, 1, :]))

            @block.scalar
            def _(act):
                act.wait_ge(softmax_in, 1)
                nc.scalar.activation(weight[:, :, :], weight[:, :, :], ACT.Exp).then_inc(softmax_ex, 1)
                nc.scalar.activation(sig[:, :], e.logits[:, :, E0], ACT.Tanh, scale=0.5).then_inc(tanh_done, 1)
                def one_round(i):
                    for u in range(2):
                        for f in range(FT):
                            m = u * FT + f
                            act.wait_ge(up_ready, i * 2 * FT + m + 1)
                            past(act, a_ready, i * 2 * FT + max(m - 1, 0))
                            nc.scalar.activation(silu[:, m % 2, :], up[:, m % 2, 0, :], ACT.Silu).then_inc(silu_ready, 1)

                one_round(0)
                with act.Fori(1, NC // 2, 1) as i:
                    one_round(i)

            @block.tensor
            def _(pe):
                pe.wait_ge(ld, 32)
                def one_round(i):
                    for u in range(2):
                        for f in range(FT):
                            m = u * FT + f
                            past(pe, a_ready, i * 2 * FT + max(m - 1, 0))
                            for s in range(2):
                                for k in range(KD):
                                    last = nc.tensor.matmul(up[:, m % 2, s, :], wu[:, k, s * IS + f * P:s * IS + (f + 1) * P],
                                                            e.hT[:, k, bass.ds(i * 2 * CH + u * CH, CH)], start=(k == 0), stop=(k == KD - 1))
                            last.then_inc(up_ready, 1)
                        pe.wait_ge(a_ready, i * 2 * FT + (u + 1) * FT)
                        past(pe, y_taken, i * 2 * TPC + u * TPC)
                        for t in range(TPC):
                            for f in range(FT):
                                last = nc.tensor.matmul(y[:, t, :], aT[:, u, f, t * P:(t + 1) * P], wd[:, f, :], start=(f == 0), stop=(f == FT - 1))
                        last.then_inc(y_ready, 1)

                one_round(0)
                with pe.Fori(1, NC // 2, 1) as i:
                    one_round(i)
                pe.wait_ge(chain, 4 + 2 * (CAP // 8))
                nc.tensor.transpose(tk[:, :], first[:, :], e.ident[0:E0, 0:E0]).then_inc(tk_ready, 1)


def routed_experts(nc, e, a):
    R = 4
    BODIES = E0 // R
    with ExitStack() as ctx:
        def sb(name, shape, dt=F32):
            return ctx.enter_context(nc.sbuf_tensor(f"re_{name}", shape, dt))

        def ps(name, shape):
            return ctx.enter_context(nc.psum_tensor(f"re_{name}", shape, F32))

        def sem(name):
            return new_sem(nc, e, f"re_{name}")

        wu = sb("wu", [P, R, KD, 2 * I0])
        wd = sb("wd", [P, R, D])
        rows = sb("rows", [P, R, ROW0])
        read_at = sb("read_at", [P, R, 1], I32)
        add_at = sb("add_at", [P, R, 1], I32)
        w = sb("w", [P, R, 1])
        rT = sb("rT", [P, 2, KD, CAP])
        silu = sb("silu", [P, 2, I0])
        act_rows = sb("act_rows", [P, 2, I0])
        actT = sb("actT", [P, 2, CAP])
        add = sb("add", [P, R, D])
        tp = ps("tp", [P, 2, KD, CAP])
        up = ps("up", [P, 2, 2 * I0])
        ta = ps("ta", [P, 2, CAP])
        y = ps("y", [P, 2, D])
        w_loaded = [sem(f"w_loaded{r}") for r in range(R)]
        gathered = [e.kept.enter_context(nc.semaphore(f"gathered{r}")) for r in range(R)]
        scattered = e.kept.enter_context(nc.semaphore("scattered"))
        read_at_ready, add_at_ready, tp_ready, rT_ready, up_ready, silu_ready, act_ready, ta_ready, actT_ready, y_ready, add_ready, w_ready = (
            sem(n) for n in ("read_at", "add_at", "tp", "rT", "up", "silu", "act", "ta", "actT", "y", "add", "w"))

        with nc.Block() as block:
            @block.sync
            def _(sp):
                def load(i, r):
                    sp.dma_start(wu[:, r, :, :], a.L0_up[bass.ds(i * R + r, 1)].rearrange("o (k p) n -> p (o k) n", p=P)).then_inc(w_loaded[r], 16)
                    sp.dma_start(wd[:, r, :], a.L0_down[bass.ds(i * R + r, 1)].rearrange("o p n -> (o p) n")).then_inc(w_loaded[r], 16)

                for r in range(R):
                    load(0, r)
                with sp.Fori(0, BODIES - 1, 1) as i:
                    for r in range(R):
                        sp.wait_ge(y_ready, i * R + r + 1)
                        load(i + 1, r)

            @block.gpsimd
            def _(pool):
                def gather(i, r):
                    nc.gpsimd.tensor_copy(read_at[:, r, :], e.from_token[:, bass.ds(i * R + r, 1)]).then_inc(read_at_ready, 1)
                    pool.wait_ge(read_at_ready, i * R + r + 1)
                    settle(pool)
                    pool.indirect_dma_start(out=rows[:, r, :], out_offset=None, in_=e.table,
                                            in_offset=bass.IndirectOffsetOnAxis(ap=read_at[:, r, :], axis=0)).then_inc(gathered[r], 16)

                def scatter(i, r):
                    nc.gpsimd.tensor_copy(add_at[:, r, :], e.to_token[:, bass.ds(i * R + r, 1)]).then_inc(add_at_ready, 1)
                    pool.wait_ge(add_at_ready, i * R + r + 1)
                    pool.wait_ge(add_ready, i * R + r + 1)
                    past(pool, scattered, i * R * 16 + r * 16)
                    settle(pool)
                    pool.indirect_dma_start(out=e.x_padded, out_offset=bass.IndirectOffsetOnAxis(ap=add_at[:, r, :], axis=0),
                                            in_=add[:, r, :], in_offset=None, bounds_check=T + CAP - 1, oob_is_err=False,
                                            compute_op=ALU.add).then_inc(scattered, 16)

                for r in range(R):
                    gather(0, r)
                def one_round(i):
                    for r in range(R):
                        pool.wait_ge(tp_ready, i * R + r + 1)
                        pool.wait_ge(w_ready, i * R + r + 1)
                        gather(i + 1, r)
                        scatter(i, r)

                one_round(0)
                with pool.Fori(1, BODIES - 1, 1) as i:
                    one_round(i)
                for r in range(R):
                    scatter(BODIES - 1, r)
                pool.wait_ge(scattered, E0 * 16)

            @block.tensor
            def _(pe):
                def turn(i, r):
                    pe.wait_ge(gathered[r % R], (i + r // R) * 16 + 16)
                    if r >= 2:
                        pe.wait_ge(rT_ready, i * R + r - 1)
                    for k in range(KD):
                        last = nc.tensor.transpose(tp[:, r % 2, k, :], rows[:, r % R, k * P:(k + 1) * P], e.ident[:, :])
                    last.then_inc(tp_ready, 1)

                def products(i, peeled):
                    for r in range(R):
                        pe.wait_ge(rT_ready, i * R + r + 1)
                        pe.wait_ge(w_loaded[r], i * 32 + 32)
                        past(pe, act_ready, i * R + max(r - 1, 0))
                        for k in range(KD):
                            last = nc.tensor.matmul(up[:, r % 2, :], rT[:, r % 2, k, :], wu[:, r, k, :], start=(k == 0), stop=(k == KD - 1))
                        last.then_inc(up_ready, 1)
                        if r < R - 1 or not peeled:
                            turn(i, r + 1)
                        pe.wait_ge(act_ready, i * R + r + 1)
                        past(pe, actT_ready, i * R + max(r - 1, 0))
                        nc.tensor.transpose(ta[:, r % 2, :], act_rows[:, r % 2, :], e.ident[:, :]).then_inc(ta_ready, 1)
                        pe.wait_ge(actT_ready, i * R + r + 1)
                        past(pe, add_ready, i * R + max(r - 1, 0))
                        nc.tensor.matmul(y[:, r % 2, :], actT[:, r % 2, :], wd[:, r, :], start=True, stop=True).then_inc(y_ready, 1)

                turn(0, 0)
                products(0, False)
                with pe.Fori(1, BODIES - 1, 1) as i:
                    products(i, False)
                products(BODIES - 1, True)

            @block.scalar
            def _(act):
                def row_copy(i, r):
                    act.wait_ge(tp_ready, i * R + r + 1)
                    nc.scalar.activation(rT[:, r % 2, :, :], tp[:, r % 2, :, :], ACT.Copy).then_inc(rT_ready, 1)

                def expert(i, peeled):
                    for r in range(R):
                        act.wait_ge(up_ready, i * R + r + 1)
                        nc.scalar.activation(silu[:, r % 2, :], up[:, r % 2, 0:I0], ACT.Silu).then_inc(silu_ready, 1)
                        if r < R - 1 or not peeled:
                            row_copy(i, r + 1)
                        act.wait_ge(ta_ready, i * R + r + 1)
                        nc.scalar.activation(actT[:, r % 2, :], ta[:, r % 2, :], ACT.Copy).then_inc(actT_ready, 1)

                row_copy(0, 0)
                with act.Fori(0, BODIES - 1, 1) as i:
                    expert(i, False)
                expert(BODIES - 1, True)

            @block.vector
            def _(dve):
                def take_weight(i, r):
                    dve.wait_ge(gathered[r], i * 16 + 16)
                    nc.vector.tensor_copy(w[:, r, :], rows[:, r, bass.ds(i * R + (D + r), 1)]).then_inc(w_ready, 1)

                def experts(i, first):
                    for r in range(R):
                        take_weight(i, r)
                        dve.wait_ge(silu_ready, i * R + r + 1)
                        nc.vector.tensor_tensor(act_rows[:, r % 2, :], silu[:, r % 2, :], up[:, r % 2, I0:2 * I0], ALU.mult).then_inc(act_ready, 1)
                        dve.wait_ge(w_ready, i * R + r + 1)
                        dve.wait_ge(y_ready, i * R + r + 1)
                        if not first:
                            dve.wait_ge(scattered, i * R * 16 + (r + 1 - R) * 16)
                        nc.vector.scalar_tensor_tensor(add[:, r, :], y[:, r % 2, :], w[:, r, :], e.row_gb0[:, :], ALU.mult, ALU.mult).then_inc(add_ready, 1)

                experts(0, True)
                with dve.Fori(1, BODIES, 1) as i:
                    experts(i, False)


def mixed_residual(nc, e):
    with ExitStack() as ctx:
        part = ctx.enter_context(nc.sbuf_tensor("mixed", [P, 2, HS, D], F32))
        scaled = [new_sem(nc, e, f"mix_scaled{n}") for n in range(2)]
        with nc.Block() as block:
            def work(eng, ops, n, parts):
                o = e.O[:, :, :].rearrange("p (j g) (n c) -> p g c n j", g=2, n=H)
                row = e.row_ga1[:, :].rearrange("p (n j) -> p n j", n=H)
                count = 0
                for g, channels in parts:
                    for c in channels:
                        ops.tensor_tensor(part[:, g, c, :].rearrange("p (n j) -> p n j", n=H), o[:, g, c], row, ALU.mult).then_inc(scaled[n], 1)
                        count += 1
                eng.wait_ge(scaled[n], count)
                for g, channels in parts:
                    x = e.X[:, g * HS + channels[0]:g * HS + channels[-1] + 1, :]
                    ops.tensor_tensor(x, x, part[:, g, channels[0]:channels[-1] + 1, :], ALU.add).then_inc(scaled[n], 1)
                eng.wait_ge(scaled[n], count + len(parts))

            @block.vector
            def _(dve):
                work(dve, nc.vector, 0, ((0, range(HS)), (1, range(6))))

            @block.gpsimd
            def _(pool):
                work(pool, nc.gpsimd, 1, ((1, range(6, HS)),))


def feed_experts(nc, e, a):
    FT = F1 // P
    TILES = 2 * NT + E1
    R = 4
    BODIES = TILES // R
    ROWS = TILES * P
    with ExitStack() as ctx:
        def sb(name, shape, dt=F32):
            return ctx.enter_context(nc.sbuf_tensor(f"fe_{name}", shape, dt))

        def ps(name, shape):
            return ctx.enter_context(nc.psum_tensor(f"fe_{name}", shape, F32))

        def sem(name):
            return new_sem(nc, e, f"fe_{name}")

        w1 = sb("w1", [P, KD, E1, F1])
        w2 = sb("w2", [P, FT, E1, D])
        best, where = sb("best", [P, NT, 8]), sb("where", [P, NT, 8], U32)
        where_f, gap, share = sb("where_f", [P, NT, 2]), sb("gap", [P, NT]), sb("share", [P, NT, 2])
        ids_i, ids = sb("ids_i", [P, ET], I32), sb("ids", [P, ET])
        starts_i, starts = sb("starts_i", [P, NT], I32), sb("starts", [P, NT])
        tile_i, tile_no = sb("tile_i", [P, TILES], I32), sb("tile_no", [P, TILES])
        earlier = sb("earlier", [P, P])
        hit = sb("hit", [P, 2, NT, ET])
        sel = sb("sel", [P, NT, E1])
        tot = sb("tot", [P, NT, E1])
        run = sb("run", [P, 2, NT, E1])
        beyond = sb("beyond", [P, E1, NT])
        tiles_e = sb("tiles_e", [P, E1])
        ends = sb("ends", [P, 2, E1])
        base = sb("base", [P, E1])
        pos = sb("pos", [P, NT, E1])
        picked = sb("picked", [P, NT, E1])
        slot, none, dead = sb("slot", [P, 2, NT]), sb("none", [P, 2, NT]), sb("dead", [P, 2, NT])
        keep, zero_w = sb("keep", [P, 2, NT]), sb("zero_w", [P, NT])
        over = sb("over", [P, TILES, E1])
        owner_f, owner = sb("owner_f", [P, TILES]), sb("owner", [P, TILES], I32)
        put_i, get_i = sb("put_i", [P, 2, NT], I32), sb("get_i", [P, 2, NT], I32)
        h_rows = sb("h_rows", [P, 2, TPC, D])
        put_at, get_at = sb("put_at", [P, 2, 2, TPC], I32), sb("get_at", [P, 2, 2, TPC], I32)
        x_in, xT = sb("x_in", [P, R, D]), sb("xT", [P, 2, KD, P])
        act_rows, aT = sb("act_rows", [P, 2, F1]), sb("aT", [P, 2, FT, P])
        y_sb = sb("y_sb", [P, R, D])
        got = sb("got", [P, 2 * TPC, D])
        mixed = sb("mixed", [P, TPC, D])
        hid, ta, y = ps("hid", [P, 2, F1]), ps("ta", [P, 2, FT, P]), ps("y", [P, 2, CH])
        tp = ps("tp", [P, 2 * KD, P])
        rt = ps("rt", [P, 2, NT, E1])
        w_loaded, made, chain, gap_ready, share_ready, sel_ready, rt_ready = (
            sem(n) for n in ("w_loaded", "made", "chain", "gap", "share", "sel", "rt"))
        rows_ready, lists_ready, put_ready, get_ready, owner_ready = (sem(n) for n in ("rows", "lists", "put", "get", "owner"))
        x_loaded = [sem(f"x_loaded{r}") for r in range(R)]
        y_stored = [sem(f"y_stored{r}") for r in range(R)]
        turned, xT_ready, hid_ready, act_ready, flipped, aT_ready, y_ready, y_saved, part_done, mixed_ready, done, stored = (
            sem(n) for n in ("turned", "xT", "hid", "act", "flipped", "aT", "y", "y_saved", "part", "mixed", "done", "stored"))
        scattered = [e.kept.enter_context(nc.semaphore(f"fe_scattered{u}")) for u in range(2)]
        fetched = [e.kept.enter_context(nc.semaphore(f"fe_fetched{r}")) for r in range(2 * TPC)]
        out_v = a.out.rearrange("(g p c) d -> p g c d", p=P, c=HS)
        queue = e.queue.rearrange("(n p) d -> n p d", p=P)
        results = e.results.rearrange("(n p) d -> n p d", p=P)

        with nc.Block() as block:
            @block.sync
            def _(sp):
                for k in range(KD):
                    sp.dma_start(w1[:, k, :, :], a.L1_w1[:, k * P:(k + 1) * P, :].rearrange("e p f -> p e f")).then_inc(w_loaded, 16)
                for f in range(FT):
                    sp.dma_start(w2[:, f, :, :], a.L1_w2[:, f * P:(f + 1) * P, :].rearrange("e p d -> p e d")).then_inc(w_loaded, 16)

                def load(i, r):
                    sp.dma_start(x_in[:, r, :], queue[bass.ds(i * R + r, 1)].rearrange("o p d -> (o p) d")).then_inc(x_loaded[r], 16)

                def store(i, r):
                    sp.wait_ge(y_saved, i * R + r + 1)
                    sp.dma_start(results[bass.ds(i * R + r, 1)].rearrange("o p d -> (o p) d"), y_sb[:, r, :]).then_inc(y_stored[r], 16)

                for s in scattered:
                    sp.wait_ge(s, NT * 16)
                for r in range(R):
                    load(0, r)
                with sp.Fori(0, BODIES - 1, 1) as i:
                    for r in range(R):
                        sp.wait_ge(turned, i * R + r + 1)
                        load(i + 1, r)
                        store(i, r)
                for r in range(R):
                    store(BODIES - 1, r)
                for c in range(NT // TPC):
                    g, t = (c * TPC) // HS, (c * TPC) % HS
                    sp.wait_ge(done, c + 1)
                    sp.dma_start(out_v[:, g, t:t + TPC, :], e.X[:, c * TPC:(c + 1) * TPC, :]).then_inc(stored, 16)
                sp.wait_ge(stored, 16 * (NT // TPC))

            @block.gpsimd
            def _(pool):
                nc.gpsimd.iota(ids_i[:, :], [[1, ET]], base=0, channel_multiplier=0).then_inc(made, 1)
                nc.gpsimd.iota(starts_i[:, :], [[P, NT]], base=0, channel_multiplier=0).then_inc(made, 1)
                nc.gpsimd.iota(tile_i[:, :], [[1, TILES]], base=0, channel_multiplier=0).then_inc(made, 1)
                nc.gpsimd.memset(earlier[:, :], 1.0).then_inc(made, 1)
                pool.wait_ge(made, 4)
                nc.gpsimd.affine_select(out=earlier[:, :], in_=earlier[:, :], compare_op=ALU.is_gt, fill=0.0,
                                        base=0, pattern=[[1, P]], channel_multiplier=-1).then_inc(made, 1)
                pool.wait_ge(lists_ready, 1)
                with pool.Fori(0, NC // 2, 1) as i:
                    for u in range(2):
                        pool.wait_ge(rows_ready, i * 2 + u + 1)
                        settle(pool)
                        nc.gpsimd.tensor_copy(put_at[:, u, :, :], put_i[:, :, bass.ds(i * 2 * TPC + u * TPC, TPC)]).then_inc(put_ready, 1)
                        pool.wait_ge(put_ready, i * 2 + u + 1)
                        settle(pool)
                        for t in range(TPC):
                            for k in range(2):
                                pool.indirect_dma_start(out=e.queue, out_offset=bass.IndirectOffsetOnAxis(ap=put_at[:, u, k, t:t + 1], axis=0),
                                                        in_=h_rows[:, u, t, :], in_offset=None, bounds_check=ROWS - 1, oob_is_err=False).then_inc(scattered[u], 16)

                for s in y_stored:
                    pool.wait_ge(s, 16 * BODIES)

                def fetch(i, u, first):
                    nc.gpsimd.tensor_copy(get_at[:, u, :, :], get_i[:, :, bass.ds(i * 2 * TPC + u * TPC, TPC)]).then_inc(get_ready, 1)
                    pool.wait_ge(get_ready, i * 2 + u + 1)
                    settle(pool)
                    for r in range(2 * TPC):
                        if not first:
                            pool.wait_ge(part_done, (i * 2 + u) * 2 * TPC - 2 * TPC + r + 1)
                            settle(pool)
                        pool.indirect_dma_start(out=got[:, r, :], out_offset=None, in_=e.results,
                                                in_offset=bass.IndirectOffsetOnAxis(ap=get_at[:, u, r % 2, r // 2:r // 2 + 1], axis=0)).then_inc(fetched[r], 16)

                fetch(0, 0, True)
                fetch(0, 1, False)
                with pool.Fori(1, NC // 2, 1) as i:
                    for u in range(2):
                        fetch(i, u, False)

            @block.vector
            def _(dve):
                n = [0]

                def link(ins):
                    n[0] += 1
                    ins.then_inc(chain, 1)
                    dve.wait_ge(chain, n[0])

                def all_of(instructions):
                    for ins in instructions:
                        ins.then_inc(chain, 1)
                        n[0] += 1
                    dve.wait_ge(chain, n[0])

                tt, flat2 = nc.vector.tensor_tensor, lambda ap: ap.rearrange("p (o n) -> p o n", o=1)
                dve.wait_ge(made, 5)
                link(nc.vector.tensor_copy(ids[:, :], ids_i[:, :]))
                link(nc.vector.tensor_copy(starts[:, :], starts_i[:, :]))
                link(nc.vector.tensor_copy(tile_no[:, :], tile_i[:, :]))
                all_of([nc.vector.max(best[:, t, :], e.logits[:, t, :]) for t in range(NT)])
                all_of([nc.vector.max_index(where[:, t, :], best[:, t, :], e.logits[:, t, :]) for t in range(NT)])
                tt(gap[:, :], best[:, :, 0], best[:, :, 1], ALU.subtract).then_inc(gap_ready, 1)
                link(nc.vector.tensor_copy(where_f[:, :, :], where[:, :, 0:2]))
                for k in range(2):
                    link(tt(hit[:, k, :, :], flat2(ids[:, :]).to_broadcast([P, NT, ET]),
                            where_f[:, :, k:k + 1].to_broadcast([P, NT, ET]), ALU.is_equal))
                tt(sel[:, :, :], hit[:, 0, :, 0:E1], hit[:, 1, :, 0:E1], ALU.add).then_inc(sel_ready, 1)
                dve.wait_ge(rt_ready, 1)
                link(nc.vector.tensor_copy(tot[:, :, :], rt[:, 1, :, :]))
                src, step = tot[:, :, :], 1
                for s in range(5):
                    dst = run[:, s % 2, :, :]
                    all_of([nc.vector.tensor_copy(dst[:, 0:step, :], src[:, 0:step, :]),
                            tt(dst[:, step:NT, :], src[:, step:NT, :], src[:, 0:NT - step, :], ALU.add)])
                    src, step = dst, step * 2
                assert step == NT
                link(tt(beyond[:, :, :], src[:, NT - 1:NT, :].rearrange("p o (e q) -> p (o e) q", q=1).to_broadcast([P, E1, NT]),
                        flat2(starts[:, :]).to_broadcast([P, E1, NT]), ALU.is_gt))
                link(nc.vector.tensor_reduce(tiles_e[:, :], beyond[:, :, :], AX.X, ALU.add))
                before, step = tiles_e[:, :], 1
                for s in range(3):
                    dst = ends[:, s % 2, :]
                    all_of([nc.vector.tensor_copy(dst[:, 0:step], before[:, 0:step]),
                            tt(dst[:, step:E1], before[:, step:E1], before[:, 0:E1 - step], ALU.add)])
                    before, step = dst, step * 2
                assert step == E1
                link(tt(base[:, :], before, tiles_e[:, :], ALU.subtract))
                link(nc.vector.tensor_scalar(base[:, :], base[:, :], float(P), None, ALU.mult))
                link(tt(pos[:, :, :], src, tot[:, :, :], ALU.subtract))
                link(tt(pos[:, :, :], rt[:, 0, :, :], pos[:, :, :], ALU.add))
                link(tt(pos[:, :, :], pos[:, :, :], flat2(base[:, :]).to_broadcast([P, NT, E1]), ALU.add))
                for k in range(2):
                    link(tt(picked[:, :, :], hit[:, k, :, 0:E1], pos[:, :, :], ALU.mult))
                    link(nc.vector.tensor_reduce(slot[:, k, :], picked[:, :, :], AX.X, ALU.add))
                    link(nc.vector.tensor_reduce(none[:, k, :], hit[:, k, :, E1:ET], AX.X, ALU.add))
                link(nc.vector.scalar_tensor_tensor(dead[:, :, :], none[:, :, :], float(ROWS), slot[:, :, :], ALU.mult, ALU.add))
                link(nc.vector.tensor_copy(get_i[:, :, :], slot[:, :, :]))
                nc.vector.tensor_copy(put_i[:, :, :], dead[:, :, :]).then_inc(lists_ready, 1)
                link(tt(over[:, :, :], flat2(before).to_broadcast([P, TILES, E1]),
                        tile_no[:, :].rearrange("p (t o) -> p t o", o=1).to_broadcast([P, TILES, E1]), ALU.is_le))
                link(nc.vector.tensor_reduce(owner_f[:, :], over[:, :, :], AX.X, ALU.add))
                link(nc.vector.tensor_scalar(owner_f[:, :], owner_f[:, :], float(E1 - 1), None, ALU.min))
                nc.vector.tensor_copy(owner[:, :], owner_f[:, :]).then_inc(owner_ready, 1)
                dve.wait_ge(share_ready, 2)
                link(nc.vector.tensor_scalar(share[:, :, :], share[:, :, :], 0.5, 0.5, ALU.mult, ALU.add))
                share_k = share[:, :, :].rearrange("p t k -> p k t")
                link(tt(none[:, :, :], share_k, none[:, :, :], ALU.mult))
                link(tt(keep[:, :, :], share_k, none[:, :, :], ALU.subtract))
                link(tt(zero_w[:, :], none[:, 0, :], none[:, 1, :], ALU.add))
                gbw = flat2(e.row_gb1[:, :]).to_broadcast([P, TPC, D])
                for c in range(NC):
                    all_of([nc.vector.scalar_tensor_tensor(mixed[:, t, :], e.H[:, c * TPC + t, :], zero_w[:, c * TPC + t:c * TPC + t + 1],
                                                           e.row_gb1[:, :], ALU.mult, ALU.mult) for t in range(TPC)])
                    x = e.X[:, c * TPC:(c + 1) * TPC, :]
                    link(tt(x, x, mixed[:, :, :], ALU.add))

                def flip_copy(i, r):
                    dve.wait_ge(flipped, i * R + r + 1)
                    nc.vector.tensor_copy(aT[:, r % 2, :, :], ta[:, r % 2, :, :]).then_inc(aT_ready, 1)

                def save(i, r, first):
                    dve.wait_ge(y_ready, i * R + r + 1)
                    if not first:
                        dve.wait_ge(y_stored[r], i * 16)
                    nc.vector.tensor_copy(y_sb[:, r, :], y[:, r % 2, 0:D]).then_inc(y_saved, 1)

                def tiles(i, first):
                    for r in range(R):
                        flip_copy(i, r)
                        save(i, r, first)

                tiles(0, True)
                with dve.Fori(1, BODIES, 1) as i:
                    tiles(i, False)

                with dve.Fori(0, NC, 1) as i:
                    for t in range(TPC):
                        dve.wait_ge(fetched[2 * t], i * 16 + 16)
                        nc.vector.tensor_scalar(mixed[:, t, :], got[:, 2 * t, :], keep[:, 0, bass.ds(i * TPC + t, 1)], None, ALU.mult).then_inc(part_done, 1)
                        dve.wait_ge(fetched[2 * t + 1], i * 16 + 16)
                        dve.wait_ge(part_done, i * 2 * TPC + 2 * t + 1)
                        nc.vector.scalar_tensor_tensor(mixed[:, t, :], got[:, 2 * t + 1, :], keep[:, 1, bass.ds(i * TPC + t, 1)], mixed[:, t, :],
                                                       ALU.mult, ALU.add).then_inc(part_done, 1)
                    dve.wait_ge(part_done, i * 2 * TPC + 2 * TPC)
                    nc.vector.tensor_tensor(mixed[:, :, :], mixed[:, :, :], gbw, ALU.mult).then_inc(mixed_ready, 1)
                    dve.wait_ge(mixed_ready, i + 1)
                    x = e.X[:, bass.ds(i * TPC, TPC), :]
                    nc.vector.tensor_tensor(x, x, mixed[:, :, :], ALU.add).then_inc(done, 1)
                    dve.wait_ge(done, i + 1)

            @block.scalar
            def _(act):
                act.wait_ge(gap_ready, 1)
                nc.scalar.activation(share[:, :, 0], gap[:, :], ACT.Tanh, scale=0.5).then_inc(share_ready, 1)
                nc.scalar.activation(share[:, :, 1], gap[:, :], ACT.Tanh, scale=-0.5).then_inc(share_ready, 1)

                def rows_of(i, u):
                    nc.scalar.activation(h_rows[:, u, :, :], e.H[:, bass.ds(i * 2 * TPC + u * TPC, TPC), :], ACT.Copy).then_inc(rows_ready, 1)

                rows_of(0, 0)
                rows_of(0, 1)
                with act.Fori(0, NC // 2 - 1, 1) as i:
                    for u in range(2):
                        act.wait_ge(scattered[u], (i + 1) * 2 * TPC * 16)
                        rows_of(i + 1, u)

                def row_copy(i, r):
                    act.wait_ge(turned, i * R + r + 1)
                    nc.scalar.activation(xT[:, r % 2, :, :], tp[:, 0:KD, :], ACT.Copy).then_inc(xT_ready, 1)

                def tiles(i, last):
                    for r in range(R):
                        act.wait_ge(hid_ready, i * R + r + 1)
                        nc.scalar.activation(act_rows[:, r % 2, :], hid[:, r % 2, :], ACT.Silu).then_inc(act_ready, 1)
                        if r < R - 1 or not last:
                            row_copy(i, r + 1)

                row_copy(0, 0)
                with act.Fori(0, BODIES - 1, 1) as i:
                    tiles(i, False)
                tiles(BODIES - 1, True)

            @block.tensor
            def _(pe):
                pe.wait_ge(sel_ready, 1)
                sel_flat = sel[:, :, :].rearrange("p t e -> p (t e)")
                nc.tensor.matmul(rt[:, 0, :, :].rearrange("p t e -> p (t e)"), earlier[:, :], sel_flat, start=True, stop=True)
                nc.tensor.matmul(rt[:, 1, :, :].rearrange("p t e -> p (t e)"), e.ones[:, :], sel_flat, start=True, stop=True).then_inc(rt_ready, 1)
                pe.wait_ge(owner_ready, 1)
                pe.wait_ge(w_loaded, 16 * (KD + FT))

                def expert_of(i, r):
                    return pe.value_load(owner[0:1, bass.ds(i * R + r, 1)], min_val=0, max_val=E1 - 1)

                def turn(i, r):
                    pe.wait_ge(x_loaded[r % R], (i + r // R) * 16 + 16)
                    if r:
                        pe.wait_ge(xT_ready, i * R + r)
                    for k in range(KD):
                        last = nc.tensor.transpose(tp[:, k, :], x_in[:, r % R, k * P:(k + 1) * P], e.ident[:, :])
                    last.then_inc(turned, 1)

                def hidden(i, r, ex):
                    pe.wait_ge(xT_ready, i * R + r + 1)
                    for k in range(KD):
                        last = nc.tensor.matmul(hid[:, r % 2, :], xT[:, r % 2, k, :], w1[:, k, bass.ds(ex, 1), :].rearrange("p o f -> p (o f)"),
                                                start=(k == 0), stop=(k == KD - 1))
                    last.then_inc(hid_ready, 1)

                def flip(i, r):
                    pe.wait_ge(act_ready, i * R + r + 1)
                    for f in range(FT):
                        last = nc.tensor.transpose(ta[:, r % 2, f, :], act_rows[:, r % 2, f * P:(f + 1) * P], e.ident[:, :])
                    last.then_inc(flipped, 1)

                def down(i, r, ex):
                    pe.wait_ge(aT_ready, i * R + r + 1)
                    if r >= 2 or not isinstance(i, int) or i:
                        pe.wait_ge(y_saved, i * R + r - 1)
                    for f in range(FT):
                        last = nc.tensor.matmul(y[:, r % 2, 0:D], aT[:, r % 2, f, :], w2[:, f, bass.ds(ex, 1), :].rearrange("p o d -> p (o d)"),
                                                start=(f == 0), stop=(f == FT - 1))
                    last.then_inc(y_ready, 1)

                def tiles(i, first, last):
                    for r in range(R):
                        hidden(i, r, expert_of(i, r))
                        if r < R - 1 or not last:
                            turn(i, r + 1)
                        if r or not first:
                            if r:
                                down(i, r - 1, expert_of(i, r - 1))
                            else:
                                down(i - 1, R - 1, expert_of(i - 1, R - 1))
                        flip(i, r)

                turn(0, 0)
                tiles(0, True, False)
                with pe.Fori(1, BODIES - 1, 1) as i:
                    tiles(i, False, False)
                tiles(BODIES - 1, False, True)
                down(BODIES - 1, R - 1, expert_of(BODIES - 1, R - 1))


def program(nc, a):
    e = Env()
    with ExitStack() as ctx:
        e.layer = ctx.enter_context(ExitStack())
        e.sems = []
        e.kept = ctx

        def sb(name, shape, dt=F32):
            return ctx.enter_context(nc.sbuf_tensor(name, shape, dt))

        def dram(name, shape, dt=F32):
            return nc.dram_tensor(name, shape, dt, kind="Internal").ap()

        e.X = sb("X", [P, NT, D])
        e.ident, e.ident_b = sb("ident", [P, P]), sb("ident_b", [P, P], BF16)
        e.ones = sb("ones", [P, P])
        e.mask_k, e.mask_q = sb("mask_k", [P, P], BF16), sb("mask_q", [P, CH + P], BF16)
        e.col, e.bias_qk = sb("col", [P, 24]), sb("bias_qk", [P, 4])
        e.row_ga0, e.row_gb0, e.row_sb0, e.row_cb0 = (sb(f"row_{n}", [P, D]) for n in ("ga0", "gb0", "sb0", "cb0"))
        e.row_ga1, e.row_gb1, e.row_sb1, e.row_cb1 = (sb(f"row_{n}", [P, D]) for n in ("ga1", "gb1", "sb1", "cb1"))
        e.w_out0, e.b_out0 = sb("w_out0", [P, KD, D]), sb("b_out0", [1, D])
        e.bn6, e.mv = sb("bn6", [P, NT, 6]), sb("mv", [P, NT, 2])
        e.var, e.root, e.rstd, e.newt = (sb(n, [P, NT]) for n in ("var", "root", "rstd", "newt"))
        e.q_dram, e.k_dram = dram("q_parts", (PARTS, D, T), BF16), dram("k_parts", (PARTS, D, T), BF16)
        e.table, e.x_padded = dram("table", (T, ROW0)), dram("x_after", (T + CAP, D))
        e.x_dram = e.x_padded[0:T, :]
        e.queue, e.results = dram("queue", ((2 * NT + E1) * P, D)), dram("results", ((2 * NT + E1) * P, D))
        e.q_heads = e.q_dram.rearrange("s (h r) t -> s h r t", r=HS)
        e.k_heads = e.k_dram.rearrange("s (h r) t -> s h r t", r=HS)

        setup(nc, e, a)
        with ExitStack() as att:
            e.V = att.enter_context(nc.sbuf_tensor("V", [P, H, NT, HS], F32))
            e.O = att.enter_context(nc.sbuf_tensor("O", [P, NT, D], F32))
            project(nc, e, 0, a.L0_w_qkv, a.L0_b_qkv[2:3, :])
            attention(nc, e, 0)
            project_out(nc, e)
        with ExitStack() as ffn:
            e.hT = ffn.enter_context(nc.sbuf_tensor("hT_0", [P, KD, T], F32))
            e.logits = ffn.enter_context(nc.sbuf_tensor("logits_0", [P, NT, E0 + 1], F32))
            e.chosen = ffn.enter_context(nc.sbuf_tensor("chosen", [P, NT, E0], F32))
            e.order = ffn.enter_context(nc.sbuf_tensor("order", [P, T // 2], F32))
            e.from_token = ffn.enter_context(nc.sbuf_tensor("from_token", [P, E0], I32))
            e.to_token = ffn.enter_context(nc.sbuf_tensor("to_token", [P, E0], I32))
            feed_norm(nc, e, 0, a.L0_gate_w, None, E0 + 1)
            shared_expert(nc, e, a)
            routed_experts(nc, e, a)
        recycle_semaphores(nc, e)
        with ExitStack() as att:
            e.V = att.enter_context(nc.sbuf_tensor("V1", [P, H, NT, HS], F32))
            e.O = att.enter_context(nc.sbuf_tensor("O1", [P, NT, D], F32))
            project(nc, e, 1, a.L1_w_qkv, None)
            attention(nc, e, 1)
            mixed_residual(nc, e)
        with ExitStack() as ffn:
            e.H = ffn.enter_context(nc.sbuf_tensor("H_1", [P, NT, D], F32))
            e.logits = ffn.enter_context(nc.sbuf_tensor("logits_1", [P, NT, ET], F32))
            feed_norm(nc, e, 1, a.L1_gate_w, a.L1_bias, ET)
            feed_experts(nc, e, a)


def lay_out(x):
    def qkv_heads(w):
        return np.ascontiguousarray(w.reshape(-1, H, 3, HS).transpose(0, 2, 1, 3).reshape(-1, 3, D))

    return {
        "x": np.ascontiguousarray(x["L0_attn_encodings"][0]),
        "L0_w_qkv": qkv_heads(x["L0_attn_attn_W"]),
        "L0_b_qkv": qkv_heads(x["L0_attn_attn_b"].reshape(1, -1))[0],
        "L0_out_W": x["L0_attn_out_W"], "L0_out_b": x["L0_attn_out_b"].reshape(1, D),
        "L0_gate_w": np.concatenate([x["L0_ffn_gate_w"], x["L0_ffn_shared_gate_w"]], axis=1),
        "L0_shared_up": x["L0_ffn_shared_gate_up_w"], "L0_shared_down": x["L0_ffn_shared_down_w"],
        "L0_up": x["L0_ffn_expert_gate_up_w"], "L0_down": x["L0_ffn_expert_down_w"],
        "L0_c": x["L0_c"], "L0_wmod": x["L0_wmod"],
        "L1_w_qkv": qkv_heads(np.ascontiguousarray(x["L1_attn_W_qkv"].transpose(1, 0, 2)).reshape(D, -1)),
        "L1_W_out": x["L1_attn_W_out"].reshape(D, D),
        "L1_gate_w": np.ascontiguousarray(x["L1_ffn_gate_w"].T), "L1_bias": x["L1_ffn_expert_bias"].reshape(1, ET),
        "L1_w1": np.ascontiguousarray(x["L1_ffn_w1"].transpose(0, 2, 1)),
        "L1_w2": np.ascontiguousarray(x["L1_ffn_w2"].transpose(0, 2, 1)),
        "L1_c": x["L1_c"], "L1_wmod": x["L1_wmod"],
    }


class Arguments:
    pass


def kernel(**inputs):
    import numpy as _np
    import concourse.bacc as _bacc
    from concourse import mybir as _mybir
    from concourse.bass_utils import run_bass_kernel_spmd as _run

    nc = _bacc.Bacc("TRN2", target_bir_lowering=False, num_devices=1)
    arrays = {f"in_{k}": _np.ascontiguousarray(v) for k, v in lay_out({k: _np.asarray(v) for k, v in inputs.items()}).items()}
    a = Arguments()
    a.__dict__.update({k[3:]: nc.dram_tensor(k, v.shape, _mybir.dt.from_np(v.dtype), kind="ExternalInput").ap()
                       for k, v in arrays.items()})
    a.out = nc.dram_tensor("out_0", (T, D), F32, kind="ExternalOutput").ap()
    program(nc, a)
    r = _run(nc, [arrays], core_ids=[0])
    return r.results[0]["out_0"].reshape(1, T, D)
```
